# Optimizing a Trainium2 kernel written in Bass

```python
import numpy as np
import jax
import jax.numpy as jnp

def _softmax(x, axis=-1):
    return jax.nn.softmax(x, axis=axis)

def _gelu(x):
    return jax.nn.gelu(x, approximate=True)

def _silu(x):
    return jax.nn.silu(x)

def _sigmoid(x):
    return jax.nn.sigmoid(x)

def _layernorm(x, axis=-1, eps=1e-05):
    m = jnp.mean(x, axis=axis, keepdims=True)
    v = jnp.var(x, axis=axis, keepdims=True)
    return (x - m) / jnp.sqrt(v + eps)

def _scatter_add(tgt, idx, src, axis=0):
    return tgt.at[idx].add(src)

def _segment_sum(src, seg, n):
    return jax.ops.segment_sum(src, seg, n)
kernel_name = 'mk_prb_d2_jaxref_r8_564524'

def setup_inputs(seed: int=0):
    np.random.seed(seed)
    _w = jnp.asarray

    def _L0_attn_setup():
        import math
        import jax, jax.numpy as jnp
        import numpy as np
        DIM = 128
        B, T = (4, 256)
        key = jax.random.key(seed)
        ks = jax.random.split(key, 7)
        std = 0.02
        x = jax.random.normal(ks[0], (B, T, DIM), dtype=jnp.float32)
        Wq = jax.random.normal(ks[1], (DIM, DIM), dtype=jnp.float32) * std
        Wk = jax.random.normal(ks[2], (DIM, DIM), dtype=jnp.float32) * std
        Wv = jax.random.normal(ks[3], (DIM, DIM), dtype=jnp.float32) * std
        Wo = jax.random.normal(ks[4], (DIM, DIM), dtype=jnp.float32) * std
        Wd = jax.random.normal(ks[5], (1, DIM), dtype=jnp.float32) * std
        bd = jnp.full((1,), 3.0, dtype=jnp.float32)
        out_scale = jnp.full((1,), 0.1, dtype=jnp.float32)
        return {'x': x, 'Wq': Wq, 'Wk': Wk, 'Wv': Wv, 'Wo': Wo, 'Wd': Wd, 'bd': bd, 'out_scale': out_scale}
    _L0_attn_in = _L0_attn_setup()

    def _L0_ffn_setup():
        import jax, jax.numpy as jnp
        import numpy as np
        B, S, D, FF, E, L = (8, 256, 128, 512, 16, 4)

        def _unipool_layer(xt, router, W1, W2):
            logits = xt @ router
            probs = jax.nn.softmax(logits, axis=-1)
            w = jnp.max(probs, axis=-1)
            idx = jnp.argmax(probs, axis=-1)

            def body(acc, params):
                w1, w2, i = params
                h = jax.nn.silu(xt @ w1) @ w2
                sel = jnp.where(idx == i, w, 0.0)
                return (acc + sel[:, None] * h, None)
            out, _ = jax.lax.scan(body, jnp.zeros_like(xt), (W1, W2, jnp.arange(W1.shape[0])))
            return out
        key = jax.random.key(seed)
        k0, k1, k2, k3 = jax.random.split(key, 4)
        x = jax.random.normal(k0, (B, S, D), dtype=jnp.float32)
        routers = jax.random.normal(k1, (L, D, E), dtype=jnp.float32) * 0.02
        W1 = jax.random.normal(k2, (E, D, FF), dtype=jnp.float32) * 0.02
        W2 = jax.random.normal(k3, (E, FF, D), dtype=jnp.float32) * 0.02
        return {'x': x, 'routers': routers, 'W1': W1, 'W2': W2}
    _L0_ffn_in = _L0_ffn_setup()

    def _L1_attn_setup():
        import jax, jax.numpy as jnp
        import numpy as np
        D = 128
        H = 16
        HD = D // H
        K = 4
        B = 8
        S = 256
        SIZES = [D, D // 2, D, D, D, D, H, H, D]
        OFF = np.cumsum([0] + SIZES)

        def _dwconv_silu(x, w):
            s = x.shape[1]
            xp = jnp.pad(x, ((0, 0), (K - 1, 0), (0, 0)))
            y = sum((xp[:, j:j + s, :] * w[:, j] for j in range(K)))
            return jax.nn.silu(y)

        def _rmsnorm(x, w, eps=1e-06):
            return x * jax.lax.rsqrt(jnp.mean(x * x, axis=-1, keepdims=True) + eps) * w

        def _forward(hidden, W_ctrl, b_ctrl, W_block, qconv_w, kconv_w, vconv_w, rms_m_w, rms_v_w, W_out, b_out):
            b, s, _ = hidden.shape
            ctrl = hidden @ W_ctrl + b_ctrl
            parts = [ctrl[..., OFF[i]:OFF[i + 1]] for i in range(9)]
            ug_in, ang_in, cand_in, q_in, k_in, v_in, a_in, be_in, og_in = parts

            def heads(t):
                return t.reshape(b, s, H, HD)
            q = heads(_dwconv_silu(q_in, qconv_w))
            k = heads(_dwconv_silu(k_in, kconv_w))
            v = heads(_dwconv_silu(v_in, vconv_w))
            q = q * jax.lax.rsqrt(jnp.sum(q * q, axis=-1, keepdims=True) + 1e-12)
            k = k * jax.lax.rsqrt(jnp.sum(k * k, axis=-1, keepdims=True) + 1e-12)
            upd = jax.nn.sigmoid(ug_in)
            ret = 1.0 - upd
            cand = jax.nn.silu(cand_in)
            cos_a = jnp.cos(ang_in)
            sin_a = jnp.sin(ang_in)
            alpha = jax.nn.sigmoid(a_in)
            beta = jax.nn.sigmoid(be_in)
            tm = lambda t: jnp.moveaxis(t, 1, 0)
            xs = (tm(upd), tm(ret), tm(cand), tm(cos_a), tm(sin_a), tm(q), tm(k), tm(v), tm(alpha), tm(beta))
            vec0 = jnp.zeros((b, D), dtype=hidden.dtype)
            S0 = jnp.zeros((b, H, HD, HD), dtype=hidden.dtype)

            def step(carry, x):
                vec, St = carry
                u, r, c, ca, sa, qt, kt, vt, at, bt = x
                vp = jnp.einsum('bpi,pij->bpj', vec.reshape(b, D // 2, 2), W_block)
                x1, x2 = (vp[..., 0], vp[..., 1])
                rot = jnp.stack([x1 * ca - x2 * sa, x1 * sa + x2 * ca], axis=-1).reshape(b, D)
                vec_new = u * rot + r * c
                pred = jnp.einsum('bhij,bhi->bhj', St, kt)
                delta = vt - pred
                S_new = at[..., None, None] * St + bt[..., None, None] * (kt[..., :, None] * delta[..., None, :])
                read = jnp.einsum('bhij,bhi->bhj', S_new, qt)
                return ((vec_new, S_new), (vec_new, read))
            _, (vec_states, reads) = jax.lax.scan(step, (vec0, S0), xs)
            vec_states = jnp.moveaxis(vec_states, 0, 1)
            reads = jnp.moveaxis(reads, 0, 1)
            m = _rmsnorm(reads, rms_m_w).reshape(b, s, D)
            vread = _rmsnorm(vec_states, rms_v_w)
            gate = jax.nn.sigmoid(og_in)
            return (jnp.concatenate([m, vread], axis=-1) @ W_out + b_out) * gate
        key = jax.random.key(seed)
        ks = jax.random.split(key, 10)
        tot = int(OFF[-1])
        W_ctrl = jax.random.normal(ks[0], (D, tot), dtype=jnp.float32) / np.sqrt(D)
        b = np.zeros(tot, np.float32)
        b[OFF[6]:OFF[7]] = 1.5
        b[OFF[7]:OFF[8]] = -2.0
        b[OFF[8]:OFF[9]] = -1.5
        b_ctrl = jnp.asarray(b)
        W_block = jax.random.normal(ks[1], (D // 2, 2, 2), dtype=jnp.float32) * 0.1

        def conv_w(k):
            w = jax.random.normal(k, (D, K), dtype=jnp.float32) * 0.02
            return w.at[:, -1].add(1.0)
        qconv_w = conv_w(ks[2])
        kconv_w = conv_w(ks[3])
        vconv_w = conv_w(ks[4])
        rms_m_w = jnp.ones((HD,), dtype=jnp.float32)
        rms_v_w = jnp.ones((D,), dtype=jnp.float32)
        W_out = jax.random.normal(ks[5], (2 * D, D), dtype=jnp.float32) * 0.02
        b_out = jnp.zeros((D,), dtype=jnp.float32)
        hidden = jax.random.normal(ks[6], (B, S, D), dtype=jnp.float32)
        return {'hidden': hidden, 'W_ctrl': W_ctrl, 'b_ctrl': b_ctrl, 'W_block': W_block, 'qconv_w': qconv_w, 'kconv_w': kconv_w, 'vconv_w': vconv_w, 'rms_m_w': rms_m_w, 'rms_v_w': rms_v_w, 'W_out': W_out, 'b_out': b_out}
    _L1_attn_in = _L1_attn_setup()

    def _L1_ffn_setup():
        import jax, jax.numpy as jnp
        import numpy as np
        B, S, D, E = (2, 256, 128, 8)
        key = jax.random.key(seed)
        ks = jax.random.split(key, 5)
        x = jax.random.normal(ks[0], (B, S, D), dtype=jnp.float32)
        router_w = jax.random.normal(ks[1], (E, D), dtype=jnp.float32) * 0.02
        router_b = jnp.zeros((E,), dtype=jnp.float32)
        expert_w = jax.random.normal(ks[2], (E, D, D), dtype=jnp.float32) * 0.02
        expert_b = jnp.zeros((E, D), dtype=jnp.float32)
        return {'x': x, 'router_w': router_w, 'router_b': router_b, 'expert_w': expert_w, 'expert_b': expert_b}
    _L1_ffn_in = _L1_ffn_setup()
    _d = {'L0_attn_x': _L0_attn_in['x'], 'L0_attn_Wq': _L0_attn_in['Wq'], 'L0_attn_Wk': _L0_attn_in['Wk'], 'L0_attn_Wv': _L0_attn_in['Wv'], 'L0_attn_Wo': _L0_attn_in['Wo'], 'L0_attn_Wd': _L0_attn_in['Wd'], 'L0_attn_bd': _L0_attn_in['bd'], 'L0_attn_out_scale': _L0_attn_in['out_scale'], 'L0_ffn_routers': _L0_ffn_in['routers'], 'L0_ffn_W1': _L0_ffn_in['W1'], 'L0_ffn_W2': _L0_ffn_in['W2'], 'L1_attn_W_ctrl': _L1_attn_in['W_ctrl'], 'L1_attn_b_ctrl': _L1_attn_in['b_ctrl'], 'L1_attn_W_block': _L1_attn_in['W_block'], 'L1_attn_qconv_w': _L1_attn_in['qconv_w'], 'L1_attn_kconv_w': _L1_attn_in['kconv_w'], 'L1_attn_vconv_w': _L1_attn_in['vconv_w'], 'L1_attn_rms_m_w': _L1_attn_in['rms_m_w'], 'L1_attn_rms_v_w': _L1_attn_in['rms_v_w'], 'L1_attn_W_out': _L1_attn_in['W_out'], 'L1_attn_b_out': _L1_attn_in['b_out'], 'L1_ffn_router_w': _L1_ffn_in['router_w'], 'L1_ffn_router_b': _L1_ffn_in['router_b'], 'L1_ffn_expert_w': _L1_ffn_in['expert_w'], 'L1_ffn_expert_b': _L1_ffn_in['expert_b']}
    _x0 = _d['L0_attn_x']
    _d['L0_attn_x'] = jax.random.normal(jax.random.fold_in(jax.random.key(seed), 1), (2, 1024, 128), dtype=_x0.dtype)
    del _x0
    return _d

def reference(L0_attn_x, L0_attn_Wq, L0_attn_Wk, L0_attn_Wv, L0_attn_Wo, L0_attn_Wd, L0_attn_bd, L0_attn_out_scale, L0_ffn_routers, L0_ffn_W1, L0_ffn_W2, L1_attn_W_ctrl, L1_attn_b_ctrl, L1_attn_W_block, L1_attn_qconv_w, L1_attn_kconv_w, L1_attn_vconv_w, L1_attn_rms_m_w, L1_attn_rms_v_w, L1_attn_W_out, L1_attn_b_out, L1_ffn_router_w, L1_ffn_router_b, L1_ffn_expert_w, L1_ffn_expert_b):

    def _L0_attn_ref(x, Wq, Wk, Wv, Wo, Wd, bd, out_scale):
        import math
        import jax, jax.numpy as jnp
        import numpy as np
        DIM = 128
        B, T = (4, 256)
        Bsz, Tlen, dim = x.shape
        scale = 1.0 / math.sqrt(dim)
        q = jnp.einsum('btd,ed->bte', x, Wq)
        k = jnp.einsum('btd,ed->bte', x, Wk)
        v = jnp.einsum('btd,ed->bte', x, Wv)
        scores = jnp.einsum('btd,bsd->bts', q, k) * scale
        decay_logits = jnp.einsum('btd,ed->bte', x, Wd)[..., 0] + bd
        decay = jax.nn.sigmoid(decay_logits)
        pos = jnp.arange(Tlen)
        diff = pos[None, :] - pos[:, None]
        causal = (diff > 0).astype(x.dtype)
        log_decay = jnp.log(decay + 1e-08)
        dist = jnp.clip(diff.astype(x.dtype) - 1.0, 0.0)
        log_weights = log_decay[:, None, :] * dist[None, :, :]
        weights = jnp.exp(log_weights) * causal[None, :, :]
        scores = scores * weights
        retrieved = jnp.einsum('bts,bsd->btd', scores, v)
        out = jnp.einsum('btd,ed->bte', retrieved, Wo) * out_scale
        return out

    def _L0_ffn_ref(x, routers, W1, W2):
        import jax, jax.numpy as jnp
        import numpy as np
        B, S, D, FF, E, L = (8, 256, 128, 512, 16, 4)

        def _unipool_layer(xt, router, W1, W2):
            logits = xt @ router
            probs = jax.nn.softmax(logits, axis=-1)
            w = jnp.max(probs, axis=-1)
            idx = jnp.argmax(probs, axis=-1)

            def body(acc, params):
                w1, w2, i = params
                h = jax.nn.silu(xt @ w1) @ w2
                sel = jnp.where(idx == i, w, 0.0)
                return (acc + sel[:, None] * h, None)
            out, _ = jax.lax.scan(body, jnp.zeros_like(xt), (W1, W2, jnp.arange(W1.shape[0])))
            return out
        b, s, d = x.shape
        xt = x.reshape(-1, d)

        def step(carry, router):
            return (_unipool_layer(carry, router, W1, W2), None)
        xt, _ = jax.lax.scan(step, xt, routers)
        return xt.reshape(b, s, d)

    def _L1_attn_ref(hidden, W_ctrl, b_ctrl, W_block, qconv_w, kconv_w, vconv_w, rms_m_w, rms_v_w, W_out, b_out):
        import jax, jax.numpy as jnp
        import numpy as np
        D = 128
        H = 16
        HD = D // H
        K = 4
        B = 8
        S = 256
        SIZES = [D, D // 2, D, D, D, D, H, H, D]
        OFF = np.cumsum([0] + SIZES)

        def _dwconv_silu(x, w):
            s = x.shape[1]
            xp = jnp.pad(x, ((0, 0), (K - 1, 0), (0, 0)))
            y = sum((xp[:, j:j + s, :] * w[:, j] for j in range(K)))
            return jax.nn.silu(y)

        def _rmsnorm(x, w, eps=1e-06):
            return x * jax.lax.rsqrt(jnp.mean(x * x, axis=-1, keepdims=True) + eps) * w

        def _forward(hidden, W_ctrl, b_ctrl, W_block, qconv_w, kconv_w, vconv_w, rms_m_w, rms_v_w, W_out, b_out):
            b, s, _ = hidden.shape
            ctrl = hidden @ W_ctrl + b_ctrl
            parts = [ctrl[..., OFF[i]:OFF[i + 1]] for i in range(9)]
            ug_in, ang_in, cand_in, q_in, k_in, v_in, a_in, be_in, og_in = parts

            def heads(t):
                return t.reshape(b, s, H, HD)
            q = heads(_dwconv_silu(q_in, qconv_w))
            k = heads(_dwconv_silu(k_in, kconv_w))
            v = heads(_dwconv_silu(v_in, vconv_w))
            q = q * jax.lax.rsqrt(jnp.sum(q * q, axis=-1, keepdims=True) + 1e-12)
            k = k * jax.lax.rsqrt(jnp.sum(k * k, axis=-1, keepdims=True) + 1e-12)
            upd = jax.nn.sigmoid(ug_in)
            ret = 1.0 - upd
            cand = jax.nn.silu(cand_in)
            cos_a = jnp.cos(ang_in)
            sin_a = jnp.sin(ang_in)
            alpha = jax.nn.sigmoid(a_in)
            beta = jax.nn.sigmoid(be_in)
            tm = lambda t: jnp.moveaxis(t, 1, 0)
            xs = (tm(upd), tm(ret), tm(cand), tm(cos_a), tm(sin_a), tm(q), tm(k), tm(v), tm(alpha), tm(beta))
            vec0 = jnp.zeros((b, D), dtype=hidden.dtype)
            S0 = jnp.zeros((b, H, HD, HD), dtype=hidden.dtype)

            def step(carry, x):
                vec, St = carry
                u, r, c, ca, sa, qt, kt, vt, at, bt = x
                vp = jnp.einsum('bpi,pij->bpj', vec.reshape(b, D // 2, 2), W_block)
                x1, x2 = (vp[..., 0], vp[..., 1])
                rot = jnp.stack([x1 * ca - x2 * sa, x1 * sa + x2 * ca], axis=-1).reshape(b, D)
                vec_new = u * rot + r * c
                pred = jnp.einsum('bhij,bhi->bhj', St, kt)
                delta = vt - pred
                S_new = at[..., None, None] * St + bt[..., None, None] * (kt[..., :, None] * delta[..., None, :])
                read = jnp.einsum('bhij,bhi->bhj', S_new, qt)
                return ((vec_new, S_new), (vec_new, read))
            _, (vec_states, reads) = jax.lax.scan(step, (vec0, S0), xs)
            vec_states = jnp.moveaxis(vec_states, 0, 1)
            reads = jnp.moveaxis(reads, 0, 1)
            m = _rmsnorm(reads, rms_m_w).reshape(b, s, D)
            vread = _rmsnorm(vec_states, rms_v_w)
            gate = jax.nn.sigmoid(og_in)
            return (jnp.concatenate([m, vread], axis=-1) @ W_out + b_out) * gate
        return _forward(hidden, W_ctrl, b_ctrl, W_block, qconv_w, kconv_w, vconv_w, rms_m_w, rms_v_w, W_out, b_out)

    def _L1_ffn_ref(x, router_w, router_b, expert_w, expert_b):
        import jax, jax.numpy as jnp
        import numpy as np
        B, S, D, E = (2, 256, 128, 8)
        logits = jnp.einsum('bsd,ed->bse', x, router_w) + router_b
        probs = jax.nn.softmax(logits, axis=-1)
        weights = jnp.max(probs, axis=-1)
        top1 = jnp.argmax(probs, axis=-1)
        y_all = jnp.einsum('bsd,eod->bseo', x, expert_w) + expert_b
        y = jnp.take_along_axis(y_all, top1[:, :, None, None], axis=2)[:, :, 0, :]
        out = y * weights[:, :, None]
        return out
    x = L0_attn_x
    xn = _layernorm(x, axis=-1)
    x = x + _L0_attn_ref(xn, L0_attn_Wq, L0_attn_Wk, L0_attn_Wv, L0_attn_Wo, L0_attn_Wd, L0_attn_bd, L0_attn_out_scale) + _L0_ffn_ref(xn, L0_ffn_routers, L0_ffn_W1, L0_ffn_W2)
    xn = _layernorm(x, axis=-1)
    x = x + _L1_attn_ref(xn, L1_attn_W_ctrl, L1_attn_b_ctrl, L1_attn_W_block, L1_attn_qconv_w, L1_attn_kconv_w, L1_attn_vconv_w, L1_attn_rms_m_w, L1_attn_rms_v_w, L1_attn_W_out, L1_attn_b_out) + _L1_ffn_ref(xn, L1_ffn_router_w, L1_ffn_router_b, L1_ffn_expert_w, L1_ffn_expert_b)
    return x

_drawn_inputs = setup_inputs


def setup_inputs(seed=0):
    import zlib

    import numpy as np

    out = dict(_drawn_inputs(seed))
    spreads = {'L1_attn_rms_m_w': (1.0, 0.2),
     'L1_attn_rms_v_w': (1.0, 0.2),
     'L1_attn_b_out': (0.0, 0.1),
     'L1_ffn_router_b': (0.0, 0.1),
     'L1_ffn_expert_b': (0.0, 0.1)}
    factors = {}
    for name, (base, spread) in spreads.items():
        noise = np.random.default_rng([zlib.crc32(name.encode()), seed]).standard_normal(out[name].shape)
        drawn = base * np.exp(spread * noise) if base else spread * noise
        out[name] = jnp.asarray(drawn.astype(out[name].dtype))
    for name, factor in factors.items():
        out[name] = (out[name] * factor).astype(out[name].dtype)
    return out
```

```python
import math

import concourse.bass as bass
from concourse import mybir
from contextlib import ExitStack

F32 = mybir.dt.float32
BF16 = mybir.dt.bfloat16
I32 = mybir.dt.int32
ALU = mybir.AluOpType
ACT = mybir.ActivationFunctionType
AX_X = mybir.AxisListType.X


def build(nc, ins, out):
    x_in = ins["L0_attn_x"]
    B, S, D = x_in.shape
    P = 128
    N = B * S
    NT = N // P
    TB = S // P
    routers, W1, W2 = ins["L0_ffn_routers"], ins["L0_ffn_W1"], ins["L0_ffn_W2"]
    L, _, E = routers.shape
    FF = W1.shape[2]
    FC = FF // P
    NS = NT + E - 1
    SCALE = float(D) ** -0.5
    G = 4
    NG = NT // G
    PRE = 5
    MID = PRE + 2 * ((NS - PRE) // 4)
    E1 = ins["L1_ffn_expert_w"].shape[0]
    HD = ins["L1_attn_rms_m_w"].shape[0]
    H = D // HD
    K = ins["L1_attn_qconv_w"].shape[1]
    NCTRL = ins["L1_attn_W_ctrl"].shape[1]
    sizes = [D, D // 2, D, D, D, D, H, H, D]
    OFF = [sum(sizes[:n]) for n in range(len(sizes) + 1)]
    C = N // P
    NC = S // C
    CG = 8
    VL = 32
    VC = S // VL
    assert B * NC == P and B * (D // 2) == P and OFF[-1] == NCTRL
    assert D == P and (MID - PRE) % 2 == 0 and (NS - MID) % 2 == 0

    xs_dram = nc.dram_tensor("sorted_x", [NS * P, D], F32, kind="Internal")
    ys_dram = nc.dram_tensor("sorted_y", [NS * P, D], F32, kind="Internal")

    with ExitStack() as ctx:
        def sb(name, shape, dt=F32):
            return ctx.enter_context(nc.sbuf_tensor(name, shape, dt))

        def sem(name):
            return ctx.enter_context(nc.semaphore(name))

        PS = ctx.enter_context(nc.psum_tensor("PS", [P, 8, 512], F32))

        W1s = sb("W1s", [P, E * FF])
        W2s = sb("W2s", [P, E * FC * D])
        xres = sb("xres", [P, NT, D])
        xcur = sb("xcur", [P, NT, D])
        xT = sb("xT", [P, N])
        slotbuf = sb("slotbuf", [P, 4 * S])
        slots = slotbuf[:, 0:NS * D].rearrange("p (t d) -> p t d", d=D)
        qT = sb("qT", [P, N])
        kT = sb("kT", [P, N])
        vtok = sb("vtok", [P, NT, D])
        wdec = sb("wdec", [P, 2, S])
        swt = sb("swt", [P, 2, S])
        retT = sb("retT", [P, S])
        ident = sb("ident", [P, P])
        ltri = sb("ltri", [P, P], BF16)
        ones_bf = sb("ones_bf", [P, P], BF16)
        dist_i = retT[:, :].bitcast(I32)
        dist = sb("dist", [P, S])
        after = sb("after", [P, P])
        rev_i = sb("rev_i", [P, E], I32)
        rev = sb("rev", [P, E])
        tix_i = sb("tix_i", [P, NS], I32)
        tix = sb("tix", [P, NS])
        one_e = sb("one_e", [P, E])
        rw = sb("rw", [P, L, E])
        rw0 = sb("rw0", [P, E + 1])
        wraw = sb("wraw", [P, 4, D])
        wT = sb("wT", [P, 4, D])
        bd = sb("bd", [P, 1])
        oscale = sb("oscale", [P, 1])
        stat = sb("stat", [P, 4, NT])
        lg = sb("lg", [P, NT, E + 1])
        sh = sb("sh", [P, NT, E])
        ex = sb("ex", [P, NT, E])
        rt = sb("rt", [P, NT, E])
        hot = sb("hot", [P, NT, E], BF16)
        hotf = sb("hotf", [P, NT, E])
        mx = sb("mx", [P, NT])
        esum = sb("esum", [P, NT])
        wprob = sb("wprob", [P, NT])
        first = sb("first", [P, NT])
        ldec = sb("ldec", [P, 3, NT])
        cnt_i = sb("cnt_i", [P, 2, E], I32)
        ecnt = sb("ecnt", [P, 3, E])
        posf = sb("posf", [P, NT])
        pos = sb("pos", [P, NT], I32)
        tcmpbuf = sb("tcmpbuf", [P, 4 * P])
        tcmp = tcmpbuf[:, 0:NS * E].rearrange("p (s e) -> p s e", e=E)
        texp = sb("texp", [P, 2, NS])
        tile_w = sb("tile_w", [P, NS], I32)
        xstage = sb("xstage", [P, 2, D])
        xTs = sb("xTs", [P, 2, P])
        hbuf = sb("hbuf", [P, 2 * S])
        hs = hbuf[:, 0:2 * FF].rearrange("p (b f) -> p b f", b=2)
        hTs = hbuf[:, 2 * FF:4 * FF].rearrange("p (b f) -> p b f", b=2)

        wc = sb("wc", [P, NCTRL])
        ew_raw = sb("ew_raw", [P, E1, D])
        ewT = sb("ewT", [P, E1 * D])
        ebias = ew_raw[:, 0:G, :]
        rw1 = sb("rw1", [P, E1])
        rb1 = sb("rb1", [P, E1])
        taps = sb("taps", [P, 3, K])
        tapdiag = sb("tapdiag", [P, 3 * K, P])
        cbias = sb("cbias", [P, 3])
        pbias = sb("pbias", [P, 5])
        abbias = sb("abbias", [P, 2 * H])
        ogbias = sb("ogbias", [P, D])
        obias = sb("obias", [P, D])
        wblk = sb("wblk", [P, 4])
        nwblk = sb("nwblk", [P, 4])
        wmrow = sb("wmrow", [1, HD])
        wmrow16 = sb("wmrow16", [1, HD, H])
        wmcol = sb("wmcol", [P, 1])
        wvcol = sb("wvcol", [P, 2])
        wo_m = sb("wo_m", [P, D])
        wo_v = sb("wo_v", [P, 2, D])
        headsel = sb("headsel", [P, H])
        headmean = sb("headmean", [P, P])
        headof = sb("headof", [P, H])
        perm = sb("perm", [P, P])
        seqmean = sb("seqmean", [P, P])
        abraw = sb("abraw", [P, C, 2 * H])
        ab = sb("ab", [P, C, 2 * H])
        nvar = wraw[:, :, :].rearrange("p (n m) d -> p n (m d)", n=2)
        nstd = wT[:, :, :].rearrange("p (n m) d -> p n (m d)", n=2)
        pred = ex[:, :, :].rearrange("p t e -> p (t e)").rearrange("p (c h) -> p c h", h=H)
        vtmp = wT[:, 0:3, :].rearrange("p n d -> p (n d)").rearrange("p (r i q) -> p r i q", r=2, i=2)
        y0 = sb("y0", [P, VC + 1, 2])
        lg1 = tcmpbuf[:, :].rearrange("p (n t e) -> p n t e", n=4, e=E1)
        sel = sb("sel", [P, NT, 32])
        rev1 = rev[:, E - E1:E]

        U = 2 * S
        u = [W1s[:, n * U:(n + 1) * U] for n in range(4)] + [W2s[:, n * U:(n + 1) * U] for n in range(4)]
        pre = W1s[:, 0:3 * B * (K - 1 + S)].rearrange("p (n b t) -> p n b t", n=3, b=B)
        post = [u[4], u[5], u[6]]
        sqb = u[7]
        u0p, u1p = swt[:, 0, :], swt[:, 1, :]
        angp, kp, cosp = retT[:, :], dist[:, :], W1s[:, 7 * S:8 * S]
        sinp = kp
        mpl = slotbuf[:, :].rearrange("p (r i t) -> p r i t", r=2, i=2)
        zneg = hbuf[:, :].rearrange("p (r t) -> p r t", r=2)
        Kc = qT[:, :].rearrange("p (t h i) -> p t h i", t=C, h=H)
        Qc = kT[:, :].rearrange("p (t h i) -> p t h i", t=C, h=H)
        Vc = vtok[:, :, :].rearrange("p t (h i) -> p t h i", h=H)
        bKc = wdec[:, :, :].rearrange("p b (t h i) -> p (b t) h i", h=H, i=HD)
        xcur_f = xcur[:, :, :].rearrange("p t d -> p (t d)")
        X = [v.rearrange("p (c h i) -> p c h i", h=H, i=HD) for v in (xcur_f, u[0])]
        tmp = u[1].rearrange("p (c h i) -> p c h i", h=H, i=HD)
        aX = u[2].rearrange("p (c h i) -> p c h i", h=H, i=HD)
        qX = [v.rearrange("p (c h i) -> p c h i", h=H, i=HD) for v in (u[3], u[7])]
        qeffT = u[4].rearrange("p (t c) -> p t c", t=C)
        olocT = swt[:, :, :].rearrange("p b (t c) -> p (b t) c", c=P)
        PT = qT[:, 0:S].rearrange("p (i c) -> p i c", i=HD)
        QT0 = kT[:, S:U]
        QT = qT[:, S:U].rearrange("p (j c) -> p j c", j=HD)
        Sall = kT[:, 0:S].rearrange("p (c j) -> p c j", j=HD)
        BD = W1s[:, 0:2 * U].rearrange("p (n b c m) -> p n b c m", n=2, b=B, c=CG)
        BDS = W1s[:, 2 * U:4 * U].rearrange("p (n b c m) -> p n b c m", n=2, b=B, c=CG)
        Y = W2s[:, U:U + 6 * S].rearrange("p (t r q c) -> p t r q c", t=VL, r=2, q=3)
        gate = vtok
        oT = u[4]
        osq = wdec[:, :, :].rearrange("p b t -> p (b t)")
        orms = u[0]
        mT = u[1]
        vT = u[2].rearrange("p (r t) -> p r t", r=2)
        vsq = u[3].rearrange("p (r t) -> p r t", r=2)
        vt4 = xcur_f.rearrange("p (r t) -> p r t", r=2)
        selT = abraw[:, :, :].rearrange("p t h -> p (t h)")

        ld_x = sem("ld_x")
        ld_small = sem("ld_small")
        ld_w1 = sem("ld_w1")
        ld_w2 = sem("ld_w2")
        ld_slots = [sem(f"ld_slots{n}") for n in range(3)]
        zeroed = sem("zeroed")
        xs_cleared = sem("xs_cleared")
        consts = sem("consts")
        pool_seq = sem("pool_seq")
        dve_seq = sem("dve_seq")
        act_seq = sem("act_seq")
        layer_x = sem("layer_x")
        xt_tr = sem("xt_tr")
        xt_ready = sem("xt_ready")
        logits_mm = sem("logits_mm")
        shifted = sem("shifted")
        exp_done = sem("exp_done")
        hot_ready = sem("hot_ready")
        rank_mm = sem("rank_mm")
        pos_ready = sem("pos_ready")
        te_ready = sem("te_ready")
        scattered = sem("scattered")
        gathered = [sem(f"gathered{g}") for g in range(NG)]
        x_staged = sem("x_staged")
        x_tr = sem("x_tr")
        x_ev = sem("x_ev")
        h_mm = sem("h_mm")
        h_act = sem("h_act")
        h_tr = sem("h_tr")
        h_ev = sem("h_ev")
        y_mm = sem("y_mm")
        y_ev = sem("y_ev")
        y_stored = sem("y_stored")
        w_tr = sem("w_tr")
        w_ready = sem("w_ready")
        dec_sig = sem("dec_sig")
        dec_eps = sem("dec_eps")
        dec_log = sem("dec_log")
        ln_var = sem("ln_var")
        ln_std = sem("ln_std")
        qkv_mm = sem("qkv_mm")
        qkv_ready = sem("qkv_ready")
        score_mm = sem("score_mm")
        decay_w = sem("decay_w")
        sw_ready = sem("sw_ready")
        ret_mm = sem("ret_mm")
        ret_ev = sem("ret_ev")
        proj_mm = sem("proj_mm")
        attn_added = sem("attn_added")
        st_out = sem("st_out")
        ld_l1 = sem("ld_l1")
        ld_ebias = sem("ld_ebias")
        consts1 = sem("consts1")
        x2_ready = sem("x2_ready")
        diag_ready = sem("diag_ready")
        pads = sem("pads")
        xstate0 = sem("xstate0")
        pa_mm = sem("pa_mm")
        pa_ev = sem("pa_ev")
        pd_mm = sem("pd_mm")
        pd_ev = sem("pd_ev")
        ab_ready = sem("ab_ready")
        sq_ready = sem("sq_ready")
        nrm_std = sem("nrm_std")
        nrm_rec = sem("nrm_rec")
        ang_red = sem("ang_red")
        sincos = sem("sincos")
        bk_ready = sem("bk_ready")
        sh1 = sem("sh1")
        ex1 = sem("ex1")
        sel_ready = sem("sel_ready")
        x_new = sem("x_new")
        ax_ready = sem("ax_ready")
        r_ready = sem("r_ready")
        rT_mm = sem("rT_mm")
        rT_ev = sem("rT_ev")
        trans_mm = sem("trans_mm")
        trans_ev = sem("trans_ev")
        bd_ready = sem("bd_ready")
        s0_ready = sem("s0_ready")
        scan_mm = [sem(f"scan_mm{b}") for b in range(B)]
        s_ready = [sem(f"s_ready{b}") for b in range(B)]
        bds_ready = sem("bds_ready")
        corr_mm = sem("corr_mm")
        y1_mm = sem("y1_mm")
        y1_ev = sem("y1_ev")
        o_ready = sem("o_ready")
        osq_ready = sem("osq_ready")
        oms_mm = sem("oms_mm")
        oms_eps = sem("oms_eps")
        orms_std = sem("orms_std")
        m_ready = sem("m_ready")
        vsq_ready = sem("vsq_ready")
        vsum = sem("vsum")
        vms_mm = sem("vms_mm")
        vms_eps = sem("vms_eps")
        vrms_std = sem("vrms_std")
        vn_ready = sem("vn_ready")
        gate_ready = sem("gate_ready")
        out_mm = sem("out_mm")
        x3_ready = sem("x3_ready")

        block = ctx.enter_context(nc.Block())

        LD_L1 = 16 * (4 + 2 * 3 + 6 * B + HD + 4)
        PA_ALL = 10 + 6 * NG + NG + 1
        TWO_PI = 2 * math.pi
        TWO_PI_HI = 6.28125
        TWO_PI_LO = TWO_PI - TWO_PI_HI
        PI_DOWN = 3.1415925
        ROUND = 1.5 * 2 ** 23

        xs_tiles = xs_dram[:, :].rearrange("(t p) d -> p t d", p=P)
        ys_tiles = ys_dram[:, :].rearrange("(t p) d -> p t d", p=P)
        x_tiles = x_in.rearrange("b (t p) d -> p (b t) d", p=P)

        @block.sync
        def _(sp):
            for g in range(NG):
                sp.dma_start(xres[:, g * G:(g + 1) * G, :], x_tiles[:, g * G:(g + 1) * G, :]).then_inc(ld_x, 16)
            for n, w in enumerate(("Wq", "Wk", "Wv", "Wo")):
                sp.dma_start(wraw[:, n, :], ins[f"L0_attn_{w}"][:, :]).then_inc(ld_small, 16)
            sp.dma_start(rw[:, :, :], routers.rearrange("l d e -> d l e")).then_inc(ld_small, 16)
            sp.dma_start(rw0[:, 0:E], routers[0, :, :]).then_inc(ld_small, 16)
            sp.dma_start(rw0[:, E:E + 1], ins["L0_attn_Wd"].rearrange("o d -> d o")).then_inc(ld_small, 16)
            sp.dma_start(bd[:, :], ins["L0_attn_bd"].partition_broadcast(P)).then_inc(ld_small, 16)
            sp.dma_start(oscale[:, :], ins["L0_attn_out_scale"].partition_broadcast(P)).then_inc(ld_small, 16)
            sp.wait_ge(zeroed, 1)
            sp.dma_start(xs_tiles, slots[:, :, :]).then_inc(xs_cleared, 16)
            sp.dma_start(W1s[:, :].rearrange("d (e f) -> d e f", e=E), W1.rearrange("e d f -> d e f")).then_inc(ld_w1, 16)
            sp.dma_start(W2s[:, :].rearrange("p (e c d) -> p e c d", e=E, c=FC),
                         W2.rearrange("e (c p) d -> p e c d", p=P)).then_inc(ld_w2, 16)
            def load(dst, src):
                sp.dma_start(dst, src).then_inc(ld_l1, 16)

            b_ctrl = ins["L1_attn_b_ctrl"]
            load(wc[:, :], ins["L1_attn_W_ctrl"][:, :])
            load(ew_raw[:, :, :], ins["L1_ffn_expert_w"].rearrange("e o d -> o e d"))
            load(rw1[:, :], ins["L1_ffn_router_w"][:, :])
            load(rb1[:, :], ins["L1_ffn_router_b"].partition_broadcast(P))
            for n, w in enumerate("kqv"):
                load(taps[:, n, :], ins[f"L1_attn_{w}conv_w"][:, :])
                part = OFF[{"q": 3, "k": 4, "v": 5}[w]]
                load(cbias[:, n:n + 1], b_ctrl[part:part + D].rearrange("(p o) -> p o", o=1))
            for b in range(B):
                half = slice(b * D // 2, (b + 1) * D // 2)
                for n, part in ((0, OFF[0]), (2, OFF[2])):
                    load(pbias[half, n:n + 2], b_ctrl[part:part + D].rearrange("(p r) -> p r", r=2))
                load(pbias[half, 4:5], b_ctrl[OFF[1]:OFF[2]].rearrange("(p o) -> p o", o=1))
                load(wblk[half, :], ins["L1_attn_W_block"].rearrange("p i j -> p (i j)"))
                load(wvcol[half, :], ins["L1_attn_rms_v_w"].rearrange("(p r) -> p r", r=2))
                load(wo_v[half, :, :], ins["L1_attn_W_out"][D:2 * D, :].rearrange("(p r) o -> p r o", r=2))
            for j in range(HD):
                load(wo_m[j * H:(j + 1) * H, :], ins["L1_attn_W_out"][0:D, :].rearrange("(h j) o -> j h o", h=H)[j])
            load(abbias[:, :], b_ctrl[OFF[6]:OFF[8]].partition_broadcast(P))
            load(ogbias[:, :], b_ctrl[OFF[8]:OFF[9]].partition_broadcast(P))
            load(obias[:, :], ins["L1_attn_b_out"].partition_broadcast(P))
            load(wmrow[:, :], ins["L1_attn_rms_m_w"].rearrange("(o i) -> o i", o=1))
            for l in range(L):
                sp.wait_ge(scattered, 16 * NT * (l + 1))
                if l == 0:
                    sp.wait_ge(xs_cleared, 16)
                else:
                    sp.wait_ge(y_stored, 16 * NS * l)
                for n, (a, b) in enumerate(((0, PRE), (PRE, MID), (MID, NS))):
                    sp.dma_start(slots[:, a:b, :], xs_tiles[:, a:b, :]).then_inc(ld_slots[n], 16)
                with sp.Fori(0, NS) as i:
                    sp.wait_ge(y_ev, i + (l * NS + 1))
                    sp.dma_start(ys_tiles[:, bass.ds(i, 1), :], slots[:, bass.ds(i, 1), :]).then_inc(y_stored, 16)
            sp.wait_ge(pads, 1)
            for t in range(G):
                sp.dma_start(ebias[32 * t:32 * t + E1, t, :], ins["L1_ffn_expert_b"][:, :]).then_inc(ld_ebias, 16)
            out_tiles = out.rearrange("b (t p) d -> p (b t) d", p=P)
            for g in range(NG):
                sp.wait_ge(x3_ready, g + 1)
                sp.dma_start(out_tiles[:, g * G:(g + 1) * G, :], xres[:, g * G:(g + 1) * G, :]).then_inc(st_out, 16)
            sp.wait_ge(st_out, 16 * NG)

        @block.gpsimd
        def _(pool):
            seq = [0]

            def step(ins_):
                seq[0] += 1
                ins_.then_inc(pool_seq, 1)
                pool.wait_ge(pool_seq, seq[0])

            pool.memset(slots[:, :, :], 0.0).then_inc(zeroed, 1)
            step(pool.memset(ident[:, :], 0.0))
            step(pool.affine_select(out=ident[:, :], in_=ident[:, :], compare_op=ALU.not_equal, fill=1.0,
                                    base=0, pattern=[[-1, P]], channel_multiplier=1))
            step(pool.memset(ones_bf[:, :], 1.0))
            step(pool.affine_select(out=ltri[:, :], in_=ones_bf[:, :], compare_op=ALU.is_gt, fill=0.0,
                                    base=0, pattern=[[1, P]], channel_multiplier=-1))
            step(pool.memset(after[:, :], 1.0))
            step(pool.affine_select(out=after[:, :], in_=after[:, :], compare_op=ALU.is_gt, fill=0.0,
                                    base=0, pattern=[[-1, P]], channel_multiplier=1))
            step(pool.iota(dist_i[:, :], pattern=[[-1, S]], base=S - P - 1, channel_multiplier=1))
            step(pool.tensor_scalar(dist[:, :], dist_i[:, :], 0.0, None, ALU.max))
            step(pool.iota(rev_i[:, :], pattern=[[-1, E]], base=E, channel_multiplier=0))
            step(pool.tensor_copy(rev[:, :], rev_i[:, :]))
            step(pool.iota(tix_i[:, :], pattern=[[1, NS]], base=0, channel_multiplier=0))
            step(pool.tensor_copy(tix[:, :], tix_i[:, :]))
            pool.memset(one_e[:, :], 1.0).then_inc(consts, 1)
            pool.wait_ge(consts, 1)
            step(pool.memset(headsel[:, :], 1.0))
            step(pool.affine_select(out=headsel[:, :], in_=headsel[:, :], compare_op=ALU.is_ge, fill=0.0,
                                    base=0, pattern=[[-HD, H]], channel_multiplier=1))
            step(pool.affine_select(out=headsel[:, :], in_=headsel[:, :], compare_op=ALU.is_ge, fill=0.0,
                                    base=HD - 1, pattern=[[HD, H]], channel_multiplier=-1))
            step(pool.memset(headof[:, :], 0.0))
            for i in range(HD):
                step(pool.affine_select(out=headof[:, :], in_=headof[:, :], compare_op=ALU.not_equal, fill=1.0,
                                        base=-H * i, pattern=[[-1, H]], channel_multiplier=1))
            step(pool.tensor_scalar(headmean[:, :].rearrange("p (i h) -> p i h", h=H),
                                    headof[:, :].unsqueeze(1).to_broadcast([P, HD, H]), 1.0 / HD, None, ALU.mult))
            step(pool.memset(perm[:, :], 0.0))
            perm3 = perm[:, :].rearrange("p (i h) -> p i h", h=H)
            step(pool.affine_select(out=perm3, in_=perm3, compare_op=ALU.not_equal, fill=1.0,
                                    base=0, pattern=[[-1, HD], [-HD, H]], channel_multiplier=1))
            step(pool.memset(seqmean[:, :], 0.0))
            for b in range(B):
                half = slice(b * P // B, (b + 1) * P // B)
                step(pool.memset(seqmean[half, half], 1.0 / D))
            pool.memset(sel[:, :, :], 0.0).then_inc(consts1, 1)
            pool.wait_ge(consts1, 1)
            pool.wait_ge(xs_cleared, 16)
            for l in range(L):
                pool.wait_ge(pos_ready, l + 1)
                for t in range(NT):
                    pool.indirect_dma_start(xs_dram[:, :], bass.IndirectOffsetOnAxis(ap=pos[:, t:t + 1], axis=0),
                                            xcur[:, t, :], None).then_inc(scattered, 16)
                def stage(k, par):
                    at = l * NS
                    if not isinstance(k, int) or k + at >= 2:
                        pool.wait_ge(x_tr, k + (at - 1))
                    src = slots[:, k, :] if isinstance(k, int) \
                        else slots[:, bass.ds(k, 1), :].rearrange("p t d -> p (t d)")
                    pool.tensor_copy(xstage[:, par, :], src).then_inc(x_staged, 1)

                pool.wait_ge(ld_slots[0], 16 * (l + 1))
                for k in range(PRE):
                    stage(k, k % 2)
                for n, (a, b) in enumerate(((PRE, MID), (MID, NS))):
                    pool.wait_ge(ld_slots[n + 1], 16 * (l + 1))
                    with pool.Fori(0, (b - a) // 2) as i:
                        for u in range(2):
                            stage(i * 2 + (a + u), (a + u) % 2)
                pool.wait_ge(y_stored, 16 * NS * (l + 1))
                for t in range(NT):
                    pool.indirect_dma_start(xcur[:, t, :], None, ys_dram[:, :],
                                            bass.IndirectOffsetOnAxis(ap=pos[:, t:t + 1], axis=0)
                                            ).then_inc(gathered[t // G], 16)

            step(pool.memset(ebias, 0.0))
            step(pool.memset(pre[:, 0, :, 0:K - 1], 0.0))
            step(pool.memset(pre[:, 1, :, 0:K - 1], 0.0))
            pool.memset(pre[:, 2, :, 0:K - 1], 0.0).then_inc(pads, 1)
            pool.wait_ge(xt_tr, NG * (L + 1))
            step(pool.memset(xcur_f, 0.0))
            pool.affine_select(out=X[0], in_=X[0], compare_op=ALU.not_equal, fill=1.0, base=0,
                               pattern=[[1, 2 * HD], [0, H], [-1, HD]], channel_multiplier=0).then_inc(xstate0, 1)
            pool.wait_ge(pd_ev, 6 + NG)
            pool.wait_ge(ab_ready, 1)
            pool.tensor_tensor(bKc, Kc, ab[:, :, H:2 * H].unsqueeze(3).to_broadcast([P, C, H, HD]),
                               ALU.mult).then_inc(bk_ready, 1)
            pool.wait_ge(pd_ev, 6 + 2 * NG)
            for t in range(C):
                pool.wait_ge(x_new, t + 1)
                if t >= 2:
                    pool.wait_ge(rT_mm, t - 1)
                pool.tensor_tensor(qX[t % 2], X[(t + 1) % 2], Qc[:, t, :, :].unsqueeze(1).to_broadcast([P, 2 * HD, H, HD]),
                                   ALU.mult).then_inc(r_ready, 1)
            pool.wait_ge(r_ready, C)
            step(pool.memset(Sall[:, 0:1, :], 0.0))
            pool.memset(Sall[:, NC:NC + 1, :], 0.0).then_inc(s0_ready, 1)
            pool.wait_ge(s0_ready, 1)
            for g in range(NC // CG):
                if g >= 2:
                    pool.wait_ge(corr_mm, g - 1)
                for b in range(B):
                    pool.wait_ge(s_ready[b], CG * (g + 1) - 1)
                    c0 = b * NC + g * CG
                    pool.tensor_tensor(BDS[:, g % 2, b, :, :].rearrange("p c (j h) -> p (c j) h", h=H),
                                       Sall[:, c0:c0 + CG, :].rearrange("p c j -> p (c j)").unsqueeze(2).to_broadcast([P, CG * HD, H]),
                                       headof[:, :].unsqueeze(1).to_broadcast([P, CG * HD, H]),
                                       ALU.mult).then_inc(bds_ready, 1)

        @block.vector
        def _(dve):
            seq = [0]

            def step(ins_):
                seq[0] += 1
                ins_.then_inc(dve_seq, 1)
                dve.wait_ge(dve_seq, seq[0])

            def layernorm_stats():
                step(dve.tensor_reduce(stat[:, 0, :], xres[:, :, :], AX_X, ALU.add))
                step(dve.tensor_scalar(stat[:, 0, :], stat[:, 0, :], 1.0 / D, None, ALU.mult))
                step(dve.tensor_tensor(xcur[:, :, :], xres[:, :, :],
                                       stat[:, 0, :].unsqueeze(2).to_broadcast([P, NT, D]), ALU.subtract))
                sq = xT[:, :].rearrange("p (t d) -> p t d", t=NT)
                step(dve.tensor_tensor(sq, xcur[:, :, :], xcur[:, :, :], ALU.mult))
                step(dve.tensor_reduce(stat[:, 1, :], sq, AX_X, ALU.add))

            dve.wait_ge(ld_x, 16 * NG)
            layernorm_stats()
            dve.tensor_scalar(stat[:, 2, :], stat[:, 1, :], 1.0 / D, 1e-5, ALU.mult, ALU.add).then_inc(ln_var, 1)
            dve.wait_ge(ln_std, 1)
            step(dve.reciprocal(stat[:, 1, :], stat[:, 3, :]))
            for g in range(NG):
                tt = slice(g * G, (g + 1) * G)
                dve.tensor_tensor(xcur[:, tt, :], xcur[:, tt, :],
                                  stat[:, 1, tt].unsqueeze(2).to_broadcast([P, G, D]), ALU.mult).then_inc(layer_x, 1)
            dve.wait_ge(layer_x, NG)

            dve.wait_ge(w_tr, 1)
            dve.tensor_copy(wT[:, :, :].rearrange("p n d -> p (n d)"), PS[:, 5, :]).then_inc(w_ready, 1)

            def route(l):
                ne = E + 1 if l == 0 else E
                dve.wait_ge(logits_mm, l + 1)
                step(dve.tensor_copy(lg[:, :, 0:ne], PS[:, 2, 0:NT * ne].rearrange("p (t e) -> p t e", t=NT)))
                if l == 0:
                    dve.tensor_scalar(ldec[:, 0, :], lg[:, :, E], bd[:, 0:1], None, ALU.add).then_inc(dec_eps, 1)
                step(dve.tensor_reduce(mx[:, :], lg[:, :, 0:E], AX_X, ALU.max))
                dve.tensor_tensor(sh[:, :, :], lg[:, :, 0:E], mx[:, :].unsqueeze(2).to_broadcast([P, NT, E]),
                                  ALU.subtract).then_inc(shifted, 1)
                dve.wait_ge(shifted, l + 1)
                step(dve.scalar_tensor_tensor(out=rt[:, :, :], in0=sh[:, :, :], scalar=0.0,
                                              in1=rev[:, :].unsqueeze(1).to_broadcast([P, NT, E]),
                                              op0=ALU.is_ge, op1=ALU.mult))
                step(dve.tensor_reduce(first[:, :], rt[:, :, :], AX_X, ALU.max))
                first_b = first[:, :].unsqueeze(2).to_broadcast([P, NT, E])
                dve.tensor_tensor(hot[:, :, :], rt[:, :, :], first_b, ALU.is_equal).then_inc(hot_ready, 1)
                step(dve.tensor_tensor(hotf[:, :, :], rt[:, :, :], first_b, ALU.is_equal))
                dve.wait_ge(exp_done, l + 1)
                step(dve.tensor_reduce(esum[:, :], ex[:, :, :], AX_X, ALU.add))
                step(dve.reciprocal(wprob[:, :], esum[:, :]))
                dve.wait_ge(rank_mm, l + 1)
                step(dve.tensor_scalar(cnt_i[:, 0, :], PS[:, 4, 0:E], float(P - 1), None, ALU.add))
                step(dve.tensor_scalar(cnt_i[:, 1, :], cnt_i[:, 0, :], P.bit_length() - 1, None, ALU.arith_shift_right))
                step(dve.tensor_copy(ecnt[:, 0, :], cnt_i[:, 1, :]))
                step(dve.tensor_tensor_scan(ecnt[:, 1, :], one_e[:, :], ecnt[:, 0, :], 0.0, ALU.mult, ALU.add))
                step(dve.tensor_tensor(ecnt[:, 2, :], ecnt[:, 1, :], ecnt[:, 0, :], ALU.subtract))
                step(dve.scalar_tensor_tensor(out=rt[:, :, :],
                                              in0=ecnt[:, 2, :].unsqueeze(1).to_broadcast([P, NT, E]), scalar=float(P),
                                              in1=PS[:, 3, 0:NT * E].rearrange("p (t e) -> p t e", t=NT),
                                              op0=ALU.mult, op1=ALU.add))
                step(dve.tensor_tensor(rt[:, :, :], rt[:, :, :], hotf[:, :, :], ALU.mult))
                step(dve.tensor_reduce(posf[:, :], rt[:, :, :], AX_X, ALU.add))
                dve.tensor_copy(pos[:, :], posf[:, :]).then_inc(pos_ready, 1)
                step(dve.tensor_tensor(tcmp[:, :, :], ecnt[:, 1, :].unsqueeze(1).to_broadcast([P, NS, E]),
                                       tix[:, :].unsqueeze(2).to_broadcast([P, NS, E]), ALU.is_le))
                step(dve.tensor_reduce(texp[:, 0, :], tcmp[:, :, :], AX_X, ALU.add))
                dve.tensor_scalar(tile_w[:, :], texp[:, 0, :], float(E - 1), float(FF), ALU.min, ALU.mult).then_inc(te_ready, 1)
                dve.wait_ge(te_ready, l + 1)

            def attention(b):
                for j in reversed(range(TB)):
                    n = b * TB + TB - 1 - j
                    w = (j + 1) * P
                    dve.wait_ge(decay_w, n + 1)
                    step(dve.tensor_tensor(wdec[:, n % 2, w - P:w], wdec[:, n % 2, w - P:w], after[:, :], ALU.mult))
                    dve.wait_ge(score_mm, n + 1)
                    if n >= 2:
                        dve.wait_ge(ret_mm, n - 1)
                    bank = 2 * (n % 2)
                    for h in range(0, w, 512):
                        e = min(w, h + 512)
                        o = dve.scalar_tensor_tensor(out=swt[:, n % 2, h:e], in0=PS[:, bank + h // 512, 0:e - h],
                                                     scalar=SCALE, in1=wdec[:, n % 2, h:e],
                                                     op0=ALU.mult, op1=ALU.mult)
                        if e < w:
                            step(o)
                    o.then_inc(sw_ready, 1)
                    dve.wait_ge(sw_ready, n + 1)
                for g in range(TB // G):
                    dve.wait_ge(proj_mm, b * (TB // G) + g + 1)
                    tt = slice(b * TB + g * G, b * TB + (g + 1) * G)
                    dve.scalar_tensor_tensor(out=xres[:, tt, :], in0=PS[:, 6 + g, :].rearrange("p (t d) -> p t d", t=G),
                                             scalar=oscale[:, 0:1], in1=xres[:, tt, :],
                                             op0=ALU.mult, op1=ALU.add).then_inc(attn_added, 1)

            def prepare():
                dve.wait_ge(ld_l1, LD_L1)
                dve.wait_ge(consts1, 1)
                for n in range(2):
                    dve.wait_ge(pd_mm, n + 1)
                    dve.tensor_copy(ewT[:, n * 512:(n + 1) * 512], PS[:, 6 + n, :]).then_inc(pd_ev, 1)
                dve.tensor_copy(wmrow16[:, :, :], wmrow[:, :].unsqueeze(2).to_broadcast([1, HD, H])).then_inc(diag_ready, 1)
                for n in range(3):
                    for j in range(K):
                        step(dve.tensor_scalar(tapdiag[:, n * K + j, :], ident[:, :], taps[:, n, j:j + 1], None, ALU.mult))
                step(dve.tensor_scalar(nwblk[:, :], wblk[:, :], -1.0, None, ALU.mult))
                step(dve.tensor_scalar(wo_v[:, 0, :], wo_v[:, 0, :], wvcol[:, 0:1], None, ALU.mult))
                dve.tensor_scalar(wo_v[:, 1, :], wo_v[:, 1, :], wvcol[:, 1:2], None, ALU.mult).then_inc(diag_ready, 1)
                dve.wait_ge(pd_mm, 3)
                dve.tensor_copy(wmcol[:, :], PS[:, 6, 0:1]).then_inc(pd_ev, 1)
                dve.wait_ge(pd_ev, 3)
                dve.wait_ge(diag_ready, 2)

            def tile_evac(l, k, x, h, par):
                at = l * NS
                if x:
                    dve.wait_ge(x_tr, k + (at + 1))
                    if not isinstance(k, int) or k + at >= 2:
                        dve.wait_ge(h_mm, k + (at - 1))
                    dve.tensor_copy(xTs[:, par, :], PS[:, par, 0:P]).then_inc(x_ev, 1)
                if h:
                    dve.wait_ge(h_tr, k + (at - 1))
                    if not isinstance(k, int) or k + at >= 4:
                        dve.wait_ge(y_mm, k + (at - 3))
                    dve.tensor_copy(hTs[:, par, :], PS[:, 4 + par, :]).then_inc(h_ev, 1)

            for l in range(L):
                if l:
                    for g in range(NG):
                        dve.wait_ge(gathered[g], 16 * G * l)
                        tt = slice(g * G, (g + 1) * G)
                        dve.tensor_tensor(xcur[:, tt, :], xcur[:, tt, :],
                                          wprob[:, tt].unsqueeze(2).to_broadcast([P, G, D]),
                                          ALU.mult).then_inc(layer_x, 1)
                    dve.wait_ge(layer_x, NG * (l + 1))
                else:
                    dve.wait_ge(ld_small, 16 * 9)
                    dve.wait_ge(consts, 1)
                route(l)
                if l == 0:
                    dve.wait_ge(dec_sig, 1)
                    dve.tensor_scalar(ldec[:, 1, :], ldec[:, 1, :], 1e-8, None, ALU.add).then_inc(dec_eps, 1)
                if l < B:
                    attention(l)
                elif l == B:
                    prepare()
                for k in range(PRE):
                    tile_evac(l, k, True, k >= 2, k % 2)
                for a, b in ((PRE, MID), (MID, NS)):
                    with dve.Fori(0, (b - a) // 2) as i:
                        for u in range(2):
                            tile_evac(l, i * 2 + (a + u), True, True, (a + u) % 2)
                for k in range(NS, NS + 2):
                    tile_evac(l, k, False, True, k % 2)
            for g in range(NG):
                dve.wait_ge(gathered[g], 16 * G * L)
                tt = slice(g * G, (g + 1) * G)
                step(dve.tensor_tensor(xcur[:, tt, :], xcur[:, tt, :],
                                       wprob[:, tt].unsqueeze(2).to_broadcast([P, G, D]), ALU.mult))
                dve.wait_ge(attn_added, B * (TB // G))
                dve.tensor_tensor(xres[:, tt, :], xres[:, tt, :], xcur[:, tt, :], ALU.add).then_inc(x2_ready, 1)
            dve.wait_ge(x2_ready, NG)

            layernorm_stats()
            dve.tensor_scalar(stat[:, 2, :], stat[:, 1, :], 1.0 / D, 1e-5, ALU.mult, ALU.add).then_inc(ln_var, 1)
            dve.wait_ge(ln_std, 2)
            step(dve.reciprocal(stat[:, 1, :], stat[:, 3, :]))
            for g in range(NG):
                tt = slice(g * G, (g + 1) * G)
                dve.tensor_tensor(xcur[:, tt, :], xcur[:, tt, :],
                                  stat[:, 1, tt].unsqueeze(2).to_broadcast([P, G, D]), ALU.mult).then_inc(layer_x, 1)
            dve.wait_ge(layer_x, NG * (L + 1))

            job = [3]

            def bank():
                dve.wait_ge(pd_mm, job[0] + 1)
                job[0] += 1
                return PS[:, 6 + (job[0] - 1) % 2, :]

            dve.tensor_tensor(abraw[:, :, :], bank().rearrange("p (t h) -> p t h", t=C),
                              abbias[:, :].unsqueeze(1).to_broadcast([P, C, 2 * H]), ALU.add).then_inc(pd_ev, 1)
            dve.wait_ge(pd_ev, job[0])
            dve.wait_ge(pa_ev, 8)
            for r, up in enumerate((u0p, u1p)):
                step(dve.scalar_tensor_tensor(out=zneg[:, r, :], in0=up, scalar=1.0, in1=zneg[:, r, :],
                                              op0=ALU.subtract, op1=ALU.mult))
            dve.wait_ge(pa_ev, 10)
            step(dve.tensor_scalar(kp, angp, 1.0 / TWO_PI, ROUND, ALU.mult, ALU.add))
            step(dve.tensor_scalar(kp, kp, ROUND, None, ALU.subtract))
            step(dve.scalar_tensor_tensor(out=angp, in0=kp, scalar=-TWO_PI_HI, in1=angp, op0=ALU.mult, op1=ALU.add))
            step(dve.scalar_tensor_tensor(out=angp, in0=kp, scalar=-TWO_PI_LO, in1=angp, op0=ALU.mult, op1=ALU.add))
            dve.tensor_scalar(angp, angp, PI_DOWN, -PI_DOWN, ALU.min, ALU.max).then_inc(ang_red, 1)
            dve.wait_ge(ang_red, 1)

            def sumsq(n):
                dve.tensor_scalar(nvar[:, n, :], bank()[:, 0:C * H], 1e-12, None, ALU.add).then_inc(pd_ev, 1)
                dve.wait_ge(pd_ev, job[0])

            sumsq(0)
            dve.wait_ge(sincos, 2)
            step(dve.tensor_tensor(cosp, cosp, cosp, ALU.mult))
            step(dve.tensor_scalar(cosp, cosp, -2.0, 1.0, ALU.mult, ALU.add))
            for i in range(2):
                a, w = 2 * i, 2 * i + 1
                step(dve.tensor_scalar(mpl[:, 0, i, :], sinp, nwblk[:, w:w + 1], None, ALU.mult))
                step(dve.scalar_tensor_tensor(out=mpl[:, 0, i, :], in0=cosp, scalar=wblk[:, a:a + 1],
                                              in1=mpl[:, 0, i, :], op0=ALU.mult, op1=ALU.add))
                step(dve.tensor_tensor(mpl[:, 0, i, :], mpl[:, 0, i, :], u0p, ALU.mult))
                step(dve.tensor_scalar(mpl[:, 1, i, :], sinp, wblk[:, a:a + 1], None, ALU.mult))
                step(dve.scalar_tensor_tensor(out=mpl[:, 1, i, :], in0=cosp, scalar=wblk[:, w:w + 1],
                                              in1=mpl[:, 1, i, :], op0=ALU.mult, op1=ALU.add))
                step(dve.tensor_tensor(mpl[:, 1, i, :], mpl[:, 1, i, :], u1p, ALU.mult))
            sumsq(1)
            dve.wait_ge(nrm_std, 1)
            dve.reciprocal(nvar, nstd).then_inc(nrm_rec, 1)
            dve.wait_ge(nrm_rec, 1)
            for n, dst in enumerate((Kc, Qc)):
                inv = nvar[:, n, :].rearrange("p (t h) -> p t h", t=C)
                for g in range(NG):
                    tt = slice(g * G, (g + 1) * G)
                    src = bank().rearrange("p (t h i) -> p t h i", t=G, h=H)
                    for t in range(G):
                        o = dve.tensor_tensor(dst[:, g * G + t, :, :], src[:, t, :, :],
                                              inv[:, g * G + t, :].unsqueeze(2).to_broadcast([P, H, HD]), ALU.mult)
                        if t < G - 1:
                            step(o)
                    o.then_inc(pd_ev, 1)
                    dve.wait_ge(pd_ev, job[0])

            dve.tensor_tensor(lg1[:, 0, :, :], bank()[:, 0:NT * E1].rearrange("p (t e) -> p t e", t=NT),
                              rb1[:, :].unsqueeze(1).to_broadcast([P, NT, E1]), ALU.add).then_inc(pd_ev, 1)
            dve.wait_ge(pd_ev, job[0])
            step(dve.tensor_reduce(mx[:, :], lg1[:, 0, :, :], AX_X, ALU.max))
            dve.tensor_tensor(lg1[:, 1, :, :], lg1[:, 0, :, :], mx[:, :].unsqueeze(2).to_broadcast([P, NT, E1]),
                              ALU.subtract).then_inc(sh1, 1)
            dve.wait_ge(sh1, 1)
            step(dve.scalar_tensor_tensor(out=lg1[:, 3, :, :], in0=lg1[:, 1, :, :], scalar=0.0,
                                          in1=rev1.unsqueeze(1).to_broadcast([P, NT, E1]),
                                          op0=ALU.is_ge, op1=ALU.mult))
            step(dve.tensor_reduce(first[:, :], lg1[:, 3, :, :], AX_X, ALU.max))
            step(dve.tensor_tensor(lg1[:, 0, :, :], lg1[:, 3, :, :], first[:, :].unsqueeze(2).to_broadcast([P, NT, E1]),
                                   ALU.is_equal))
            dve.wait_ge(ex1, 1)
            step(dve.tensor_reduce(esum[:, :], lg1[:, 2, :, :], AX_X, ALU.add))
            step(dve.reciprocal(wprob[:, :], esum[:, :]))
            dve.tensor_tensor(sel[:, :, 0:E1], lg1[:, 0, :, :], wprob[:, :].unsqueeze(2).to_broadcast([P, NT, E1]),
                              ALU.mult).then_inc(sel_ready, 1)
            dve.wait_ge(sel_ready, 1)

            dve.wait_ge(xstate0, 1)
            dve.wait_ge(bk_ready, 1)
            dve.wait_ge(pa_ev, PA_ALL)
            for t in range(C):
                x, xn = X[t % 2], X[(t + 1) % 2]
                step(dve.tensor_tensor(tmp, x, Kc[:, t, :, :].unsqueeze(1).to_broadcast([P, 2 * HD, H, HD]), ALU.mult))
                step(dve.tensor_reduce(pred[:, :, :], tmp, AX_X, ALU.add))
                step(dve.tensor_tensor(pred[:, HD:2 * HD, :], pred[:, HD:2 * HD, :],
                                       Vc[:, t, :, :].rearrange("p h j -> p j h"), ALU.subtract))
                step(dve.tensor_tensor(tmp, pred[:, :, :].unsqueeze(3).to_broadcast([P, 2 * HD, H, HD]),
                                       bKc[:, t, :, :].unsqueeze(1).to_broadcast([P, 2 * HD, H, HD]), ALU.mult))
                dve.wait_ge(ax_ready, t + 1)
                if t >= 2:
                    dve.wait_ge(r_ready, t - 1)
                dve.tensor_tensor(xn, aX, tmp, ALU.subtract).then_inc(x_new, 1)
                dve.wait_ge(x_new, t + 1)

            M4 = mpl.rearrange("p r i (c t) -> p r i c t", t=VL)
            Z3 = zneg.rearrange("p r (c t) -> p r c t", t=VL)

            def vec_step(t):
                if t == 0:
                    for r in range(2):
                        step(dve.tensor_copy(Y[:, 0, r, 0:2, :], M4[:, r, :, :, 0]))
                    step(dve.tensor_scalar(Y[:, 0, :, 2, :], Z3[:, :, :, 0], -1.0, None, ALU.mult))
                    return
                for r in range(2):
                    step(dve.tensor_tensor(vtmp[:, r, :, :].rearrange("p i (q c) -> p i q c", q=3),
                                           M4[:, r, :, :, t].unsqueeze(2).to_broadcast([P, 2, 3, VC]),
                                           Y[:, t - 1, :, :, :], ALU.mult))
                step(dve.tensor_tensor(Y[:, t, :, :, :].rearrange("p r q c -> p r (q c)"),
                                       vtmp[:, :, 0, :], vtmp[:, :, 1, :], ALU.add))
                step(dve.tensor_tensor(Y[:, t, :, 2, :], Y[:, t, :, 2, :], Z3[:, :, :, t], ALU.subtract))

            def expert_half(t, half):
                if half == 0:
                    dve.wait_ge(y1_mm, t + 1)
                for e in range(half * E1 // 2, (half + 1) * E1 // 2):
                    o = dve.scalar_tensor_tensor(out=xres[:, t, :], in0=PS[:, 6 + e * D // 512, e * D % 512:e * D % 512 + D],
                                                 scalar=sel[:, t, e:e + 1], in1=xres[:, t, :],
                                                 op0=ALU.mult, op1=ALU.add)
                    if e < E1 - 1:
                        step(o)
                if half == 1:
                    o.then_inc(y1_ev, 1)
                    dve.wait_ge(y1_ev, t + 1)

            dve.wait_ge(trans_ev, 6)
            dve.wait_ge(s0_ready, 1)
            for b in range(B):
                dve.tensor_copy(Sall[:, b * NC + 1, :], QT[:, :, b * NC]).then_inc(s_ready[b], 1)
            for c in range(1, NC - 1):
                for b in range(B):
                    dve.wait_ge(scan_mm[b], c)
                    dve.tensor_tensor(Sall[:, b * NC + c + 1, :], PS[:, 4 + b, 0:HD], QT[:, :, b * NC + c],
                                      ALU.add).then_inc(s_ready[b], 1)
                if c <= VL:
                    vec_step(c - 1)
                elif (c - VL - 1) // 2 < NT:
                    expert_half((c - VL - 1) // 2, (c - VL - 1) % 2)
            for n in range(NC - 2 - VL, 2 * NT):
                expert_half(n // 2, n % 2)

            step(dve.memset(y0[:, 0, :], 0.0))
            for c in range(VC):
                step(dve.scalar_tensor_tensor(out=y0[:, c + 1, :], in0=Y[:, VL - 1, :, 0, c], scalar=y0[:, c, 0:1],
                                              in1=Y[:, VL - 1, :, 2, c], op0=ALU.mult, op1=ALU.add))
                step(dve.scalar_tensor_tensor(out=y0[:, c + 1, :], in0=Y[:, VL - 1, :, 1, c], scalar=y0[:, c, 1:2],
                                              in1=y0[:, c + 1, :], op0=ALU.mult, op1=ALU.add))
            dve.wait_ge(corr_mm, NC // CG)
            for r in range(2):
                vr = vT[:, r, :].rearrange("p (c t) -> p t c", t=VL)
                t4 = vt4[:, r, :].rearrange("p (c t) -> p t c", t=VL)
                for i in range(2):
                    start = y0[:, 0:VC, i].unsqueeze(1).to_broadcast([P, VL, VC])
                    step(dve.tensor_tensor(t4, Y[:, :, r, i, :], start, ALU.mult))
                    step(dve.tensor_tensor(vr, t4, Y[:, :, r, 2, :] if i == 0 else vr, ALU.add))

            for n in range(NG):
                src = PS[:, n, :].rearrange("p (c t) -> p c t", t=C)
                cc = slice(n * (P // NG), (n + 1) * (P // NG))
                o = dve.tensor_tensor(oT[:, n * 512:(n + 1) * 512].rearrange("p (c t) -> p c t", t=C), src,
                                      olocT[:, :, cc].rearrange("p t c -> p c t"), ALU.add)
                if n < NG - 1:
                    step(o)
            o.then_inc(o_ready, 1)
            dve.wait_ge(o_ready, 1)
            for g in range(NG):
                dve.tensor_tensor(gate[:, g * G:(g + 1) * G, :], bank().rearrange("p (t d) -> p t d", t=G),
                                  ogbias[:, :].unsqueeze(1).to_broadcast([P, G, D]), ALU.add).then_inc(pd_ev, 1)
                dve.wait_ge(pd_ev, job[0])
            for g in range(NG):
                tt = slice(g * G, (g + 1) * G)
                dve.tensor_tensor(xres[:, tt, :], xres[:, tt, :], bank().rearrange("p (t d) -> p t d", t=G),
                                  ALU.add).then_inc(pd_ev, 1)
                dve.wait_ge(pd_ev, job[0])
            dve.wait_ge(vsq_ready, 1)
            dve.tensor_tensor(vsq[:, 0, :], vsq[:, 0, :], vsq[:, 1, :], ALU.add).then_inc(vsum, 1)
            for n in range(2):
                dve.wait_ge(vms_mm, n + 1)
                dve.tensor_scalar(vt4[:, 0, n * 512:(n + 1) * 512], PS[:, 4 + n, :], 1e-6, None, ALU.add).then_inc(vms_eps, 1)
            for n in range(NG):
                dve.wait_ge(oms_mm, n + 1)
                dve.tensor_scalar(orms[:, n * 512:(n + 1) * 512], PS[:, n, :], 1e-6, None, ALU.add).then_inc(oms_eps, 1)
            dve.wait_ge(vrms_std, 1)
            step(dve.reciprocal(vt4[:, 1, :], vt4[:, 1, :]))
            step(dve.tensor_tensor(vT[:, 0, :], vT[:, 0, :], vt4[:, 1, :], ALU.mult))
            dve.tensor_tensor(vT[:, 1, :], vT[:, 1, :], vt4[:, 1, :], ALU.mult).then_inc(vn_ready, 1)
            dve.wait_ge(orms_std, 1)
            step(dve.reciprocal(osq, osq))
            dve.scalar_tensor_tensor(out=mT, in0=oT, scalar=wmcol[:, 0:1], in1=osq,
                                     op0=ALU.mult, op1=ALU.mult).then_inc(m_ready, 1)
            dve.wait_ge(gate_ready, 1)
            for g in range(NG):
                tt = slice(g * G, (g + 1) * G)
                dve.wait_ge(out_mm, g + 1)
                step(dve.tensor_tensor(xcur[:, tt, :], PS[:, 2 + g, :].rearrange("p (t d) -> p t d", t=G),
                                       obias[:, :].unsqueeze(1).to_broadcast([P, G, D]), ALU.add))
                step(dve.tensor_tensor(xcur[:, tt, :], xcur[:, tt, :], gate[:, tt, :], ALU.mult))
                dve.tensor_tensor(xres[:, tt, :], xres[:, tt, :], xcur[:, tt, :], ALU.add).then_inc(x3_ready, 1)

        @block.scalar
        def _(act):
            act.wait_ge(ln_var, 1)
            act.activation(stat[:, 3, :], stat[:, 2, :], ACT.Sqrt).then_inc(ln_std, 1)

            def tokens_T(l):
                for g in range(NG):
                    act.wait_ge(xt_tr, l * NG + g + 1)
                    act.activation(xT[:, g * 512:(g + 1) * 512], PS[:, g % 2, :], ACT.Copy).then_inc(xt_ready, 1)

            def qkv():
                for n in range(3 * NG):
                    act.wait_ge(qkv_mm, n + 1)
                    bank = PS[:, 5 + n % 3, :]
                    if n < 2 * NG:
                        dst = (qT, kT)[n // NG][:, (n % NG) * 512:(n % NG + 1) * 512]
                    else:
                        g = n - 2 * NG
                        dst = vtok[:, g * G:(g + 1) * G, :].rearrange("p t d -> p (t d)")
                    act.activation(dst, bank, ACT.Copy).then_inc(qkv_ready, 1)

            def attention(b):
                for j in reversed(range(TB)):
                    n = b * TB + TB - 1 - j
                    w = (j + 1) * P
                    if n >= 2:
                        act.wait_ge(sw_ready, n - 1)
                    act.activation(wdec[:, n % 2, 0:w], dist[:, S - w:S], ACT.Exp,
                                   scale=ldec[:, 2, b * TB + j:b * TB + j + 1]).then_inc(decay_w, 1)
                act.wait_ge(ret_mm, (b + 1) * TB)
                for h in range(S // 512):
                    if b:
                        act.wait_ge(proj_mm, b * (TB // G))
                    act.activation(retT[:, h * 512:(h + 1) * 512], PS[:, 4 + h, :], ACT.Copy).then_inc(ret_ev, 1)

            def tile_act(l, k, h, y, par):
                at = l * NS
                if h:
                    act.wait_ge(h_mm, k + at)
                    if not isinstance(k, int) or k + at >= 3:
                        act.wait_ge(h_tr, k + (at - 2))
                    act.activation(hs[:, 1 - par, :], PS[:, 3 - par, :], ACT.Silu).then_inc(h_act, 1)
                if y:
                    act.wait_ge(y_mm, k + (at - 2))
                    dst = slots[:, bass.ds(k - 3, 1), :].rearrange("p t d -> p (t d)") if not isinstance(k, int) \
                        else slots[:, k - 3, :]
                    act.activation(dst, PS[:, 7 - par, 0:D], ACT.Copy).then_inc(y_ev, 1)

            for l in range(L):
                tokens_T(l)
                act.wait_ge(shifted, l + 1)
                act.activation(ex[:, :, :], sh[:, :, :], ACT.Exp).then_inc(exp_done, 1)
                if l == 0:
                    act.wait_ge(dec_eps, 1)
                    act.activation(ldec[:, 1, :], ldec[:, 0, :], ACT.Sigmoid).then_inc(dec_sig, 1)
                    act.wait_ge(dec_eps, 2)
                    act.activation(ldec[:, 2, :], ldec[:, 1, :], ACT.Ln).then_inc(dec_log, 1)
                    act.wait_ge(dec_log, 1)
                    qkv()
                if l < B:
                    attention(l)
                for k in range(1, PRE):
                    tile_act(l, k, True, k >= 3, k % 2)
                for a, b in ((PRE, MID), (MID, NS)):
                    with act.Fori(0, (b - a) // 2) as i:
                        for u in range(2):
                            tile_act(l, i * 2 + (a + u), True, True, (a + u) % 2)
                for k in range(NS, NS + 3):
                    tile_act(l, k, k == NS, True, k % 2)

            act.wait_ge(ln_var, 2)
            act.activation(stat[:, 3, :], stat[:, 2, :], ACT.Sqrt).then_inc(ln_std, 1)
            tokens_T(L)

            job = [0]

            def evac(dst, func, **more):
                act.wait_ge(pa_mm, job[0] + 1)
                act.activation(dst, PS[:, 2 + job[0] % 4, :], func, **more).then_inc(pa_ev, 1)
                job[0] += 1

            def plane(n, dst, func):
                for h in range(S // 512):
                    evac(dst[:, h * 512:(h + 1) * 512], func, bias=pbias[:, n:n + 1])

            def ctrl(n):
                for b in range(B):
                    for h in range(S // 512):
                        a = K - 1 + h * 512
                        evac(pre[:, n, b, a:a + 512], ACT.Identity, bias=cbias[:, n:n + 1])

            def conv(n):
                for g in range(NG):
                    evac(post[n][:, g * 512:(g + 1) * 512], ACT.Silu)

            def square(n):
                act.wait_ge(pa_ev, job[0])
                if n:
                    act.wait_ge(pd_mm, 5)
                act.activation(sqb, post[n], ACT.Square).then_inc(sq_ready, 1)

            plane(0, u0p, ACT.Sigmoid)
            plane(1, u1p, ACT.Sigmoid)
            act.wait_ge(pd_ev, 4)
            act.activation(ab[:, :, :], abraw[:, :, :], ACT.Sigmoid).then_inc(ab_ready, 1)
            plane(2, zneg[:, 0, :], ACT.Silu)
            plane(3, zneg[:, 1, :], ACT.Silu)
            plane(4, angp, ACT.Identity)
            ctrl(0)
            conv(0)
            square(0)
            act.wait_ge(ang_red, 1)
            act.activation(cosp, angp, ACT.Sin, scale=0.5).then_inc(sincos, 1)
            act.activation(sinp, angp, ACT.Sin).then_inc(sincos, 1)
            ctrl(1)
            conv(1)
            square(1)
            ctrl(2)
            conv(2)
            act.wait_ge(pd_ev, 6)
            act.activation(nstd, nvar, ACT.Sqrt).then_inc(nrm_std, 1)
            for g in range(NG):
                evac(Vc[:, g * G:(g + 1) * G, :, :].rearrange("p t h i -> p (t h i)"), ACT.Copy)
            act.wait_ge(sh1, 1)
            act.activation(lg1[:, 2, :, :], lg1[:, 1, :, :], ACT.Exp).then_inc(ex1, 1)
            act.wait_ge(ab_ready, 1)
            evac(selT, ACT.Copy)

            def reads_evac(g):
                act.wait_ge(rT_mm, G * (g + 1))
                tt = slice(g * G, (g + 1) * G)
                act.activation(qeffT[:, tt, :].rearrange("p t c -> p (t c)"), PS[:, g % 2, :], ACT.Copy).then_inc(rT_ev, 1)
                act.activation(olocT[:, tt, :].rearrange("p t c -> p (t c)"), PS[:, 2 + g % 2, :], ACT.Copy).then_inc(rT_ev, 1)

            act.wait_ge(ab_ready, 1)
            act.wait_ge(xstate0, 1)
            for t in range(C):
                if t:
                    act.wait_ge(x_new, t)
                for h in range(H):
                    o = act.activation(aX[:, :, h, :], X[t % 2][:, :, h, :],
                                       ACT.Copy, scale=ab[:, t, h:h + 1])
                o.then_inc(ax_ready, 1)
                if t % G == 1 and t > G:
                    reads_evac(t // G - 1)
            def trans_evac(n, dst):
                act.wait_ge(trans_mm, n + 1)
                act.activation(dst, PS[:, (4, 5, 6, 7, 6, 7)[n], :], ACT.Copy).then_inc(trans_ev, 1)

            for n in range(2):
                trans_evac(n, PT[:, 4 * n:4 * n + 4, :].rearrange("p i c -> p (i c)"))
            for n in range(2):
                trans_evac(2 + n, QT0[:, n * 512:(n + 1) * 512])
            for n in range(2):
                trans_evac(4 + n, QT[:, 4 * n:4 * n + 4, :].rearrange("p i c -> p (i c)"))
            reads_evac(NG - 1)
            act.wait_ge(trans_ev, 6)
            PTb = PT.rearrange("p i (b c) -> p b c i", b=B)
            for g in range(NC // CG):
                if g >= 2:
                    for b in range(B):
                        act.wait_ge(scan_mm[b], CG * (g - 1) - 1)
                for h in range(H):
                    o = act.activation(BD[:, g % 2, :, :, h::H], PTb[:, :, g * CG:(g + 1) * CG, :],
                                       ACT.Copy, scale=headof[:, h:h + 1])
                o.then_inc(bd_ready, 1)

            act.wait_ge(o_ready, 1)
            act.activation(osq, oT, ACT.Square).then_inc(osq_ready, 1)
            act.activation(vsq[:, :, :], vT[:, :, :], ACT.Square).then_inc(vsq_ready, 1)
            act.wait_ge(pd_ev, 15 + NG)
            act.activation(gate[:, :, :], gate[:, :, :], ACT.Sigmoid).then_inc(gate_ready, 1)
            act.wait_ge(vms_eps, 2)
            act.activation(vt4[:, 1, :], vt4[:, 0, :], ACT.Sqrt).then_inc(vrms_std, 1)
            act.wait_ge(oms_eps, NG)
            act.activation(osq, orms, ACT.Sqrt).then_inc(orms_std, 1)

        @block.tensor
        def _(pe):
            def tokens_T(l):
                for g in range(NG):
                    pe.wait_ge(layer_x, l * NG + g + 1)
                    if g >= 2:
                        pe.wait_ge(xt_ready, l * NG + g - 1)
                    for t in range(G):
                        m = pe.transpose(PS[:, g % 2, t * P:(t + 1) * P], xcur[:, g * G + t, :], ident[:, :])
                    m.then_inc(xt_tr, 1)

            def logits(l):
                ne = E + 1 if l == 0 else E
                rhs = rw0[:, :] if l == 0 else rw[:, l, :]
                for t in range(NT):
                    if t % G == 0:
                        pe.wait_ge(xt_ready, l * NG + t // G + 1)
                    m = pe.matmul(PS[:, 2, t * ne:(t + 1) * ne], xT[:, t * P:(t + 1) * P], rhs, start=True, stop=True)
                m.then_inc(logits_mm, 1)

            def ranks(l):
                pe.wait_ge(hot_ready, l + 1)
                pe.matmul(PS[:, 3, 0:NT * E], ltri[:, :], hot[:, :, :].rearrange("p t e -> p (t e)"),
                          start=True, stop=False)
                for t in range(NT - 1):
                    later = PS[:, 3, (t + 1) * E:NT * E].rearrange("p (t e) -> p t e", e=E)
                    pe.matmul(later, ones_bf[:, :], hot[:, t:t + 1, :].to_broadcast([P, NT - 1 - t, E]),
                              start=False, stop=(t == NT - 2))
                for t in range(NT):
                    m = pe.matmul(PS[:, 4, 0:E], ones_bf[:, :], hot[:, t, :], start=(t == 0), stop=(t == NT - 1))
                m.then_inc(rank_mm, 1)

            def qkv():
                pe.wait_ge(w_ready, 1)
                for n in range(3 * NG):
                    if n >= 3:
                        pe.wait_ge(qkv_ready, n - 2)
                    bank = PS[:, 5 + n % 3, :]
                    g = n % NG
                    if n < 2 * NG:
                        m = pe.matmul(bank, wT[:, n // NG, :], xT[:, g * 512:(g + 1) * 512], start=True, stop=True)
                    else:
                        for t in range(G):
                            m = pe.matmul(bank[:, t * P:(t + 1) * P], xT[:, (g * G + t) * P:(g * G + t + 1) * P],
                                          wT[:, 2, :], start=True, stop=True)
                    m.then_inc(qkv_mm, 1)

            def attention(b):
                pe.wait_ge(qkv_ready, 3 * NG)
                pe.wait_ge(pos_ready, b + 1)

                def scores(j):
                    n = b * TB + TB - 1 - j
                    if n >= 2:
                        pe.wait_ge(sw_ready, n - 1)
                    w = (j + 1) * P
                    s0 = (b * TB + j) * P
                    for h in range(0, w, 512):
                        e = min(w, h + 512)
                        m = pe.matmul(PS[:, 2 * (n % 2) + h // 512, 0:e - h], kT[:, s0:s0 + P],
                                      qT[:, b * S + h:b * S + e], start=True, stop=True)
                    m.then_inc(score_mm, 1)

                def retrieve(j):
                    n = b * TB + TB - 1 - j
                    pe.wait_ge(sw_ready, n + 1)
                    w = (j + 1) * P
                    for h in range(0, w, 512):
                        e = min(w, h + 512)
                        m = pe.matmul(PS[:, 4 + h // 512, 0:e - h], vtok[:, b * TB + j, :], swt[:, n % 2, h:e],
                                      start=(j == TB - 1), stop=(j == h // P))
                    m.then_inc(ret_mm, 1)

                scores(TB - 1)
                for j in reversed(range(TB)):
                    if j:
                        scores(j - 1)
                    retrieve(j)
                if b:
                    pe.wait_ge(attn_added, b * (TB // G))
                for g in range(TB // G):
                    pe.wait_ge(ret_ev, b * (S // 512) + g + 1)
                    for t in range(G):
                        m = pe.matmul(PS[:, 6 + g, t * P:(t + 1) * P], retT[:, (g * G + t) * P:(g * G + t + 1) * P],
                                      wT[:, 3, :], start=True, stop=True)
                    m.then_inc(proj_mm, 1)

            def prepare():
                pe.wait_ge(ld_l1, LD_L1)
                pe.wait_ge(pos_ready, B + 1)
                for n in range(2):
                    for e in range(4):
                        m = pe.transpose(PS[:, 6 + n, e * D:(e + 1) * D], ew_raw[:, n * 4 + e, :], ident[:, :])
                    m.then_inc(pd_mm, 1)
                pe.wait_ge(diag_ready, 1)
                pe.wait_ge(pd_ev, 1)
                pe.matmul(PS[:, 6, 0:1], wmrow16[0:1, :, :].rearrange("p i h -> p (i h)"), ident[0:1, 0:1],
                          start=True, stop=True).then_inc(pd_mm, 1)
                pe.wait_ge(pd_ev, 3)

            def weights_of(k):
                return pe.value_load(tile_w[0:1, bass.ds(k, 1)])

            def tile_mm(l, k, x, m1, th, m2, par):
                at = l * NS
                if x:
                    pe.wait_ge(x_staged, k + (at + 1))
                    pe.transpose(PS[:, par, 0:P], xstage[:, par, :], ident[:, :]).then_inc(x_tr, 1)
                if m1:
                    pe.wait_ge(x_ev, k + at)
                    w = weights_of(k - 1)
                    pe.matmul(PS[:, 3 - par, :], xTs[:, 1 - par, :], W1s[:, bass.ds(w, FF)],
                              start=True, stop=True).then_inc(h_mm, 1)
                if th:
                    pe.wait_ge(h_act, k + (at - 1))
                    for c in range(FC):
                        m = pe.transpose(PS[:, 4 + par, c * P:(c + 1) * P], hs[:, par, c * P:(c + 1) * P], ident[:, :])
                    m.then_inc(h_tr, 1)
                if m2:
                    pe.wait_ge(h_ev, k + (at - 2))
                    if not th:
                        pe.wait_ge(y_ev, k + (at - 4))
                    w = weights_of(k - 3)
                    for c in range(FC):
                        m = pe.matmul(PS[:, 7 - par, 0:D], hTs[:, 1 - par, c * P:(c + 1) * P],
                                      W2s[:, bass.ds(w + c * D, D)], start=(c == 0), stop=(c == FC - 1))
                    m.then_inc(y_mm, 1)

            pe.wait_ge(consts, 1)
            for l in range(L):
                tokens_T(l)
                if l == 0:
                    pe.wait_ge(ld_small, 16 * 9)
                    for n in range(4):
                        m = pe.transpose(PS[:, 5, n * P:(n + 1) * P], wraw[:, n, :], ident[:, :])
                    m.then_inc(w_tr, 1)
                logits(l)
                ranks(l)
                if l == 0:
                    qkv()
                if l < B:
                    attention(l)
                    pe.wait_ge(attn_added, (l + 1) * (TB // G))
                elif l == B:
                    prepare()
                pe.wait_ge(te_ready, l + 1)
                if l == 0:
                    pe.wait_ge(ld_w1, 16)
                    pe.wait_ge(ld_w2, 16)
                for k in range(PRE):
                    tile_mm(l, k, True, k >= 1, k >= 2, k >= 3, k % 2)
                for a, b in ((PRE, MID), (MID, NS)):
                    with pe.Fori(0, (b - a) // 2) as i:
                        for u in range(2):
                            tile_mm(l, i * 2 + (a + u), True, True, True, True, (a + u) % 2)
                for k in range(NS, NS + 3):
                    tile_mm(l, k, False, k == NS, k <= NS + 1, True, k % 2)

            tokens_T(L)
            pe.wait_ge(xt_ready, NG * (L + 1))
            pe.wait_ge(diag_ready, 2)
            pe.wait_ge(pads, 1)

            aj, dj = [0], [3]

            def abank():
                n = aj[0]
                aj[0] += 1
                if n >= 4:
                    pe.wait_ge(pa_ev, n - 3)
                return PS[:, 2 + n % 4, :]

            def dbank():
                n = dj[0]
                dj[0] += 1
                pe.wait_ge(pd_ev, n - 1)
                return PS[:, 6 + n % 2, :]

            def plane(first_col, stride):
                for h in range(S // 512):
                    o = abank()
                    for b in range(B):
                        m = pe.matmul(o[b * 64:(b + 1) * 64, :], wc[:, first_col:first_col + 63 * stride + 1:stride],
                                      xT[:, b * S + h * 512:b * S + (h + 1) * 512], start=True, stop=True)
                    m.then_inc(pa_mm, 1)

            def ctrl(part):
                for g in range(NG):
                    pe.matmul(abank(), wc[:, OFF[part]:OFF[part + 1]], xT[:, g * 512:(g + 1) * 512],
                              start=True, stop=True).then_inc(pa_mm, 1)

            def conv(n):
                before = aj[0] - NG
                for b in range(B):
                    for h in range(S // 512):
                        o = abank()
                        pe.wait_ge(pa_ev, before + b * 2 + h + 1)
                        for j in range(K):
                            m = pe.matmul(o, tapdiag[:, n * K + j, :], pre[:, n, b, h * 512 + j:h * 512 + j + 512],
                                          start=(j == 0), stop=(j == K - 1))
                        m.then_inc(pa_mm, 1)

            def by_step(v, t):
                return v.rearrange("p (c t) -> p t c", t=C)[:, t, :]

            def sumsq(n):
                o = dbank()
                pe.wait_ge(sq_ready, n + 1)
                for t in range(C):
                    m = pe.matmul(o[:, t * H:(t + 1) * H], by_step(sqb, t), headsel[:, :], start=True, stop=True)
                m.then_inc(pd_mm, 1)

            def chunks(v, bank, done):
                for g in range(NG):
                    o = bank()
                    for t in range(G):
                        m = pe.transpose(o[:, t * P:(t + 1) * P], by_step(v, g * G + t), ident[:, :])
                    m.then_inc(done, 1)

            plane(OFF[0], 2)
            plane(OFF[0] + 1, 2)
            o = dbank()
            for t in range(C):
                m = pe.matmul(o[:, t * 2 * H:(t + 1) * 2 * H], by_step(xT[:, :], t), wc[:, OFF[6]:OFF[8]], start=True, stop=True)
            m.then_inc(pd_mm, 1)
            plane(OFF[2], 2)
            plane(OFF[2] + 1, 2)
            plane(OFF[1], 1)
            ctrl(4)
            conv(0)
            ctrl(3)
            sumsq(0)
            conv(1)
            ctrl(5)
            sumsq(1)
            conv(2)
            chunks(post[0], dbank, pd_mm)
            chunks(post[1], dbank, pd_mm)
            pe.wait_ge(pa_ev, aj[0])
            chunks(post[2], abank, pa_mm)
            o = dbank()
            for t in range(NT):
                m = pe.matmul(o[:, t * E1:(t + 1) * E1], xT[:, t * P:(t + 1) * P], rw1[:, :], start=True, stop=True)
            m.then_inc(pd_mm, 1)
            o = abank()
            pe.wait_ge(sel_ready, 1)
            for g in range(NG):
                m = pe.transpose(o[:, g * P:(g + 1) * P], sel[:, g * G:(g + 1) * G, :].rearrange("p t e -> p (t e)"),
                                 ident[:, :])
            m.then_inc(pa_mm, 1)

            pe.wait_ge(pa_ev, PA_ALL)
            for t in range(C):
                g = t // G
                if t % G == 0 and g >= 2:
                    pe.wait_ge(rT_ev, 2 * (g - 1))
                pe.wait_ge(r_ready, t + 1)
                for n in range(2):
                    for i in range(HD):
                        m = pe.matmul(PS[:, 2 * n + g % 2, (t % G) * P:(t % G + 1) * P],
                                      qX[t % 2].rearrange("p c h i -> p (c h) i")[:, n * P:(n + 1) * P, i], ident[:, :],
                                      start=(i == 0), stop=(i == HD - 1))
                m.then_inc(rT_mm, 1)
            pe.wait_ge(x_new, C)
            pe.wait_ge(pd_ev, dj[0])
            for n in range(4):
                for i in range(4):
                    x = X[C % 2]
                    if n < 2:
                        src = x.rearrange("p c h i -> p (c h) i")[:, 0:P, n * 4 + i]
                    else:
                        src = x[:, HD + (n - 2) * 4 + i, :, :].rearrange("p h i -> p (h i)")
                    m = pe.transpose(PS[:, 4 + n, i * P:(i + 1) * P], src, ident[:, :])
                m.then_inc(trans_mm, 1)
            for n in range(2):
                pe.wait_ge(trans_ev, 3 + n)
                pe.matmul(PS[:, 6 + n, :], perm[:, :], QT0[:, n * 512:(n + 1) * 512],
                          start=True, stop=True).then_inc(trans_mm, 1)
            pe.wait_ge(trans_ev, 6)

            def experts(t):
                if t:
                    pe.wait_ge(y1_ev, t)
                for n in range(E1 * D // 512):
                    m = pe.matmul(PS[:, 6 + n, :], xT[:, t * P:(t + 1) * P], ewT[:, n * 512:(n + 1) * 512],
                                  start=True, stop=True)
                m.then_inc(y1_mm, 1)

            def correct(g):
                if g == 0:
                    pe.wait_ge(rT_ev, 2 * NG)
                pe.wait_ge(bds_ready, B * (g + 1))
                for b in range(B):
                    for c in range(CG):
                        ch = b * NC + g * CG + c
                        m = pe.matmul(PS[:, ch // 32, (ch % 32) * C:(ch % 32 + 1) * C], BDS[:, g % 2, b, c, :],
                                      qeffT[:, :, ch], start=True, stop=True)
                m.then_inc(corr_mm, 1)

            for c in range(1, NC - 1):
                if c % CG == 0 or c == 1:
                    pe.wait_ge(bd_ready, c // CG + 1)
                for b in range(B):
                    pe.wait_ge(s_ready[b], c)
                    pe.matmul(PS[:, 4 + b, 0:HD], BD[:, (c // CG) % 2, b, c % CG, :], Sall[:, b * NC + c, :],
                              start=True, stop=True).then_inc(scan_mm[b], 1)
                if c % CG == CG - 1 and c >= 2 * CG - 1:
                    correct(c // CG - 1)
                if c >= VL and (c - VL) % 2 == 0:
                    experts((c - VL) // 2)
            for t in range((NC - 2 - VL) // 2 + 1, NT):
                experts(t)
            for b in range(B):
                pe.wait_ge(s_ready[b], NC - 1)
            for g in range((NC - 2) // CG - 0 if (NC - 2) % CG == CG - 1 else (NC - 2) // CG - 1, NC // CG):
                correct(g)
            pe.wait_ge(y1_ev, NT)
            for g in range(NG):
                o = dbank()
                for t in range(G):
                    tt = g * G + t
                    m = pe.matmul(o[:, t * P:(t + 1) * P], xT[:, tt * P:(tt + 1) * P], wc[:, OFF[8]:OFF[9]],
                                  start=True, stop=True)
                m.then_inc(pd_mm, 1)
            for g in range(NG):
                o = dbank()
                if g == 0:
                    pe.wait_ge(ld_ebias, 16 * G)
                pe.matmul(o, selT[:, g * P:(g + 1) * P], ebias.rearrange("p t o -> p (t o)"),
                          start=True, stop=True).then_inc(pd_mm, 1)
            pe.wait_ge(vsum, 1)
            for n in range(2):
                pe.matmul(PS[:, 4 + n, :], seqmean[:, :], vsq[:, 0, n * 512:(n + 1) * 512],
                          start=True, stop=True).then_inc(vms_mm, 1)
            pe.wait_ge(osq_ready, 1)
            for n in range(NG):
                pe.matmul(PS[:, n, :], headmean[:, :], osq[:, n * 512:(n + 1) * 512],
                          start=True, stop=True).then_inc(oms_mm, 1)
            pe.wait_ge(vn_ready, 1)
            pe.wait_ge(m_ready, 1)
            for g in range(NG):
                for t in range(G):
                    tt = g * G + t
                    b, tb = tt // TB, tt % TB
                    half = slice(b * 64, (b + 1) * 64)
                    o = PS[:, 2 + g, t * D:(t + 1) * D]
                    pe.matmul(o, mT[:, tt * P:(tt + 1) * P], wo_m[:, :], start=True, stop=False)
                    for r in range(2):
                        m = pe.matmul(o, vT[half, r, tb * P:(tb + 1) * P], wo_v[half, r, :], start=False, stop=(r == 1))
                m.then_inc(out_mm, 1)


_INS = ["L0_attn_x", "L0_attn_Wq", "L0_attn_Wk", "L0_attn_Wv", "L0_attn_Wo", "L0_attn_Wd", "L0_attn_bd",
        "L0_attn_out_scale", "L0_ffn_routers", "L0_ffn_W1", "L0_ffn_W2", "L1_attn_W_ctrl", "L1_attn_b_ctrl",
        "L1_attn_W_block", "L1_attn_qconv_w", "L1_attn_kconv_w", "L1_attn_vconv_w", "L1_attn_rms_m_w",
        "L1_attn_rms_v_w", "L1_attn_W_out", "L1_attn_b_out", "L1_ffn_router_w", "L1_ffn_router_b",
        "L1_ffn_expert_w", "L1_ffn_expert_b"]
_TRANSPOSED = ["L1_ffn_router_w"]
_OUTS = [((2, 1024, 128), "float32")]


def kernel(**inputs):
    import numpy as _np
    import concourse.bacc as _bacc
    from concourse import mybir as _mybir
    from concourse.bass_utils import run_bass_kernel_spmd as _run

    nc = _bacc.Bacc("TRN2", target_bir_lowering=False, num_devices=1)
    arrays, args = {}, {}
    for name in _INS:
        a = _np.ascontiguousarray(_np.asarray(inputs[name]).T if name in _TRANSPOSED else inputs[name])
        arrays[f"in_{name}_dram"] = a
        args[name] = nc.dram_tensor(f"in_{name}_dram", a.shape, _mybir.dt.from_np(a.dtype), kind="ExternalInput").ap()
    outs = []
    for i, (shape, dtype) in enumerate(_OUTS):
        dt = _mybir.dt.from_np(_np.dtype(dtype))
        outs.append(nc.dram_tensor(f"out_{i}_dram", shape, dt, kind="ExternalOutput").ap())
    build(nc, args, outs[0])
    r = _run(nc, [arrays], core_ids=[0])
    return r.results[0]["out_0_dram"]
```

```python
import math

import concourse.bass as bass
from concourse import mybir
from contextlib import ExitStack

F32 = mybir.dt.float32
BF16 = mybir.dt.bfloat16
I32 = mybir.dt.int32
ALU = mybir.AluOpType
ACT = mybir.ActivationFunctionType
AX_X = mybir.AxisListType.X


def build(nc, ins, out):
    x_in = ins["L0_attn_x"]
    B, S, D = x_in.shape
    P = 128
    N = B * S
    NT = N // P
    TB = S // P
    routers, W1, W2 = ins["L0_ffn_routers"], ins["L0_ffn_W1"], ins["L0_ffn_W2"]
    L, _, E = routers.shape
    FF = W1.shape[2]
    FC = FF // P
    NS = NT + E - 1
    SCALE = float(D) ** -0.5
    G = 4
    NG = NT // G
    R = 4
    PRE = R + (NS - R) % R
    XW = D + 2
    E1 = ins["L1_ffn_expert_w"].shape[0]
    HD = ins["L1_attn_rms_m_w"].shape[0]
    H = D // HD
    K = ins["L1_attn_qconv_w"].shape[1]
    NCTRL = ins["L1_attn_W_ctrl"].shape[1]
    sizes = [D, D // 2, D, D, D, D, H, H, D]
    OFF = [sum(sizes[:n]) for n in range(len(sizes) + 1)]
    C = N // P
    NC = S // C
    CG = 8
    VL = 32
    VC = S // VL
    assert B * NC == P and B * (D // 2) == P and OFF[-1] == NCTRL
    assert D == P and (NS - PRE) % R == 0 and PRE > R

    xs_dram = [nc.dram_tensor(f"sorted_x{l}", [NS * P, XW], F32, kind="Internal") for l in range(L)]
    y_dram = nc.dram_tensor("results", [N + NS * P, D], F32, kind="Internal")

    with ExitStack() as ctx:
        def sb(name, shape, dt=F32):
            return ctx.enter_context(nc.sbuf_tensor(name, shape, dt))

        def sem(name):
            return ctx.enter_context(nc.semaphore(name))

        PS = ctx.enter_context(nc.psum_tensor("PS", [P, 8, 512], F32))

        W1s = sb("W1s", [P, E * FF])
        W2s = sb("W2s", [P, E * FC * D])
        xres = sb("xres", [P, NT, D])
        xrow = sb("xrow", [P, NT, XW])
        xcur = xrow[:, :, 0:D]
        xT = sb("xT", [P, N])
        slotbuf = sb("slotbuf", [P, 4 * S])
        blank = slotbuf[:, 0:NS * XW].rearrange("p (t d) -> p t d", d=XW)
        qT = sb("qT", [P, N])
        kT = sb("kT", [P, N])
        vtok = sb("vtok", [P, NT, D])
        wdec = sb("wdec", [P, 2, S])
        swt = sb("swt", [P, 2, S])
        retT = sb("retT", [P, S])
        ident = sb("ident", [P, P])
        ltri = sb("ltri", [P, P], BF16)
        ones_bf = sb("ones_bf", [P, P], BF16)
        dist_i = retT[:, :].bitcast(I32)
        dist = sb("dist", [P, S])
        after = sb("after", [P, P])
        row_i = sb("row_i", [P, NS], I32)
        rev_i = sb("rev_i", [P, E], I32)
        rev = sb("rev", [P, E])
        tix_i = sb("tix_i", [P, NS], I32)
        tix = sb("tix", [P, NS])
        one_e = sb("one_e", [P, E])
        rw = sb("rw", [P, L, E])
        rw0 = sb("rw0", [P, E + 1])
        wraw = sb("wraw", [P, 4, D])
        wT = sb("wT", [P, 4, D])
        bd = sb("bd", [P, 1])
        oscale = sb("oscale", [P, 1])
        stat = sb("stat", [P, 4, NT])
        lg = sb("lg", [P, NT, E + 1])
        sh = sb("sh", [P, NT, E])
        ex = sb("ex", [P, NT, E])
        rt = sb("rt", [P, NT, E])
        hot = sb("hot", [P, NT, E], BF16)
        hotf = sb("hotf", [P, NT, E])
        mx = sb("mx", [P, NT])
        esum = sb("esum", [P, NT])
        wprob = sb("wprob", [P, NT])
        first = sb("first", [P, NT])
        ldec = sb("ldec", [P, 3, NT])
        cnt_i = sb("cnt_i", [P, 2, E], I32)
        ecnt = sb("ecnt", [P, 3, E])
        posf = sb("posf", [P, NT])
        pos = sb("pos", [P, NT], I32)
        tcmpbuf = sb("tcmpbuf", [P, 4 * P])
        tcmp = tcmpbuf[:, 0:NS * E].rearrange("p (s e) -> p s e", e=E)
        texp = sb("texp", [P, 2, NS])
        tile_w = sb("tile_w", [P, NS], I32)
        slot_id = sb("slot_id", [P, R], I32)
        slot_w = sb("slot_w", [P, R])
        xTs = sb("xTs", [P, 2, P])
        hbuf = sb("hbuf", [P, 2 * S])
        hTs = hbuf[:, 0:2 * FF].rearrange("p (b f) -> p b f", b=2)
        xring = hbuf[:, 2 * FF:2 * FF + R * XW].rearrange("p (r d) -> p r d", r=R)
        yring = wdec[:, 0, 0:R * D].rearrange("p (r d) -> p r d", r=R)
        w1st = swt[:, 0, 0:2 * FF].rearrange("p (b f) -> p b f", b=2)
        w2st = swt[:, 1, 0:2 * FF].rearrange("p (b f) -> p b f", b=2)

        wc = sb("wc", [P, NCTRL])
        ew_raw = sb("ew_raw", [P, E1, D])
        ewT = sb("ewT", [P, E1 * D])
        ebias = ew_raw[:, 0:G, :]
        rw1 = sb("rw1", [P, E1])
        rb1 = sb("rb1", [P, E1])
        taps = sb("taps", [P, 3, K])
        tapdiag = sb("tapdiag", [P, 3 * K, P])
        cbias = sb("cbias", [P, 3])
        pbias = sb("pbias", [P, 5])
        abbias = sb("abbias", [P, 2 * H])
        ogbias = sb("ogbias", [P, D])
        obias = sb("obias", [P, D])
        wblk = sb("wblk", [P, 4])
        nwblk = sb("nwblk", [P, 4])
        wmrow = sb("wmrow", [1, HD])
        wmrow16 = sb("wmrow16", [1, HD, H])
        wmcol = sb("wmcol", [P, 1])
        wvcol = sb("wvcol", [P, 2])
        wo_m = sb("wo_m", [P, D])
        wo_v = sb("wo_v", [P, 2, D])
        headsel = sb("headsel", [P, H])
        headmean = sb("headmean", [P, P])
        headof = sb("headof", [P, H])
        perm = sb("perm", [P, P])
        seqmean = sb("seqmean", [P, P])
        abraw = sb("abraw", [P, C, 2 * H])
        ab = sb("ab", [P, C, 2 * H])
        nvar = wraw[:, :, :].rearrange("p (n m) d -> p n (m d)", n=2)
        nstd = wT[:, :, :].rearrange("p (n m) d -> p n (m d)", n=2)
        pred = ex[:, :, :].rearrange("p t e -> p (t e)").rearrange("p (c h) -> p c h", h=H)
        vtmp = wT[:, 0:3, :].rearrange("p n d -> p (n d)").rearrange("p (r i q) -> p r i q", r=2, i=2)
        y0 = sb("y0", [P, VC + 1, 2])
        lg1 = tcmpbuf[:, :].rearrange("p (n t e) -> p n t e", n=4, e=E1)
        sel = sb("sel", [P, NT, 32])
        rev1 = rev[:, E - E1:E]

        U = 2 * S
        u = [W1s[:, n * U:(n + 1) * U] for n in range(4)] + [W2s[:, n * U:(n + 1) * U] for n in range(4)]
        pre = W1s[:, 0:3 * B * (K - 1 + S)].rearrange("p (n b t) -> p n b t", n=3, b=B)
        post = [u[4], u[5], u[6]]
        sqb = u[7]
        u0p, u1p = swt[:, 0, :], swt[:, 1, :]
        angp, kp, cosp = retT[:, :], dist[:, :], W1s[:, 7 * S:8 * S]
        sinp = kp
        mpl = slotbuf[:, :].rearrange("p (r i t) -> p r i t", r=2, i=2)
        zneg = hbuf[:, :].rearrange("p (r t) -> p r t", r=2)
        Kc = qT[:, :].rearrange("p (t h i) -> p t h i", t=C, h=H)
        Qc = kT[:, :].rearrange("p (t h i) -> p t h i", t=C, h=H)
        Vc = vtok[:, :, :].rearrange("p t (h i) -> p t h i", h=H)
        bKc = wdec[:, :, :].rearrange("p b (t h i) -> p (b t) h i", h=H, i=HD)
        xcur_f = xrow[:, :, :].rearrange("p t d -> p (t d)")[:, 0:N]
        X = [v.rearrange("p (c h i) -> p c h i", h=H, i=HD) for v in (xcur_f, u[0])]
        tmp = u[1].rearrange("p (c h i) -> p c h i", h=H, i=HD)
        aX = u[2].rearrange("p (c h i) -> p c h i", h=H, i=HD)
        qX = [v.rearrange("p (c h i) -> p c h i", h=H, i=HD) for v in (u[3], u[7])]
        qeffT = u[4].rearrange("p (t c) -> p t c", t=C)
        olocT = swt[:, :, :].rearrange("p b (t c) -> p (b t) c", c=P)
        PT = qT[:, 0:S].rearrange("p (i c) -> p i c", i=HD)
        QT0 = kT[:, S:U]
        QT = qT[:, S:U].rearrange("p (j c) -> p j c", j=HD)
        Sall = kT[:, 0:S].rearrange("p (c j) -> p c j", j=HD)
        BD = W1s[:, 0:2 * U].rearrange("p (n b c m) -> p n b c m", n=2, b=B, c=CG)
        BDS = W1s[:, 2 * U:4 * U].rearrange("p (n b c m) -> p n b c m", n=2, b=B, c=CG)
        Y = W2s[:, U:U + 6 * S].rearrange("p (t r q c) -> p t r q c", t=VL, r=2, q=3)
        gate = vtok
        oT = u[4]
        osq = wdec[:, :, :].rearrange("p b t -> p (b t)")
        orms = u[0]
        mT = u[1]
        vT = u[2].rearrange("p (r t) -> p r t", r=2)
        vsq = u[3].rearrange("p (r t) -> p r t", r=2)
        vt4 = xcur_f.rearrange("p (r t) -> p r t", r=2)
        selT = abraw[:, :, :].rearrange("p t h -> p (t h)")

        ld_x = sem("ld_x")
        ld_small = sem("ld_small")
        ld_w1 = sem("ld_w1")
        ld_w2 = sem("ld_w2")
        zeroed = sem("zeroed")
        xs_cleared = [sem(f"xs_cleared{l}") for l in range(L)]
        ld_tile = [sem(f"ld_tile{r}") for r in range(R)]
        consts = sem("consts")
        pool_seq = sem("pool_seq")
        dve_seq = sem("dve_seq")
        act_seq = sem("act_seq")
        layer_x = sem("layer_x")
        xt_tr = sem("xt_tr")
        xt_ready = sem("xt_ready")
        logits_mm = sem("logits_mm")
        shifted = sem("shifted")
        exp_done = sem("exp_done")
        hot_ready = sem("hot_ready")
        rank_mm = sem("rank_mm")
        pos_ready = sem("pos_ready")
        te_ready = sem("te_ready")
        scattered = sem("scattered")
        ld_tok = [sem(f"ld_tok{g}") for g in range(NG)]
        x_tr = sem("x_tr")
        x_ev = sem("x_ev")
        w1_staged = sem("w1_staged")
        w2_staged = sem("w2_staged")
        id_ready = sem("id_ready")
        h_mm = sem("h_mm")
        h_act = sem("h_act")
        y_mm = sem("y_mm")
        y_ev = sem("y_ev")
        y_put = [sem(f"y_put{r}") for r in range(R)]
        w_tr = sem("w_tr")
        w_ready = sem("w_ready")
        dec_sig = sem("dec_sig")
        dec_eps = sem("dec_eps")
        dec_log = sem("dec_log")
        ln_var = sem("ln_var")
        ln_std = sem("ln_std")
        qkv_mm = sem("qkv_mm")
        qkv_ready = sem("qkv_ready")
        score_mm = sem("score_mm")
        decay_w = sem("decay_w")
        sw_ready = sem("sw_ready")
        ret_mm = sem("ret_mm")
        ret_ev = sem("ret_ev")
        proj_mm = sem("proj_mm")
        attn_added = sem("attn_added")
        st_out = sem("st_out")
        ld_l1 = sem("ld_l1")
        ld_ebias = sem("ld_ebias")
        consts1 = sem("consts1")
        x2_ready = sem("x2_ready")
        diag_ready = sem("diag_ready")
        pads = sem("pads")
        xstate0 = sem("xstate0")
        pa_mm = sem("pa_mm")
        pa_ev = sem("pa_ev")
        pd_mm = sem("pd_mm")
        pd_ev = sem("pd_ev")
        ab_ready = sem("ab_ready")
        sq_ready = sem("sq_ready")
        nrm_std = sem("nrm_std")
        nrm_rec = sem("nrm_rec")
        ang_red = sem("ang_red")
        sincos = sem("sincos")
        bk_ready = sem("bk_ready")
        sh1 = sem("sh1")
        ex1 = sem("ex1")
        sel_ready = sem("sel_ready")
        x_new = sem("x_new")
        ax_ready = sem("ax_ready")
        r_ready = sem("r_ready")
        rT_mm = sem("rT_mm")
        rT_ev = sem("rT_ev")
        trans_mm = sem("trans_mm")
        trans_ev = sem("trans_ev")
        bd_ready = sem("bd_ready")
        s0_ready = sem("s0_ready")
        scan_mm = [sem(f"scan_mm{b}") for b in range(B)]
        s_ready = [sem(f"s_ready{b}") for b in range(B)]
        bds_ready = sem("bds_ready")
        corr_mm = sem("corr_mm")
        y1_mm = sem("y1_mm")
        y1_ev = sem("y1_ev")
        o_ready = sem("o_ready")
        osq_ready = sem("osq_ready")
        oms_mm = sem("oms_mm")
        oms_eps = sem("oms_eps")
        orms_std = sem("orms_std")
        m_ready = sem("m_ready")
        vsq_ready = sem("vsq_ready")
        vsum = sem("vsum")
        vms_mm = sem("vms_mm")
        vms_eps = sem("vms_eps")
        vrms_std = sem("vrms_std")
        vn_ready = sem("vn_ready")
        gate_ready = sem("gate_ready")
        out_mm = sem("out_mm")
        x3_ready = sem("x3_ready")

        block = ctx.enter_context(nc.Block())

        LD_L1 = 16 * (4 + 2 * 3 + 6 * B + HD + 4)
        PA_ALL = 10 + 6 * NG + NG + 1
        TWO_PI = 2 * math.pi
        TWO_PI_HI = 6.28125
        TWO_PI_LO = TWO_PI - TWO_PI_HI
        PI_DOWN = 3.1415925
        ROUND = 1.5 * 2 ** 23

        y_tiles = y_dram[0:N, :].rearrange("(t p) d -> p t d", p=P)
        xs_tiles = [xs[:, :].rearrange("(t p) d -> p t d", p=P) for xs in xs_dram]
        USES = [(NS - r + R - 1) // R for r in range(R)]

        def passed(l, i, c):
            return i + (c // R + 1 + l * USES[c % R])

        x_tiles = x_in.rearrange("b (t p) d -> p (b t) d", p=P)

        @block.sync
        def _(sp):
            for g in range(NG):
                sp.dma_start(xres[:, g * G:(g + 1) * G, :], x_tiles[:, g * G:(g + 1) * G, :]).then_inc(ld_x, 16)
            for n, w in enumerate(("Wq", "Wk", "Wv", "Wo")):
                sp.dma_start(wraw[:, n, :], ins[f"L0_attn_{w}"][:, :]).then_inc(ld_small, 16)
            sp.dma_start(rw[:, :, :], routers.rearrange("l d e -> d l e")).then_inc(ld_small, 16)
            sp.dma_start(rw0[:, 0:E], routers[0, :, :]).then_inc(ld_small, 16)
            sp.dma_start(rw0[:, E:E + 1], ins["L0_attn_Wd"].rearrange("o d -> d o")).then_inc(ld_small, 16)
            sp.dma_start(bd[:, :], ins["L0_attn_bd"].partition_broadcast(P)).then_inc(ld_small, 16)
            sp.dma_start(oscale[:, :], ins["L0_attn_out_scale"].partition_broadcast(P)).then_inc(ld_small, 16)
            sp.wait_ge(zeroed, 1)
            sp.dma_start(xs_tiles[0], blank).then_inc(xs_cleared[0], 16)
            sp.dma_start(W1s[:, :].rearrange("d (e f) -> d e f", e=E), W1.rearrange("e d f -> d e f")).then_inc(ld_w1, 16)
            sp.dma_start(W2s[:, :].rearrange("p (e c d) -> p e c d", e=E, c=FC),
                         W2.rearrange("e (c p) d -> p e c d", p=P)).then_inc(ld_w2, 16)
            for l in range(1, L):
                sp.dma_start(xs_tiles[l], blank).then_inc(xs_cleared[l], 16)
            def load(dst, src):
                sp.dma_start(dst, src).then_inc(ld_l1, 16)

            b_ctrl = ins["L1_attn_b_ctrl"]
            load(wc[:, :], ins["L1_attn_W_ctrl"][:, :])
            load(ew_raw[:, :, :], ins["L1_ffn_expert_w"].rearrange("e o d -> o e d"))
            load(rw1[:, :], ins["L1_ffn_router_w"][:, :])
            load(rb1[:, :], ins["L1_ffn_router_b"].partition_broadcast(P))
            for n, w in enumerate("kqv"):
                load(taps[:, n, :], ins[f"L1_attn_{w}conv_w"][:, :])
                part = OFF[{"q": 3, "k": 4, "v": 5}[w]]
                load(cbias[:, n:n + 1], b_ctrl[part:part + D].rearrange("(p o) -> p o", o=1))
            for b in range(B):
                half = slice(b * D // 2, (b + 1) * D // 2)
                for n, part in ((0, OFF[0]), (2, OFF[2])):
                    load(pbias[half, n:n + 2], b_ctrl[part:part + D].rearrange("(p r) -> p r", r=2))
                load(pbias[half, 4:5], b_ctrl[OFF[1]:OFF[2]].rearrange("(p o) -> p o", o=1))
                load(wblk[half, :], ins["L1_attn_W_block"].rearrange("p i j -> p (i j)"))
                load(wvcol[half, :], ins["L1_attn_rms_v_w"].rearrange("(p r) -> p r", r=2))
                load(wo_v[half, :, :], ins["L1_attn_W_out"][D:2 * D, :].rearrange("(p r) o -> p r o", r=2))
            for j in range(HD):
                load(wo_m[j * H:(j + 1) * H, :], ins["L1_attn_W_out"][0:D, :].rearrange("(h j) o -> j h o", h=H)[j])
            load(abbias[:, :], b_ctrl[OFF[6]:OFF[8]].partition_broadcast(P))
            load(ogbias[:, :], b_ctrl[OFF[8]:OFF[9]].partition_broadcast(P))
            load(obias[:, :], ins["L1_attn_b_out"].partition_broadcast(P))
            load(wmrow[:, :], ins["L1_attn_rms_m_w"].rearrange("(o i) -> o i", o=1))
            for l in range(L):
                def load_tile(i, c):
                    k = i * R + c
                    r = c % R
                    if c >= R:
                        sp.wait_ge(x_tr, k + (l * NS - R + 1))
                        sp.wait_ge(id_ready, k * 2 + 2 * (l * NS - R + 1))
                    src = xs_tiles[l][:, bass.ds(k, 1), :].rearrange("p t d -> p (t d)") if not isinstance(k, int) \
                        else xs_tiles[l][:, k, :]
                    sp.dma_start(xring[:, r, :], src).then_inc(ld_tile[r], 16)

                sp.wait_ge(scattered, 16 * NT * (l + 1))
                for k in range(PRE):
                    load_tile(0, k)
                with sp.Fori(0, (NS - PRE) // R) as i:
                    for n in range(R):
                        load_tile(i, PRE + n)
                for r in range(R):
                    sp.wait_ge(y_put[r], 16 * USES[r] * (l + 1))
                for g in range(NG):
                    tt = slice(g * G, (g + 1) * G)
                    sp.dma_start(xcur[:, tt, :], y_tiles[:, tt, :]).then_inc(ld_tok[g], 16)
            sp.wait_ge(pads, 1)
            for t in range(G):
                sp.dma_start(ebias[32 * t:32 * t + E1, t, :], ins["L1_ffn_expert_b"][:, :]).then_inc(ld_ebias, 16)
            out_tiles = out.rearrange("b (t p) d -> p (b t) d", p=P)
            for g in range(NG):
                sp.wait_ge(x3_ready, g + 1)
                sp.dma_start(out_tiles[:, g * G:(g + 1) * G, :], xres[:, g * G:(g + 1) * G, :]).then_inc(st_out, 16)
            sp.wait_ge(st_out, 16 * NG)

        @block.gpsimd
        def _(pool):
            seq = [0]

            def step(ins_):
                seq[0] += 1
                ins_.then_inc(pool_seq, 1)
                pool.wait_ge(pool_seq, seq[0])

            step(pool.memset(slotbuf[:, :], 0.0))
            step(pool.iota(row_i[:, 0:NS], pattern=[[P, NS]], base=N, channel_multiplier=1))
            pool.tensor_copy(blank[:, :, D], row_i[:, 0:NS]).then_inc(zeroed, 1)
            pool.wait_ge(zeroed, 1)
            step(pool.iota(row_i[:, 0:NT], pattern=[[P, NT]], base=0, channel_multiplier=1))
            step(pool.tensor_copy(xrow[:, :, D], row_i[:, 0:NT]))
            step(pool.memset(ident[:, :], 0.0))
            step(pool.affine_select(out=ident[:, :], in_=ident[:, :], compare_op=ALU.not_equal, fill=1.0,
                                    base=0, pattern=[[-1, P]], channel_multiplier=1))
            step(pool.memset(ones_bf[:, :], 1.0))
            step(pool.affine_select(out=ltri[:, :], in_=ones_bf[:, :], compare_op=ALU.is_gt, fill=0.0,
                                    base=0, pattern=[[1, P]], channel_multiplier=-1))
            step(pool.memset(after[:, :], 1.0))
            step(pool.affine_select(out=after[:, :], in_=after[:, :], compare_op=ALU.is_gt, fill=0.0,
                                    base=0, pattern=[[-1, P]], channel_multiplier=1))
            step(pool.iota(dist_i[:, :], pattern=[[-1, S]], base=S - P - 1, channel_multiplier=1))
            step(pool.tensor_scalar(dist[:, :], dist_i[:, :], 0.0, None, ALU.max))
            step(pool.iota(rev_i[:, :], pattern=[[-1, E]], base=E, channel_multiplier=0))
            step(pool.tensor_copy(rev[:, :], rev_i[:, :]))
            step(pool.iota(tix_i[:, :], pattern=[[1, NS]], base=0, channel_multiplier=0))
            step(pool.tensor_copy(tix[:, :], tix_i[:, :]))
            pool.memset(one_e[:, :], 1.0).then_inc(consts, 1)
            pool.wait_ge(consts, 1)
            step(pool.memset(headsel[:, :], 1.0))
            step(pool.affine_select(out=headsel[:, :], in_=headsel[:, :], compare_op=ALU.is_ge, fill=0.0,
                                    base=0, pattern=[[-HD, H]], channel_multiplier=1))
            step(pool.affine_select(out=headsel[:, :], in_=headsel[:, :], compare_op=ALU.is_ge, fill=0.0,
                                    base=HD - 1, pattern=[[HD, H]], channel_multiplier=-1))
            step(pool.memset(headof[:, :], 0.0))
            for i in range(HD):
                step(pool.affine_select(out=headof[:, :], in_=headof[:, :], compare_op=ALU.not_equal, fill=1.0,
                                        base=-H * i, pattern=[[-1, H]], channel_multiplier=1))
            step(pool.tensor_scalar(headmean[:, :].rearrange("p (i h) -> p i h", h=H),
                                    headof[:, :].unsqueeze(1).to_broadcast([P, HD, H]), 1.0 / HD, None, ALU.mult))
            step(pool.memset(perm[:, :], 0.0))
            perm3 = perm[:, :].rearrange("p (i h) -> p i h", h=H)
            step(pool.affine_select(out=perm3, in_=perm3, compare_op=ALU.not_equal, fill=1.0,
                                    base=0, pattern=[[-1, HD], [-HD, H]], channel_multiplier=1))
            step(pool.memset(seqmean[:, :], 0.0))
            for b in range(B):
                half = slice(b * P // B, (b + 1) * P // B)
                step(pool.memset(seqmean[half, half], 1.0 / D))
            pool.memset(sel[:, :, :], 0.0).then_inc(consts1, 1)
            pool.wait_ge(consts1, 1)
            for l in range(L):
                pool.wait_ge(xs_cleared[l], 16)
                pool.wait_ge(pos_ready, l + 1)
                for t in range(NT):
                    pool.indirect_dma_start(xs_dram[l][:, :], bass.IndirectOffsetOnAxis(ap=pos[:, t:t + 1], axis=0),
                                            xrow[:, t, :], None).then_inc(scattered, 16)

                def put(i, c):
                    k = i * R + c
                    r = c % R
                    ids, results = (k * 2 + 2 * (l * NS + 1), k + (l * NS + 1))
                    if not isinstance(k, int):
                        ids, results = pool.to_reg(ids), pool.to_reg(results)
                    pool.wait_ge(xs_cleared[l], 16)
                    pool.wait_ge(id_ready, ids)
                    pool.wait_ge(y_ev, results)
                    pool.indirect_dma_start(y_dram[:, :], bass.IndirectOffsetOnAxis(ap=slot_id[:, r:r + 1], axis=0),
                                            yring[:, r, :], None).then_inc(y_put[r], 16)

                for k in range(PRE):
                    put(0, k)
                with pool.Fori(0, (NS - PRE) // R) as i:
                    for n in range(R):
                        put(i, PRE + n)

            step(pool.memset(ebias, 0.0))
            step(pool.memset(pre[:, 0, :, 0:K - 1], 0.0))
            step(pool.memset(pre[:, 1, :, 0:K - 1], 0.0))
            pool.memset(pre[:, 2, :, 0:K - 1], 0.0).then_inc(pads, 1)
            pool.wait_ge(xt_tr, NG * (L + 1))
            step(pool.memset(xcur_f, 0.0))
            pool.affine_select(out=X[0], in_=X[0], compare_op=ALU.not_equal, fill=1.0, base=0,
                               pattern=[[1, 2 * HD], [0, H], [-1, HD]], channel_multiplier=0).then_inc(xstate0, 1)
            pool.wait_ge(pd_ev, 6 + NG)
            pool.wait_ge(ab_ready, 1)
            pool.tensor_tensor(bKc, Kc, ab[:, :, H:2 * H].unsqueeze(3).to_broadcast([P, C, H, HD]),
                               ALU.mult).then_inc(bk_ready, 1)
            pool.wait_ge(pd_ev, 6 + 2 * NG)
            for t in range(C):
                pool.wait_ge(x_new, t + 1)
                if t >= 2:
                    pool.wait_ge(rT_mm, t - 1)
                pool.tensor_tensor(qX[t % 2], X[(t + 1) % 2], Qc[:, t, :, :].unsqueeze(1).to_broadcast([P, 2 * HD, H, HD]),
                                   ALU.mult).then_inc(r_ready, 1)
            pool.wait_ge(r_ready, C)
            step(pool.memset(Sall[:, 0:1, :], 0.0))
            pool.memset(Sall[:, NC:NC + 1, :], 0.0).then_inc(s0_ready, 1)
            pool.wait_ge(s0_ready, 1)
            for g in range(NC // CG):
                if g >= 2:
                    pool.wait_ge(corr_mm, g - 1)
                for b in range(B):
                    pool.wait_ge(s_ready[b], CG * (g + 1) - 1)
                    c0 = b * NC + g * CG
                    pool.tensor_tensor(BDS[:, g % 2, b, :, :].rearrange("p c (j h) -> p (c j) h", h=H),
                                       Sall[:, c0:c0 + CG, :].rearrange("p c j -> p (c j)").unsqueeze(2).to_broadcast([P, CG * HD, H]),
                                       headof[:, :].unsqueeze(1).to_broadcast([P, CG * HD, H]),
                                       ALU.mult).then_inc(bds_ready, 1)

        @block.vector
        def _(dve):
            seq = [0]

            def step(ins_):
                seq[0] += 1
                ins_.then_inc(dve_seq, 1)
                dve.wait_ge(dve_seq, seq[0])

            def layernorm_stats():
                step(dve.tensor_reduce(stat[:, 0, :], xres[:, :, :], AX_X, ALU.add))
                step(dve.tensor_scalar(stat[:, 0, :], stat[:, 0, :], 1.0 / D, None, ALU.mult))
                step(dve.tensor_tensor(xcur[:, :, :], xres[:, :, :],
                                       stat[:, 0, :].unsqueeze(2).to_broadcast([P, NT, D]), ALU.subtract))
                sq = xT[:, :].rearrange("p (t d) -> p t d", t=NT)
                step(dve.tensor_tensor(sq, xcur[:, :, :], xcur[:, :, :], ALU.mult))
                step(dve.tensor_reduce(stat[:, 1, :], sq, AX_X, ALU.add))

            dve.wait_ge(ld_x, 16 * NG)
            layernorm_stats()
            dve.tensor_scalar(stat[:, 2, :], stat[:, 1, :], 1.0 / D, 1e-5, ALU.mult, ALU.add).then_inc(ln_var, 1)
            dve.wait_ge(ln_std, 1)
            step(dve.reciprocal(stat[:, 1, :], stat[:, 3, :]))
            for g in range(NG):
                tt = slice(g * G, (g + 1) * G)
                dve.tensor_tensor(xcur[:, tt, :], xcur[:, tt, :],
                                  stat[:, 1, tt].unsqueeze(2).to_broadcast([P, G, D]), ALU.mult).then_inc(layer_x, 1)
            dve.wait_ge(layer_x, NG)

            dve.wait_ge(w_tr, 1)
            dve.tensor_copy(wT[:, :, :].rearrange("p n d -> p (n d)"), PS[:, 5, :]).then_inc(w_ready, 1)

            def route(l):
                ne = E + 1 if l == 0 else E
                dve.wait_ge(logits_mm, l + 1)
                step(dve.tensor_copy(lg[:, :, 0:ne], PS[:, 2, 0:NT * ne].rearrange("p (t e) -> p t e", t=NT)))
                if l == 0:
                    dve.tensor_scalar(ldec[:, 0, :], lg[:, :, E], bd[:, 0:1], None, ALU.add).then_inc(dec_eps, 1)
                step(dve.tensor_reduce(mx[:, :], lg[:, :, 0:E], AX_X, ALU.max))
                dve.tensor_tensor(sh[:, :, :], lg[:, :, 0:E], mx[:, :].unsqueeze(2).to_broadcast([P, NT, E]),
                                  ALU.subtract).then_inc(shifted, 1)
                dve.wait_ge(shifted, l + 1)
                step(dve.scalar_tensor_tensor(out=rt[:, :, :], in0=sh[:, :, :], scalar=0.0,
                                              in1=rev[:, :].unsqueeze(1).to_broadcast([P, NT, E]),
                                              op0=ALU.is_ge, op1=ALU.mult))
                step(dve.tensor_reduce(first[:, :], rt[:, :, :], AX_X, ALU.max))
                first_b = first[:, :].unsqueeze(2).to_broadcast([P, NT, E])
                dve.tensor_tensor(hot[:, :, :], rt[:, :, :], first_b, ALU.is_equal).then_inc(hot_ready, 1)
                step(dve.tensor_tensor(hotf[:, :, :], rt[:, :, :], first_b, ALU.is_equal))
                dve.wait_ge(exp_done, l + 1)
                step(dve.tensor_reduce(esum[:, :], ex[:, :, :], AX_X, ALU.add))
                step(dve.reciprocal(xrow[:, :, D + 1], esum[:, :]))
                dve.wait_ge(rank_mm, l + 1)
                step(dve.tensor_scalar(cnt_i[:, 0, :], PS[:, 4, 0:E], float(P - 1), None, ALU.add))
                step(dve.tensor_scalar(cnt_i[:, 1, :], cnt_i[:, 0, :], P.bit_length() - 1, None, ALU.arith_shift_right))
                step(dve.tensor_copy(ecnt[:, 0, :], cnt_i[:, 1, :]))
                step(dve.tensor_tensor_scan(ecnt[:, 1, :], one_e[:, :], ecnt[:, 0, :], 0.0, ALU.mult, ALU.add))
                step(dve.tensor_tensor(ecnt[:, 2, :], ecnt[:, 1, :], ecnt[:, 0, :], ALU.subtract))
                step(dve.scalar_tensor_tensor(out=rt[:, :, :],
                                              in0=ecnt[:, 2, :].unsqueeze(1).to_broadcast([P, NT, E]), scalar=float(P),
                                              in1=PS[:, 3, 0:NT * E].rearrange("p (t e) -> p t e", t=NT),
                                              op0=ALU.mult, op1=ALU.add))
                step(dve.tensor_tensor(rt[:, :, :], rt[:, :, :], hotf[:, :, :], ALU.mult))
                step(dve.tensor_reduce(posf[:, :], rt[:, :, :], AX_X, ALU.add))
                dve.tensor_copy(pos[:, :], posf[:, :]).then_inc(pos_ready, 1)
                step(dve.tensor_tensor(tcmp[:, :, :], ecnt[:, 1, :].unsqueeze(1).to_broadcast([P, NS, E]),
                                       tix[:, :].unsqueeze(2).to_broadcast([P, NS, E]), ALU.is_le))
                step(dve.tensor_reduce(texp[:, 0, :], tcmp[:, :, :], AX_X, ALU.add))
                dve.tensor_scalar(tile_w[:, :], texp[:, 0, :], float(E - 1), float(FF), ALU.min, ALU.mult).then_inc(te_ready, 1)
                dve.wait_ge(te_ready, l + 1)

            def attention(b):
                for j in reversed(range(TB)):
                    n = b * TB + TB - 1 - j
                    w = (j + 1) * P
                    dve.wait_ge(decay_w, n + 1)
                    step(dve.tensor_tensor(wdec[:, n % 2, w - P:w], wdec[:, n % 2, w - P:w], after[:, :], ALU.mult))
                    dve.wait_ge(score_mm, n + 1)
                    if n >= 2:
                        dve.wait_ge(ret_mm, n - 1)
                    bank = 2 * (n % 2)
                    for h in range(0, w, 512):
                        e = min(w, h + 512)
                        o = dve.scalar_tensor_tensor(out=swt[:, n % 2, h:e], in0=PS[:, bank + h // 512, 0:e - h],
                                                     scalar=SCALE, in1=wdec[:, n % 2, h:e],
                                                     op0=ALU.mult, op1=ALU.mult)
                        if e < w:
                            step(o)
                    o.then_inc(sw_ready, 1)
                    dve.wait_ge(sw_ready, n + 1)
                for g in range(TB // G):
                    dve.wait_ge(proj_mm, b * (TB // G) + g + 1)
                    tt = slice(b * TB + g * G, b * TB + (g + 1) * G)
                    dve.scalar_tensor_tensor(out=xres[:, tt, :], in0=PS[:, 6 + g, :].rearrange("p (t d) -> p t d", t=G),
                                             scalar=oscale[:, 0:1], in1=xres[:, tt, :],
                                             op0=ALU.mult, op1=ALU.add).then_inc(attn_added, 1)

            def prepare():
                dve.wait_ge(ld_l1, LD_L1)
                dve.wait_ge(consts1, 1)
                for n in range(2):
                    dve.wait_ge(pd_mm, n + 1)
                    dve.tensor_copy(ewT[:, n * 512:(n + 1) * 512], PS[:, 6 + n, :]).then_inc(pd_ev, 1)
                dve.tensor_copy(wmrow16[:, :, :], wmrow[:, :].unsqueeze(2).to_broadcast([1, HD, H])).then_inc(diag_ready, 1)
                for n in range(3):
                    for j in range(K):
                        step(dve.tensor_scalar(tapdiag[:, n * K + j, :], ident[:, :], taps[:, n, j:j + 1], None, ALU.mult))
                step(dve.tensor_scalar(nwblk[:, :], wblk[:, :], -1.0, None, ALU.mult))
                step(dve.tensor_scalar(wo_v[:, 0, :], wo_v[:, 0, :], wvcol[:, 0:1], None, ALU.mult))
                dve.tensor_scalar(wo_v[:, 1, :], wo_v[:, 1, :], wvcol[:, 1:2], None, ALU.mult).then_inc(diag_ready, 1)
                dve.wait_ge(pd_mm, 3)
                dve.tensor_copy(wmcol[:, :], PS[:, 6, 0:1]).then_inc(pd_ev, 1)
                dve.wait_ge(pd_ev, 3)
                dve.wait_ge(diag_ready, 2)

            def tile_dve(l, i, c):
                k = i * R + c
                at = l * NS
                if c < NS:
                    if c >= 2:
                        dve.wait_ge(h_mm, k + (at - 1))
                    w = dve.value_load(tile_w[0:1, bass.ds(k, 1)], min_val=0, max_val=(E - 1) * FF)
                    dve.tensor_copy(w1st[:, c % 2, :], W1s[:, bass.ds(w, FF)]).then_inc(w1_staged, 1)
                    dve.wait_ge(x_tr, k + (at + 1))
                    dve.tensor_copy(xTs[:, c % 2, :], PS[:, c % 2, 0:P]).then_inc(x_ev, 1)
                if c >= 1:
                    r = (c - 1) % R
                    if c > R:
                        dve.wait_ge(y_put[r], passed(l, i, c - 1 - R) * 16)
                    dve.tensor_copy(slot_id[:, r:r + 1], xring[:, r, D:D + 1]).then_inc(id_ready, 1)
                    dve.tensor_copy(slot_w[:, r:r + 1], xring[:, r, D + 1:D + 2]).then_inc(id_ready, 1)
                if c < NS:
                    if c >= 2:
                        dve.wait_ge(y_mm, k + (at - 1))
                    dve.tensor_copy(w2st[:, c % 2, :], W2s[:, bass.ds(w, FC * D)]).then_inc(w2_staged, 1)

            for l in range(L):
                if l == 0:
                    dve.wait_ge(ld_small, 16 * 9)
                    dve.wait_ge(consts, 1)
                route(l)
                if l == 0:
                    dve.wait_ge(dec_sig, 1)
                    dve.tensor_scalar(ldec[:, 1, :], ldec[:, 1, :], 1e-8, None, ALU.add).then_inc(dec_eps, 1)
                if l < B:
                    attention(l)
                elif l == B:
                    prepare()
                if l == 0:
                    dve.wait_ge(ld_w1, 16)
                    dve.wait_ge(ld_w2, 16)
                for k in range(PRE):
                    tile_dve(l, 0, k)
                with dve.Fori(0, (NS - PRE) // R) as i:
                    for n in range(R):
                        tile_dve(l, i, PRE + n)
                tile_dve(l, 0, NS)
            for g in range(NG):
                dve.wait_ge(ld_tok[g], 16 * L)
                tt = slice(g * G, (g + 1) * G)
                dve.wait_ge(attn_added, B * (TB // G))
                dve.tensor_tensor(xres[:, tt, :], xres[:, tt, :], xcur[:, tt, :], ALU.add).then_inc(x2_ready, 1)
            dve.wait_ge(x2_ready, NG)

            layernorm_stats()
            dve.tensor_scalar(stat[:, 2, :], stat[:, 1, :], 1.0 / D, 1e-5, ALU.mult, ALU.add).then_inc(ln_var, 1)
            dve.wait_ge(ln_std, 2)
            step(dve.reciprocal(stat[:, 1, :], stat[:, 3, :]))
            for g in range(NG):
                tt = slice(g * G, (g + 1) * G)
                dve.tensor_tensor(xcur[:, tt, :], xcur[:, tt, :],
                                  stat[:, 1, tt].unsqueeze(2).to_broadcast([P, G, D]), ALU.mult).then_inc(layer_x, 1)
            dve.wait_ge(layer_x, 2 * NG)

            job = [3]

            def bank():
                dve.wait_ge(pd_mm, job[0] + 1)
                job[0] += 1
                return PS[:, 6 + (job[0] - 1) % 2, :]

            dve.tensor_tensor(abraw[:, :, :], bank().rearrange("p (t h) -> p t h", t=C),
                              abbias[:, :].unsqueeze(1).to_broadcast([P, C, 2 * H]), ALU.add).then_inc(pd_ev, 1)
            dve.wait_ge(pd_ev, job[0])
            dve.wait_ge(pa_ev, 8)
            for r, up in enumerate((u0p, u1p)):
                step(dve.scalar_tensor_tensor(out=zneg[:, r, :], in0=up, scalar=1.0, in1=zneg[:, r, :],
                                              op0=ALU.subtract, op1=ALU.mult))
            dve.wait_ge(pa_ev, 10)
            step(dve.tensor_scalar(kp, angp, 1.0 / TWO_PI, ROUND, ALU.mult, ALU.add))
            step(dve.tensor_scalar(kp, kp, ROUND, None, ALU.subtract))
            step(dve.scalar_tensor_tensor(out=angp, in0=kp, scalar=-TWO_PI_HI, in1=angp, op0=ALU.mult, op1=ALU.add))
            step(dve.scalar_tensor_tensor(out=angp, in0=kp, scalar=-TWO_PI_LO, in1=angp, op0=ALU.mult, op1=ALU.add))
            dve.tensor_scalar(angp, angp, PI_DOWN, -PI_DOWN, ALU.min, ALU.max).then_inc(ang_red, 1)
            dve.wait_ge(ang_red, 1)

            def sumsq(n):
                dve.tensor_scalar(nvar[:, n, :], bank()[:, 0:C * H], 1e-12, None, ALU.add).then_inc(pd_ev, 1)
                dve.wait_ge(pd_ev, job[0])

            sumsq(0)
            dve.wait_ge(sincos, 2)
            step(dve.tensor_tensor(cosp, cosp, cosp, ALU.mult))
            step(dve.tensor_scalar(cosp, cosp, -2.0, 1.0, ALU.mult, ALU.add))
            for i in range(2):
                a, w = 2 * i, 2 * i + 1
                step(dve.tensor_scalar(mpl[:, 0, i, :], sinp, nwblk[:, w:w + 1], None, ALU.mult))
                step(dve.scalar_tensor_tensor(out=mpl[:, 0, i, :], in0=cosp, scalar=wblk[:, a:a + 1],
                                              in1=mpl[:, 0, i, :], op0=ALU.mult, op1=ALU.add))
                step(dve.tensor_tensor(mpl[:, 0, i, :], mpl[:, 0, i, :], u0p, ALU.mult))
                step(dve.tensor_scalar(mpl[:, 1, i, :], sinp, wblk[:, a:a + 1], None, ALU.mult))
                step(dve.scalar_tensor_tensor(out=mpl[:, 1, i, :], in0=cosp, scalar=wblk[:, w:w + 1],
                                              in1=mpl[:, 1, i, :], op0=ALU.mult, op1=ALU.add))
                step(dve.tensor_tensor(mpl[:, 1, i, :], mpl[:, 1, i, :], u1p, ALU.mult))
            sumsq(1)
            dve.wait_ge(nrm_std, 1)
            dve.reciprocal(nvar, nstd).then_inc(nrm_rec, 1)
            dve.wait_ge(nrm_rec, 1)
            for n, dst in enumerate((Kc, Qc)):
                inv = nvar[:, n, :].rearrange("p (t h) -> p t h", t=C)
                for g in range(NG):
                    tt = slice(g * G, (g + 1) * G)
                    src = bank().rearrange("p (t h i) -> p t h i", t=G, h=H)
                    for t in range(G):
                        o = dve.tensor_tensor(dst[:, g * G + t, :, :], src[:, t, :, :],
                                              inv[:, g * G + t, :].unsqueeze(2).to_broadcast([P, H, HD]), ALU.mult)
                        if t < G - 1:
                            step(o)
                    o.then_inc(pd_ev, 1)
                    dve.wait_ge(pd_ev, job[0])

            dve.tensor_tensor(lg1[:, 0, :, :], bank()[:, 0:NT * E1].rearrange("p (t e) -> p t e", t=NT),
                              rb1[:, :].unsqueeze(1).to_broadcast([P, NT, E1]), ALU.add).then_inc(pd_ev, 1)
            dve.wait_ge(pd_ev, job[0])
            step(dve.tensor_reduce(mx[:, :], lg1[:, 0, :, :], AX_X, ALU.max))
            dve.tensor_tensor(lg1[:, 1, :, :], lg1[:, 0, :, :], mx[:, :].unsqueeze(2).to_broadcast([P, NT, E1]),
                              ALU.subtract).then_inc(sh1, 1)
            dve.wait_ge(sh1, 1)
            step(dve.scalar_tensor_tensor(out=lg1[:, 3, :, :], in0=lg1[:, 1, :, :], scalar=0.0,
                                          in1=rev1.unsqueeze(1).to_broadcast([P, NT, E1]),
                                          op0=ALU.is_ge, op1=ALU.mult))
            step(dve.tensor_reduce(first[:, :], lg1[:, 3, :, :], AX_X, ALU.max))
            step(dve.tensor_tensor(lg1[:, 0, :, :], lg1[:, 3, :, :], first[:, :].unsqueeze(2).to_broadcast([P, NT, E1]),
                                   ALU.is_equal))
            dve.wait_ge(ex1, 1)
            step(dve.tensor_reduce(esum[:, :], lg1[:, 2, :, :], AX_X, ALU.add))
            step(dve.reciprocal(wprob[:, :], esum[:, :]))
            dve.tensor_tensor(sel[:, :, 0:E1], lg1[:, 0, :, :], wprob[:, :].unsqueeze(2).to_broadcast([P, NT, E1]),
                              ALU.mult).then_inc(sel_ready, 1)
            dve.wait_ge(sel_ready, 1)

            dve.wait_ge(xstate0, 1)
            dve.wait_ge(bk_ready, 1)
            dve.wait_ge(pa_ev, PA_ALL)
            for t in range(C):
                x, xn = X[t % 2], X[(t + 1) % 2]
                step(dve.tensor_tensor(tmp, x, Kc[:, t, :, :].unsqueeze(1).to_broadcast([P, 2 * HD, H, HD]), ALU.mult))
                step(dve.tensor_reduce(pred[:, :, :], tmp, AX_X, ALU.add))
                step(dve.tensor_tensor(pred[:, HD:2 * HD, :], pred[:, HD:2 * HD, :],
                                       Vc[:, t, :, :].rearrange("p h j -> p j h"), ALU.subtract))
                step(dve.tensor_tensor(tmp, pred[:, :, :].unsqueeze(3).to_broadcast([P, 2 * HD, H, HD]),
                                       bKc[:, t, :, :].unsqueeze(1).to_broadcast([P, 2 * HD, H, HD]), ALU.mult))
                dve.wait_ge(ax_ready, t + 1)
                if t >= 2:
                    dve.wait_ge(r_ready, t - 1)
                dve.tensor_tensor(xn, aX, tmp, ALU.subtract).then_inc(x_new, 1)
                dve.wait_ge(x_new, t + 1)

            M4 = mpl.rearrange("p r i (c t) -> p r i c t", t=VL)
            Z3 = zneg.rearrange("p r (c t) -> p r c t", t=VL)

            def vec_step(t):
                if t == 0:
                    for r in range(2):
                        step(dve.tensor_copy(Y[:, 0, r, 0:2, :], M4[:, r, :, :, 0]))
                    step(dve.tensor_scalar(Y[:, 0, :, 2, :], Z3[:, :, :, 0], -1.0, None, ALU.mult))
                    return
                for r in range(2):
                    step(dve.tensor_tensor(vtmp[:, r, :, :].rearrange("p i (q c) -> p i q c", q=3),
                                           M4[:, r, :, :, t].unsqueeze(2).to_broadcast([P, 2, 3, VC]),
                                           Y[:, t - 1, :, :, :], ALU.mult))
                step(dve.tensor_tensor(Y[:, t, :, :, :].rearrange("p r q c -> p r (q c)"),
                                       vtmp[:, :, 0, :], vtmp[:, :, 1, :], ALU.add))
                step(dve.tensor_tensor(Y[:, t, :, 2, :], Y[:, t, :, 2, :], Z3[:, :, :, t], ALU.subtract))

            def expert_half(t, half):
                if half == 0:
                    dve.wait_ge(y1_mm, t + 1)
                for e in range(half * E1 // 2, (half + 1) * E1 // 2):
                    o = dve.scalar_tensor_tensor(out=xres[:, t, :], in0=PS[:, 6 + e * D // 512, e * D % 512:e * D % 512 + D],
                                                 scalar=sel[:, t, e:e + 1], in1=xres[:, t, :],
                                                 op0=ALU.mult, op1=ALU.add)
                    if e < E1 - 1:
                        step(o)
                if half == 1:
                    o.then_inc(y1_ev, 1)
                    dve.wait_ge(y1_ev, t + 1)

            dve.wait_ge(trans_ev, 6)
            dve.wait_ge(s0_ready, 1)
            for b in range(B):
                dve.tensor_copy(Sall[:, b * NC + 1, :], QT[:, :, b * NC]).then_inc(s_ready[b], 1)
            for c in range(1, NC - 1):
                for b in range(B):
                    dve.wait_ge(scan_mm[b], c)
                    dve.tensor_tensor(Sall[:, b * NC + c + 1, :], PS[:, 4 + b, 0:HD], QT[:, :, b * NC + c],
                                      ALU.add).then_inc(s_ready[b], 1)
                if c <= VL:
                    vec_step(c - 1)
                elif (c - VL - 1) // 2 < NT:
                    expert_half((c - VL - 1) // 2, (c - VL - 1) % 2)
            for n in range(NC - 2 - VL, 2 * NT):
                expert_half(n // 2, n % 2)

            step(dve.memset(y0[:, 0, :], 0.0))
            for c in range(VC):
                step(dve.scalar_tensor_tensor(out=y0[:, c + 1, :], in0=Y[:, VL - 1, :, 0, c], scalar=y0[:, c, 0:1],
                                              in1=Y[:, VL - 1, :, 2, c], op0=ALU.mult, op1=ALU.add))
                step(dve.scalar_tensor_tensor(out=y0[:, c + 1, :], in0=Y[:, VL - 1, :, 1, c], scalar=y0[:, c, 1:2],
                                              in1=y0[:, c + 1, :], op0=ALU.mult, op1=ALU.add))
            dve.wait_ge(corr_mm, NC // CG)
            for r in range(2):
                vr = vT[:, r, :].rearrange("p (c t) -> p t c", t=VL)
                t4 = vt4[:, r, :].rearrange("p (c t) -> p t c", t=VL)
                for i in range(2):
                    start = y0[:, 0:VC, i].unsqueeze(1).to_broadcast([P, VL, VC])
                    step(dve.tensor_tensor(t4, Y[:, :, r, i, :], start, ALU.mult))
                    step(dve.tensor_tensor(vr, t4, Y[:, :, r, 2, :] if i == 0 else vr, ALU.add))

            for n in range(NG):
                src = PS[:, n, :].rearrange("p (c t) -> p c t", t=C)
                cc = slice(n * (P // NG), (n + 1) * (P // NG))
                o = dve.tensor_tensor(oT[:, n * 512:(n + 1) * 512].rearrange("p (c t) -> p c t", t=C), src,
                                      olocT[:, :, cc].rearrange("p t c -> p c t"), ALU.add)
                if n < NG - 1:
                    step(o)
            o.then_inc(o_ready, 1)
            dve.wait_ge(o_ready, 1)
            for g in range(NG):
                dve.tensor_tensor(gate[:, g * G:(g + 1) * G, :], bank().rearrange("p (t d) -> p t d", t=G),
                                  ogbias[:, :].unsqueeze(1).to_broadcast([P, G, D]), ALU.add).then_inc(pd_ev, 1)
                dve.wait_ge(pd_ev, job[0])
            for g in range(NG):
                tt = slice(g * G, (g + 1) * G)
                dve.tensor_tensor(xres[:, tt, :], xres[:, tt, :], bank().rearrange("p (t d) -> p t d", t=G),
                                  ALU.add).then_inc(pd_ev, 1)
                dve.wait_ge(pd_ev, job[0])
            dve.wait_ge(vsq_ready, 1)
            dve.tensor_tensor(vsq[:, 0, :], vsq[:, 0, :], vsq[:, 1, :], ALU.add).then_inc(vsum, 1)
            for n in range(2):
                dve.wait_ge(vms_mm, n + 1)
                dve.tensor_scalar(vt4[:, 0, n * 512:(n + 1) * 512], PS[:, 4 + n, :], 1e-6, None, ALU.add).then_inc(vms_eps, 1)
            for n in range(NG):
                dve.wait_ge(oms_mm, n + 1)
                dve.tensor_scalar(orms[:, n * 512:(n + 1) * 512], PS[:, n, :], 1e-6, None, ALU.add).then_inc(oms_eps, 1)
            dve.wait_ge(vrms_std, 1)
            step(dve.reciprocal(vt4[:, 1, :], vt4[:, 1, :]))
            step(dve.tensor_tensor(vT[:, 0, :], vT[:, 0, :], vt4[:, 1, :], ALU.mult))
            dve.tensor_tensor(vT[:, 1, :], vT[:, 1, :], vt4[:, 1, :], ALU.mult).then_inc(vn_ready, 1)
            dve.wait_ge(orms_std, 1)
            step(dve.reciprocal(osq, osq))
            dve.scalar_tensor_tensor(out=mT, in0=oT, scalar=wmcol[:, 0:1], in1=osq,
                                     op0=ALU.mult, op1=ALU.mult).then_inc(m_ready, 1)
            dve.wait_ge(gate_ready, 1)
            for g in range(NG):
                tt = slice(g * G, (g + 1) * G)
                dve.wait_ge(out_mm, g + 1)
                step(dve.tensor_tensor(xcur[:, tt, :], PS[:, 2 + g, :].rearrange("p (t d) -> p t d", t=G),
                                       obias[:, :].unsqueeze(1).to_broadcast([P, G, D]), ALU.add))
                step(dve.tensor_tensor(xcur[:, tt, :], xcur[:, tt, :], gate[:, tt, :], ALU.mult))
                dve.tensor_tensor(xres[:, tt, :], xres[:, tt, :], xcur[:, tt, :], ALU.add).then_inc(x3_ready, 1)

        @block.scalar
        def _(act):
            act.wait_ge(ln_var, 1)
            act.activation(stat[:, 3, :], stat[:, 2, :], ACT.Sqrt).then_inc(ln_std, 1)

            def tokens_T(l):
                for g in range(NG):
                    act.wait_ge(xt_tr, l * NG + g + 1)
                    act.activation(xT[:, g * 512:(g + 1) * 512], PS[:, g % 2, :], ACT.Copy).then_inc(xt_ready, 1)

            def qkv():
                for n in range(3 * NG):
                    act.wait_ge(qkv_mm, n + 1)
                    bank = PS[:, 5 + n % 3, :]
                    if n < 2 * NG:
                        dst = (qT, kT)[n // NG][:, (n % NG) * 512:(n % NG + 1) * 512]
                    else:
                        g = n - 2 * NG
                        dst = vtok[:, g * G:(g + 1) * G, :].rearrange("p t d -> p (t d)")
                    act.activation(dst, bank, ACT.Copy).then_inc(qkv_ready, 1)

            def attention(b):
                for j in reversed(range(TB)):
                    n = b * TB + TB - 1 - j
                    w = (j + 1) * P
                    if n >= 2:
                        act.wait_ge(sw_ready, n - 1)
                    act.activation(wdec[:, n % 2, 0:w], dist[:, S - w:S], ACT.Exp,
                                   scale=ldec[:, 2, b * TB + j:b * TB + j + 1]).then_inc(decay_w, 1)
                act.wait_ge(ret_mm, (b + 1) * TB)
                for h in range(S // 512):
                    if b:
                        act.wait_ge(proj_mm, b * (TB // G))
                    act.activation(retT[:, h * 512:(h + 1) * 512], PS[:, 4 + h, :], ACT.Copy).then_inc(ret_ev, 1)

            def tile_act(l, i, c):
                k = i * R + c
                at = l * NS
                if 1 <= c <= NS:
                    act.wait_ge(h_mm, k + at)
                    if c >= 3:
                        act.wait_ge(y_mm, k + (at - 2))
                    act.activation(hTs[:, (c - 1) % 2, :], PS[:, 2 + (c - 1) % 2, :], ACT.Silu).then_inc(h_act, 1)
                if c >= 2:
                    r = (c - 2) % R
                    act.wait_ge(y_mm, k + (at - 1))
                    act.wait_ge(id_ready, k * 2 + 2 * (at - 1))
                    if c >= R + 2:
                        act.wait_ge(y_put[r], passed(l, i, c - 2 - R) * 16)
                    act.activation(yring[:, r, :], PS[:, 4 + c % 2, 0:D], ACT.Copy,
                                   scale=slot_w[:, r:r + 1]).then_inc(y_ev, 1)

            for l in range(L):
                tokens_T(l)
                act.wait_ge(shifted, l + 1)
                act.activation(ex[:, :, :], sh[:, :, :], ACT.Exp).then_inc(exp_done, 1)
                if l == 0:
                    act.wait_ge(dec_eps, 1)
                    act.activation(ldec[:, 1, :], ldec[:, 0, :], ACT.Sigmoid).then_inc(dec_sig, 1)
                    act.wait_ge(dec_eps, 2)
                    act.activation(ldec[:, 2, :], ldec[:, 1, :], ACT.Ln).then_inc(dec_log, 1)
                    act.wait_ge(dec_log, 1)
                    qkv()
                if l < B:
                    attention(l)
                for k in range(1, PRE):
                    tile_act(l, 0, k)
                with act.Fori(0, (NS - PRE) // R) as i:
                    for n in range(R):
                        tile_act(l, i, PRE + n)
                for k in range(NS, NS + 2):
                    tile_act(l, 0, k)

            act.wait_ge(ln_var, 2)
            act.activation(stat[:, 3, :], stat[:, 2, :], ACT.Sqrt).then_inc(ln_std, 1)
            tokens_T(L)

            job = [0]

            def evac(dst, func, **more):
                act.wait_ge(pa_mm, job[0] + 1)
                act.activation(dst, PS[:, 2 + job[0] % 4, :], func, **more).then_inc(pa_ev, 1)
                job[0] += 1

            def plane(n, dst, func):
                for h in range(S // 512):
                    evac(dst[:, h * 512:(h + 1) * 512], func, bias=pbias[:, n:n + 1])

            def ctrl(n):
                for b in range(B):
                    for h in range(S // 512):
                        a = K - 1 + h * 512
                        evac(pre[:, n, b, a:a + 512], ACT.Identity, bias=cbias[:, n:n + 1])

            def conv(n):
                for g in range(NG):
                    evac(post[n][:, g * 512:(g + 1) * 512], ACT.Silu)

            def square(n):
                act.wait_ge(pa_ev, job[0])
                if n:
                    act.wait_ge(pd_mm, 5)
                act.activation(sqb, post[n], ACT.Square).then_inc(sq_ready, 1)

            plane(0, u0p, ACT.Sigmoid)
            plane(1, u1p, ACT.Sigmoid)
            act.wait_ge(pd_ev, 4)
            act.activation(ab[:, :, :], abraw[:, :, :], ACT.Sigmoid).then_inc(ab_ready, 1)
            plane(2, zneg[:, 0, :], ACT.Silu)
            plane(3, zneg[:, 1, :], ACT.Silu)
            plane(4, angp, ACT.Identity)
            ctrl(0)
            conv(0)
            square(0)
            act.wait_ge(ang_red, 1)
            act.activation(cosp, angp, ACT.Sin, scale=0.5).then_inc(sincos, 1)
            act.activation(sinp, angp, ACT.Sin).then_inc(sincos, 1)
            ctrl(1)
            conv(1)
            square(1)
            ctrl(2)
            conv(2)
            act.wait_ge(pd_ev, 6)
            act.activation(nstd, nvar, ACT.Sqrt).then_inc(nrm_std, 1)
            for g in range(NG):
                evac(Vc[:, g * G:(g + 1) * G, :, :].rearrange("p t h i -> p (t h i)"), ACT.Copy)
            act.wait_ge(sh1, 1)
            act.activation(lg1[:, 2, :, :], lg1[:, 1, :, :], ACT.Exp).then_inc(ex1, 1)
            act.wait_ge(ab_ready, 1)
            evac(selT, ACT.Copy)

            def reads_evac(g):
                act.wait_ge(rT_mm, G * (g + 1))
                tt = slice(g * G, (g + 1) * G)
                act.activation(qeffT[:, tt, :].rearrange("p t c -> p (t c)"), PS[:, g % 2, :], ACT.Copy).then_inc(rT_ev, 1)
                act.activation(olocT[:, tt, :].rearrange("p t c -> p (t c)"), PS[:, 2 + g % 2, :], ACT.Copy).then_inc(rT_ev, 1)

            act.wait_ge(ab_ready, 1)
            act.wait_ge(xstate0, 1)
            for t in range(C):
                if t:
                    act.wait_ge(x_new, t)
                for h in range(H):
                    o = act.activation(aX[:, :, h, :], X[t % 2][:, :, h, :],
                                       ACT.Copy, scale=ab[:, t, h:h + 1])
                o.then_inc(ax_ready, 1)
                if t % G == 1 and t > G:
                    reads_evac(t // G - 1)
            def trans_evac(n, dst):
                act.wait_ge(trans_mm, n + 1)
                act.activation(dst, PS[:, (4, 5, 6, 7, 6, 7)[n], :], ACT.Copy).then_inc(trans_ev, 1)

            for n in range(2):
                trans_evac(n, PT[:, 4 * n:4 * n + 4, :].rearrange("p i c -> p (i c)"))
            for n in range(2):
                trans_evac(2 + n, QT0[:, n * 512:(n + 1) * 512])
            for n in range(2):
                trans_evac(4 + n, QT[:, 4 * n:4 * n + 4, :].rearrange("p i c -> p (i c)"))
            reads_evac(NG - 1)
            act.wait_ge(trans_ev, 6)
            PTb = PT.rearrange("p i (b c) -> p b c i", b=B)
            for g in range(NC // CG):
                if g >= 2:
                    for b in range(B):
                        act.wait_ge(scan_mm[b], CG * (g - 1) - 1)
                for h in range(H):
                    o = act.activation(BD[:, g % 2, :, :, h::H], PTb[:, :, g * CG:(g + 1) * CG, :],
                                       ACT.Copy, scale=headof[:, h:h + 1])
                o.then_inc(bd_ready, 1)

            act.wait_ge(o_ready, 1)
            act.activation(osq, oT, ACT.Square).then_inc(osq_ready, 1)
            act.activation(vsq[:, :, :], vT[:, :, :], ACT.Square).then_inc(vsq_ready, 1)
            act.wait_ge(pd_ev, 15 + NG)
            act.activation(gate[:, :, :], gate[:, :, :], ACT.Sigmoid).then_inc(gate_ready, 1)
            act.wait_ge(vms_eps, 2)
            act.activation(vt4[:, 1, :], vt4[:, 0, :], ACT.Sqrt).then_inc(vrms_std, 1)
            act.wait_ge(oms_eps, NG)
            act.activation(osq, orms, ACT.Sqrt).then_inc(orms_std, 1)

        @block.tensor
        def _(pe):
            def tokens_T(l):
                for g in range(NG):
                    if l % L == 0:
                        pe.wait_ge(layer_x, l // L * NG + g + 1)
                    else:
                        pe.wait_ge(ld_tok[g], 16 * l)
                    if g >= 2:
                        pe.wait_ge(xt_ready, l * NG + g - 1)
                    for t in range(G):
                        m = pe.transpose(PS[:, g % 2, t * P:(t + 1) * P], xcur[:, g * G + t, :], ident[:, :])
                    m.then_inc(xt_tr, 1)

            def logits(l):
                ne = E + 1 if l == 0 else E
                rhs = rw0[:, :] if l == 0 else rw[:, l, :]
                for t in range(NT):
                    if t % G == 0:
                        pe.wait_ge(xt_ready, l * NG + t // G + 1)
                    m = pe.matmul(PS[:, 2, t * ne:(t + 1) * ne], xT[:, t * P:(t + 1) * P], rhs, start=True, stop=True)
                m.then_inc(logits_mm, 1)

            def ranks(l):
                pe.wait_ge(hot_ready, l + 1)
                pe.matmul(PS[:, 3, 0:NT * E], ltri[:, :], hot[:, :, :].rearrange("p t e -> p (t e)"),
                          start=True, stop=False)
                for t in range(NT - 1):
                    later = PS[:, 3, (t + 1) * E:NT * E].rearrange("p (t e) -> p t e", e=E)
                    pe.matmul(later, ones_bf[:, :], hot[:, t:t + 1, :].to_broadcast([P, NT - 1 - t, E]),
                              start=False, stop=(t == NT - 2))
                for t in range(NT):
                    m = pe.matmul(PS[:, 4, 0:E], ones_bf[:, :], hot[:, t, :], start=(t == 0), stop=(t == NT - 1))
                m.then_inc(rank_mm, 1)

            def qkv():
                pe.wait_ge(w_ready, 1)
                for n in range(3 * NG):
                    if n >= 3:
                        pe.wait_ge(qkv_ready, n - 2)
                    bank = PS[:, 5 + n % 3, :]
                    g = n % NG
                    if n < 2 * NG:
                        m = pe.matmul(bank, wT[:, n // NG, :], xT[:, g * 512:(g + 1) * 512], start=True, stop=True)
                    else:
                        for t in range(G):
                            m = pe.matmul(bank[:, t * P:(t + 1) * P], xT[:, (g * G + t) * P:(g * G + t + 1) * P],
                                          wT[:, 2, :], start=True, stop=True)
                    m.then_inc(qkv_mm, 1)

            def attention(b):
                pe.wait_ge(qkv_ready, 3 * NG)
                pe.wait_ge(pos_ready, b + 1)

                def scores(j):
                    n = b * TB + TB - 1 - j
                    if n >= 2:
                        pe.wait_ge(sw_ready, n - 1)
                    w = (j + 1) * P
                    s0 = (b * TB + j) * P
                    for h in range(0, w, 512):
                        e = min(w, h + 512)
                        m = pe.matmul(PS[:, 2 * (n % 2) + h // 512, 0:e - h], kT[:, s0:s0 + P],
                                      qT[:, b * S + h:b * S + e], start=True, stop=True)
                    m.then_inc(score_mm, 1)

                def retrieve(j):
                    n = b * TB + TB - 1 - j
                    pe.wait_ge(sw_ready, n + 1)
                    w = (j + 1) * P
                    for h in range(0, w, 512):
                        e = min(w, h + 512)
                        m = pe.matmul(PS[:, 4 + h // 512, 0:e - h], vtok[:, b * TB + j, :], swt[:, n % 2, h:e],
                                      start=(j == TB - 1), stop=(j == h // P))
                    m.then_inc(ret_mm, 1)

                scores(TB - 1)
                for j in reversed(range(TB)):
                    if j:
                        scores(j - 1)
                    retrieve(j)
                if b:
                    pe.wait_ge(attn_added, b * (TB // G))
                for g in range(TB // G):
                    pe.wait_ge(ret_ev, b * (S // 512) + g + 1)
                    for t in range(G):
                        m = pe.matmul(PS[:, 6 + g, t * P:(t + 1) * P], retT[:, (g * G + t) * P:(g * G + t + 1) * P],
                                      wT[:, 3, :], start=True, stop=True)
                    m.then_inc(proj_mm, 1)

            def prepare():
                pe.wait_ge(ld_l1, LD_L1)
                pe.wait_ge(pos_ready, B + 1)
                for n in range(2):
                    for e in range(4):
                        m = pe.transpose(PS[:, 6 + n, e * D:(e + 1) * D], ew_raw[:, n * 4 + e, :], ident[:, :])
                    m.then_inc(pd_mm, 1)
                pe.wait_ge(diag_ready, 1)
                pe.wait_ge(pd_ev, 1)
                pe.matmul(PS[:, 6, 0:1], wmrow16[0:1, :, :].rearrange("p i h -> p (i h)"), ident[0:1, 0:1],
                          start=True, stop=True).then_inc(pd_mm, 1)
                pe.wait_ge(pd_ev, 3)

            def tile_mm(l, i, c):
                k = i * R + c
                at = l * NS
                if c < NS:
                    pe.wait_ge(ld_tile[c % R], passed(l, i, c) * 16)
                    pe.transpose(PS[:, c % 2, 0:P], xring[:, c % R, 0:D], ident[:, :]).then_inc(x_tr, 1)
                if 1 <= c <= NS:
                    n = (c - 1) % 2
                    pe.wait_ge(w1_staged, k + at)
                    pe.wait_ge(x_ev, k + at)
                    for f in range(FC):
                        m = pe.matmul(PS[:, 2 + n, f * P:(f + 1) * P], w1st[:, n, f * P:(f + 1) * P], xTs[:, n, :],
                                      start=True, stop=True)
                    m.then_inc(h_mm, 1)
                if c >= 2:
                    n = c % 2
                    pe.wait_ge(w2_staged, k + (at - 1))
                    pe.wait_ge(h_act, k + (at - 1))
                    if c >= 4:
                        pe.wait_ge(y_ev, k + (at - 3))
                    for f in range(FC):
                        m = pe.matmul(PS[:, 4 + n, 0:D], hTs[:, n, f * P:(f + 1) * P], w2st[:, n, f * D:(f + 1) * D],
                                      start=(f == 0), stop=(f == FC - 1))
                    m.then_inc(y_mm, 1)

            pe.wait_ge(consts, 1)
            for l in range(L):
                tokens_T(l)
                if l == 0:
                    pe.wait_ge(ld_small, 16 * 9)
                    for n in range(4):
                        m = pe.transpose(PS[:, 5, n * P:(n + 1) * P], wraw[:, n, :], ident[:, :])
                    m.then_inc(w_tr, 1)
                logits(l)
                ranks(l)
                if l == 0:
                    qkv()
                if l < B:
                    attention(l)
                    pe.wait_ge(attn_added, (l + 1) * (TB // G))
                elif l == B:
                    prepare()
                for k in range(PRE):
                    tile_mm(l, 0, k)
                with pe.Fori(0, (NS - PRE) // R) as i:
                    for n in range(R):
                        tile_mm(l, i, PRE + n)
                for k in range(NS, NS + 2):
                    tile_mm(l, 0, k)

            tokens_T(L)
            pe.wait_ge(xt_ready, NG * (L + 1))
            pe.wait_ge(diag_ready, 2)
            pe.wait_ge(pads, 1)

            aj, dj = [0], [3]

            def abank():
                n = aj[0]
                aj[0] += 1
                if n >= 4:
                    pe.wait_ge(pa_ev, n - 3)
                return PS[:, 2 + n % 4, :]

            def dbank():
                n = dj[0]
                dj[0] += 1
                pe.wait_ge(pd_ev, n - 1)
                return PS[:, 6 + n % 2, :]

            def plane(first_col, stride):
                for h in range(S // 512):
                    o = abank()
                    for b in range(B):
                        m = pe.matmul(o[b * 64:(b + 1) * 64, :], wc[:, first_col:first_col + 63 * stride + 1:stride],
                                      xT[:, b * S + h * 512:b * S + (h + 1) * 512], start=True, stop=True)
                    m.then_inc(pa_mm, 1)

            def ctrl(part):
                for g in range(NG):
                    pe.matmul(abank(), wc[:, OFF[part]:OFF[part + 1]], xT[:, g * 512:(g + 1) * 512],
                              start=True, stop=True).then_inc(pa_mm, 1)

            def conv(n):
                before = aj[0] - NG
                for b in range(B):
                    for h in range(S // 512):
                        o = abank()
                        pe.wait_ge(pa_ev, before + b * 2 + h + 1)
                        for j in range(K):
                            m = pe.matmul(o, tapdiag[:, n * K + j, :], pre[:, n, b, h * 512 + j:h * 512 + j + 512],
                                          start=(j == 0), stop=(j == K - 1))
                        m.then_inc(pa_mm, 1)

            def by_step(v, t):
                return v.rearrange("p (c t) -> p t c", t=C)[:, t, :]

            def sumsq(n):
                o = dbank()
                pe.wait_ge(sq_ready, n + 1)
                for t in range(C):
                    m = pe.matmul(o[:, t * H:(t + 1) * H], by_step(sqb, t), headsel[:, :], start=True, stop=True)
                m.then_inc(pd_mm, 1)

            def chunks(v, bank, done):
                for g in range(NG):
                    o = bank()
                    for t in range(G):
                        m = pe.transpose(o[:, t * P:(t + 1) * P], by_step(v, g * G + t), ident[:, :])
                    m.then_inc(done, 1)

            plane(OFF[0], 2)
            plane(OFF[0] + 1, 2)
            o = dbank()
            for t in range(C):
                m = pe.matmul(o[:, t * 2 * H:(t + 1) * 2 * H], by_step(xT[:, :], t), wc[:, OFF[6]:OFF[8]], start=True, stop=True)
            m.then_inc(pd_mm, 1)
            plane(OFF[2], 2)
            plane(OFF[2] + 1, 2)
            plane(OFF[1], 1)
            ctrl(4)
            conv(0)
            ctrl(3)
            sumsq(0)
            conv(1)
            ctrl(5)
            sumsq(1)
            conv(2)
            chunks(post[0], dbank, pd_mm)
            chunks(post[1], dbank, pd_mm)
            pe.wait_ge(pa_ev, aj[0])
            chunks(post[2], abank, pa_mm)
            o = dbank()
            for t in range(NT):
                m = pe.matmul(o[:, t * E1:(t + 1) * E1], xT[:, t * P:(t + 1) * P], rw1[:, :], start=True, stop=True)
            m.then_inc(pd_mm, 1)
            o = abank()
            pe.wait_ge(sel_ready, 1)
            for g in range(NG):
                m = pe.transpose(o[:, g * P:(g + 1) * P], sel[:, g * G:(g + 1) * G, :].rearrange("p t e -> p (t e)"),
                                 ident[:, :])
            m.then_inc(pa_mm, 1)

            pe.wait_ge(pa_ev, PA_ALL)
            for t in range(C):
                g = t // G
                if t % G == 0 and g >= 2:
                    pe.wait_ge(rT_ev, 2 * (g - 1))
                pe.wait_ge(r_ready, t + 1)
                for n in range(2):
                    for i in range(HD):
                        m = pe.matmul(PS[:, 2 * n + g % 2, (t % G) * P:(t % G + 1) * P],
                                      qX[t % 2].rearrange("p c h i -> p (c h) i")[:, n * P:(n + 1) * P, i], ident[:, :],
                                      start=(i == 0), stop=(i == HD - 1))
                m.then_inc(rT_mm, 1)
            pe.wait_ge(x_new, C)
            pe.wait_ge(pd_ev, dj[0])
            for n in range(4):
                for i in range(4):
                    x = X[C % 2]
                    if n < 2:
                        src = x.rearrange("p c h i -> p (c h) i")[:, 0:P, n * 4 + i]
                    else:
                        src = x[:, HD + (n - 2) * 4 + i, :, :].rearrange("p h i -> p (h i)")
                    m = pe.transpose(PS[:, 4 + n, i * P:(i + 1) * P], src, ident[:, :])
                m.then_inc(trans_mm, 1)
            for n in range(2):
                pe.wait_ge(trans_ev, 3 + n)
                pe.matmul(PS[:, 6 + n, :], perm[:, :], QT0[:, n * 512:(n + 1) * 512],
                          start=True, stop=True).then_inc(trans_mm, 1)
            pe.wait_ge(trans_ev, 6)

            def experts(t):
                if t:
                    pe.wait_ge(y1_ev, t)
                for n in range(E1 * D // 512):
                    m = pe.matmul(PS[:, 6 + n, :], xT[:, t * P:(t + 1) * P], ewT[:, n * 512:(n + 1) * 512],
                                  start=True, stop=True)
                m.then_inc(y1_mm, 1)

            def correct(g):
                if g == 0:
                    pe.wait_ge(rT_ev, 2 * NG)
                pe.wait_ge(bds_ready, B * (g + 1))
                for b in range(B):
                    for c in range(CG):
                        ch = b * NC + g * CG + c
                        m = pe.matmul(PS[:, ch // 32, (ch % 32) * C:(ch % 32 + 1) * C], BDS[:, g % 2, b, c, :],
                                      qeffT[:, :, ch], start=True, stop=True)
                m.then_inc(corr_mm, 1)

            for c in range(1, NC - 1):
                if c % CG == 0 or c == 1:
                    pe.wait_ge(bd_ready, c // CG + 1)
                for b in range(B):
                    pe.wait_ge(s_ready[b], c)
                    pe.matmul(PS[:, 4 + b, 0:HD], BD[:, (c // CG) % 2, b, c % CG, :], Sall[:, b * NC + c, :],
                              start=True, stop=True).then_inc(scan_mm[b], 1)
                if c % CG == CG - 1 and c >= 2 * CG - 1:
                    correct(c // CG - 1)
                if c >= VL and (c - VL) % 2 == 0:
                    experts((c - VL) // 2)
            for t in range((NC - 2 - VL) // 2 + 1, NT):
                experts(t)
            for b in range(B):
                pe.wait_ge(s_ready[b], NC - 1)
            for g in range((NC - 2) // CG - 0 if (NC - 2) % CG == CG - 1 else (NC - 2) // CG - 1, NC // CG):
                correct(g)
            pe.wait_ge(y1_ev, NT)
            for g in range(NG):
                o = dbank()
                for t in range(G):
                    tt = g * G + t
                    m = pe.matmul(o[:, t * P:(t + 1) * P], xT[:, tt * P:(tt + 1) * P], wc[:, OFF[8]:OFF[9]],
                                  start=True, stop=True)
                m.then_inc(pd_mm, 1)
            for g in range(NG):
                o = dbank()
                if g == 0:
                    pe.wait_ge(ld_ebias, 16 * G)
                pe.matmul(o, selT[:, g * P:(g + 1) * P], ebias.rearrange("p t o -> p (t o)"),
                          start=True, stop=True).then_inc(pd_mm, 1)
            pe.wait_ge(vsum, 1)
            for n in range(2):
                pe.matmul(PS[:, 4 + n, :], seqmean[:, :], vsq[:, 0, n * 512:(n + 1) * 512],
                          start=True, stop=True).then_inc(vms_mm, 1)
            pe.wait_ge(osq_ready, 1)
            for n in range(NG):
                pe.matmul(PS[:, n, :], headmean[:, :], osq[:, n * 512:(n + 1) * 512],
                          start=True, stop=True).then_inc(oms_mm, 1)
            pe.wait_ge(vn_ready, 1)
            pe.wait_ge(m_ready, 1)
            for g in range(NG):
                for t in range(G):
                    tt = g * G + t
                    b, tb = tt // TB, tt % TB
                    half = slice(b * 64, (b + 1) * 64)
                    o = PS[:, 2 + g, t * D:(t + 1) * D]
                    pe.matmul(o, mT[:, tt * P:(tt + 1) * P], wo_m[:, :], start=True, stop=False)
                    for r in range(2):
                        m = pe.matmul(o, vT[half, r, tb * P:(tb + 1) * P], wo_v[half, r, :], start=False, stop=(r == 1))
                m.then_inc(out_mm, 1)


_INS = ["L0_attn_x", "L0_attn_Wq", "L0_attn_Wk", "L0_attn_Wv", "L0_attn_Wo", "L0_attn_Wd", "L0_attn_bd",
        "L0_attn_out_scale", "L0_ffn_routers", "L0_ffn_W1", "L0_ffn_W2", "L1_attn_W_ctrl", "L1_attn_b_ctrl",
        "L1_attn_W_block", "L1_attn_qconv_w", "L1_attn_kconv_w", "L1_attn_vconv_w", "L1_attn_rms_m_w",
        "L1_attn_rms_v_w", "L1_attn_W_out", "L1_attn_b_out", "L1_ffn_router_w", "L1_ffn_router_b",
        "L1_ffn_expert_w", "L1_ffn_expert_b"]
_TRANSPOSED = ["L1_ffn_router_w"]
_OUTS = [((2, 1024, 128), "float32")]


def kernel(**inputs):
    import numpy as _np
    import concourse.bacc as _bacc
    from concourse import mybir as _mybir
    from concourse.bass_utils import run_bass_kernel_spmd as _run

    nc = _bacc.Bacc("TRN2", target_bir_lowering=False, num_devices=1)
    arrays, args = {}, {}
    for name in _INS:
        a = _np.ascontiguousarray(_np.asarray(inputs[name]).T if name in _TRANSPOSED else inputs[name])
        arrays[f"in_{name}_dram"] = a
        args[name] = nc.dram_tensor(f"in_{name}_dram", a.shape, _mybir.dt.from_np(a.dtype), kind="ExternalInput").ap()
    outs = []
    for i, (shape, dtype) in enumerate(_OUTS):
        dt = _mybir.dt.from_np(_np.dtype(dtype))
        outs.append(nc.dram_tensor(f"out_{i}_dram", shape, dt, kind="ExternalOutput").ap())
    build(nc, args, outs[0])
    r = _run(nc, [arrays], core_ids=[0])
    return r.results[0]["out_0_dram"]
```

```python
import math

import concourse.bass as bass
from concourse import mybir
from contextlib import ExitStack

F32 = mybir.dt.float32
BF16 = mybir.dt.bfloat16
I32 = mybir.dt.int32
ALU = mybir.AluOpType
ACT = mybir.ActivationFunctionType
AX_X = mybir.AxisListType.X


def build(nc, ins, out):
    x_in = ins["L0_attn_x"]
    B, S, D = x_in.shape
    P = 128
    N = B * S
    NT = N // P
    TB = S // P
    routers, W1, W2 = ins["L0_ffn_routers"], ins["L0_ffn_W1"], ins["L0_ffn_W2"]
    L, _, E = routers.shape
    FF = W1.shape[2]
    FC = FF // P
    NS = NT + E - 1
    SCALE = float(D) ** -0.5
    G = 4
    NG = NT // G
    R = 4
    UR = 2
    UT = UR * R
    PRE = R + (NS - R) % UT
    XW = D + 2
    E1 = ins["L1_ffn_expert_w"].shape[0]
    HD = ins["L1_attn_rms_m_w"].shape[0]
    H = D // HD
    K = ins["L1_attn_qconv_w"].shape[1]
    NCTRL = ins["L1_attn_W_ctrl"].shape[1]
    sizes = [D, D // 2, D, D, D, D, H, H, D]
    OFF = [sum(sizes[:n]) for n in range(len(sizes) + 1)]
    HS = 2
    HP = H // HS
    DP = D // HS
    CH = P // HS
    C = N // CH
    NC = S // C
    CB = 512 // C
    SB = 512 // DP
    XN = 2 * HD * HP * HD
    QR = 4
    JP = P // DP
    CG = 4
    LOGIT_BANKS = (2, 5, 6, 7)
    CS, SR = 2, 4
    NCS = NC // CS
    VL = 16
    VC = S // VL
    VP = VC // 2
    ORDER = (0, 2, 1, 3)
    LAG = 3
    VQ = VP // 2
    VFINAL = 2
    VADD = VFINAL + 2 * (3 + B) + 1
    VSUM, VINV = VADD + 1, VADD + 4
    VPROJ = VINV + 1
    READS_AT = NC // 2 + LAG + 1
    LEN_AT, TURN_AT = READS_AT + 2, READS_AT + 5
    ROUTE_AT = 1
    HALVES_AT = {4: (0, 1), 6: (2, 3), 7: (4, 5), 8: (6, 7), 15: (14, 15), 20: (20, 21),
                 **{t: (t - 1,) for t in range(9, 15)}, **{t: (t,) for t in range(16, 20)}, **{t: (t + 1,) for t in range(21, C - 1)}}
    EXPERTS_AT = {6: 1, 7: 2, 8: 3, 9: 4, 10: 5, 12: 6, 14: 7, 15: 8, 17: 9, 19: 10, **{2 * t - 2: t for t in range(11, NT)}}
    SUMS_AT = {5: 0, 7: 1, 8: 2, 9: 3, 11: 4, 13: 5, 15: 6, 16: 7, 18: 8, 20: 9, **{2 * t + 1: t for t in range(10, NT - 2)},
               2 * NT - 2: NT - 2, 2 * NT - 1: NT - 1}
    SELT_AT = 4
    BK_AT = 2
    VSTEPS = C - 12
    VPER = 3
    U_EV = 5 * NG + 3 * 2
    V_EV = U_EV + NG
    C_EV = V_EV + 2 * 2
    assert B * NC * HS == P and B * (D // 2) == P and OFF[-1] == NCTRL
    assert VPROJ + 2 * NG < NC and TURN_AT + 2 < NC
    assert D == P and (NS - PRE) % UT == 0 and PRE > R and B + 1 < L

    xs_dram = [nc.dram_tensor(f"sorted_x{l}", [NS * P, XW], F32, kind="Internal") for l in range(L)]
    y_dram = nc.dram_tensor("results", [N + NS * P, D], F32, kind="Internal")

    with ExitStack() as ctx:
        def sb(name, shape, dt=F32):
            return ctx.enter_context(nc.sbuf_tensor(name, shape, dt))

        def sem(name):
            return ctx.enter_context(nc.semaphore(name))

        PS = ctx.enter_context(nc.psum_tensor("PS", [P, 8, 512], F32))

        W1s = sb("W1s", [P, E * FF])
        W2s = sb("W2s", [P, E * FC * D])
        xres = sb("xres", [P, NT, D])
        xrow = sb("xrow", [P, NT, XW])
        xcur = xrow[:, :, 0:D]
        xT = sb("xT", [P, N])
        slotbuf = sb("slotbuf", [P, 4 * S])
        blank = slotbuf[:, 0:NS * XW].rearrange("p (t d) -> p t d", d=XW)
        qT = sb("qT", [P, N])
        kT = sb("kT", [P, N])
        vtok = sb("vtok", [P, NT, D])
        wdec = sb("wdec", [P, 2, S])
        swt = sb("swt", [P, 2, S])
        retT = sb("retT", [P, S])
        ident = sb("ident", [P, P])
        ltri = sb("ltri", [P, P], BF16)
        ones_bf = sb("ones_bf", [P, P], BF16)
        zero_bf = sb("zero_bf", [P, NT * E], BF16)
        dist_i = retT[:, :].bitcast(I32)
        dist = sb("dist", [P, S])
        after = sb("after", [P, P])
        row_i = sb("row_i", [P, NS], I32)
        rev_i = sb("rev_i", [P, E], I32)
        rev = sb("rev", [P, E])
        tix_i = sb("tix_i", [P, NS], I32)
        tix = sb("tix", [P, NS])
        one_e = sb("one_e", [P, E])
        rw = sb("rw", [P, L, E])
        rw0 = sb("rw0", [P, E + 1])
        wraw = sb("wraw", [P, 4, D])
        wT = sb("wT", [P, 4, D])
        bd = sb("bd", [P, 1])
        oscale = sb("oscale", [P, 1])
        stat = sb("stat", [P, 3, NT])
        sh = sb("sh", [P, NT, E])
        ex = sb("ex", [P, NT, E])
        rt = sb("rt", [P, NT, E])
        hot = sb("hot", [P, NT, E], BF16)
        hotf = sb("hotf", [P, NT, E])
        mx = sb("mx", [P, NT])
        esum = sb("esum", [P, NT])
        wprob = sb("wprob", [P, NT])
        first = sb("first", [P, NT])
        ldec = sb("ldec", [P, 3, NT])
        ecnt = sb("ecnt", [P, 3, E])
        pos = sb("pos", [P, NT], I32)
        tcmpbuf = sb("tcmpbuf", [P, 4 * P])
        tcmp = tcmpbuf[:, 0:NS * E].rearrange("p (s e) -> p s e", e=E)
        texp = sb("texp", [P, 2, NS])
        tile_w = sb("tile_w", [P, NS], I32)
        slot_id = sb("slot_id", [P, R], I32)
        slot_w = sb("slot_w", [P, R])
        xTs = sb("xTs", [P, 2, P])
        hbuf = sb("hbuf", [P, 2 * S])
        hTs = hbuf[:, 0:2 * FF].rearrange("p (b f) -> p b f", b=2)
        xring = hbuf[:, 2 * FF:2 * FF + R * XW].rearrange("p (r d) -> p r d", r=R)
        yring = wdec[:, 0, 0:R * D].rearrange("p (r d) -> p r d", r=R)
        w1st = swt[:, 0, 0:2 * FF].rearrange("p (b f) -> p b f", b=2)
        w2st = swt[:, 1, 0:2 * FF].rearrange("p (b f) -> p b f", b=2)

        selbuf = sb("selbuf", [P, NT * 32])

        wc = sb("wc", [P, NCTRL])
        ew_raw = sb("ew_raw", [P, E1, D])
        ewT = sb("ewT", [P, E1 * D])
        ebias = ew_raw[:, 0:G, :]
        rw1 = sb("rw1", [P, E1])
        rb1 = sb("rb1", [P, E1])
        taps = sb("taps", [P, 3, K])
        cosb = sb("cosb", [P, S])
        plane_tmp = sb("plane_tmp", [P, S])
        cbias = sb("cbias", [P, 3])
        pbias = sb("pbias", [P, 5])
        abbias = sb("abbias", [P, 2 * HP])
        ogbias = sb("ogbias", [P, D])
        obias = sb("obias", [P, D])
        wblk = sb("wblk", [P, 4])
        nwblk = sb("nwblk", [P, 4])
        wmrow = sb("wmrow", [1, HD])
        wmrow16 = sb("wmrow16", [1, HS, HD, HP])
        wmcol = sb("wmcol", [P, 1])
        wvcol = sb("wvcol", [P, 1])
        wo_m = sb("wo_m", [P, D])
        wo_v = sb("wo_v", [P, D])
        headsel = sb("headsel", [P, H])
        headmean = sb("headmean", [P, H])
        headof = sb("headof", [P, H])
        headin = sb("headin", [P, HP])
        perm = sb("perm", [P, P])
        seqmean = sb("seqmean", [P, B])
        eps_col = sb("eps_col", [P, 1])
        eps_kq = sb("eps_kq", [P, 1])
        ones_row = sb("ones_row", [1, P])
        abraw = sb("abraw", [P, C, 2 * HP])
        ab = sb("ab", [P, C, 2 * HP])
        nstd = wraw[:, :, :].rearrange("p n d -> p (n d)").rearrange("p (n m) -> p n m", n=2)
        pred = ex[:, :, :].rearrange("p t e -> p (t e)")[:, 0:2 * HD * HP].rearrange("p (c h) -> p c h", h=HP)
        scratch = plane_tmp[:, :]
        vprod = wT[:, :, :].rearrange("p n d -> p (n d)")[:, 0:8 * VC].rearrange("p (r i q c) -> p r i q c", r=2, i=2, q=2)
        yprod = scratch[:, 0:4 * VC].rearrange("p (r i c) -> p r i c", r=2, i=2)
        ysum = scratch[:, 4 * VC:6 * VC].rearrange("p (r c) -> p r c", r=2)
        mpair = scratch[:, 6 * VC:6 * VC + 4 * VP].rearrange("p (r i c) -> p r i c", r=2, i=2)
        zpair = scratch[:, 8 * VC:8 * VC + 2 * VP].rearrange("p (r c) -> p r c", r=2)
        mquad = scratch[:, 10 * VC:10 * VC + 4 * VQ].rearrange("p (r i c) -> p r i c", r=2, i=2)
        zquad = scratch[:, 11 * VC:11 * VC + 2 * VQ].rearrange("p (r c) -> p r c", r=2)
        y0 = sb("y0", [P, 2, VC])
        lg1 = tcmpbuf[:, :].rearrange("p (n t e) -> p n t e", n=4, e=E1)
        sel = selbuf[:, :].rearrange("p (t e) -> p t e", t=NT)
        rev1 = rev[:, E - E1:E]

        U = 2 * S
        u = [W1s[:, n * U:(n + 1) * U] for n in range(4)] + [W2s[:, n * U:(n + 1) * U] for n in range(4)]
        pre = W1s[:, 0:3 * B * (K - 1 + S)].rearrange("p (n b t) -> p n b t", n=3, b=B)
        post = [u[4], u[5], u[6]]
        squares_of = (u[7], vtok[:, :, :].rearrange("p t d -> p (t d)"))
        u0p, u1p = swt[:, 0, :], swt[:, 1, :]
        angp, kp, cosp = retT[:, :], dist[:, :], cosb[:, :]
        sinp = kp
        cos_part = (plane_tmp[:, :], angp, W1s[:, 7 * S:8 * S], cosp)
        mpl = slotbuf[:, :].rearrange("p (r i t) -> p r i t", r=2, i=2)
        zneg = hbuf[:, :].rearrange("p (r t) -> p r t", r=2)
        Mt = mpl.rearrange("p r i (t c) -> p r i t c", t=VL)
        Zt = zneg.rearrange("p r (t c) -> p r t c", t=VL)
        Kc = qT[:, :].rearrange("p (t h i) -> p t h i", t=C, h=HP)
        Qc = kT[:, :].rearrange("p (t h i) -> p t h i", t=C, h=HP)
        Vc = vtok[:, :, :].rearrange("p t d -> p (t d)").rearrange("p (t h i) -> p t h i", t=C, h=HP)
        bKc = wdec[:, :, :].rearrange("p b (t h i) -> p (b t) h i", h=HP, i=HD)
        xcur_f = xrow[:, :, :].rearrange("p t d -> p (t d)")[:, 0:XN]
        X = [v.rearrange("p (c h i) -> p c h i", h=HP, i=HD) for v in (xcur_f, u[0][:, 0:XN])]
        tmp = u[1][:, 0:XN].rearrange("p (c h i) -> p c h i", h=HP, i=HD)
        aX = u[2][:, 0:XN].rearrange("p (c h i) -> p c h i", h=HP, i=HD)
        qX = [v.rearrange("p (c h i) -> p c h i", h=HP, i=HD)
              for v in (u[3][:, 0:XN], u[3][:, XN:2 * XN], u[1][:, XN:2 * XN], u[2][:, XN:2 * XN])]
        qeffT = u[4].rearrange("p (t c) -> p t c", t=C)
        olocT = swt[:, :, :].rearrange("p b (t c) -> p (b t) c", c=CH)
        PT = qT[:, 0:HD * CH].rearrange("p (i c) -> p i c", i=HD)
        QT = qT[:, HD * CH:2 * HD * CH].rearrange("p (j c) -> p j c", j=HD)
        QT0 = u[2][:, 0:HD * CH].rearrange("p (q m c) -> p q m c", q=HS, c=CH)
        Sall = kT[:, 0:HD * CH].rearrange("p (c j) -> p c j", j=HD)
        BD = u[3][:, U // 2:U // 2 + 2 * B * CG * DP].rearrange("p (n b c m) -> p n b c m", n=2, b=B, c=CG)
        BDS = u[3][:, 0:SR * B * CS * DP].rearrange("p (n b c m) -> p n b c m", n=SR, b=B, c=CS)
        gate = u[5].rearrange("p (t d) -> p t d", d=D)
        vproj = u[6].rearrange("p (t d) -> p t d", d=D)
        vT = u[7].rearrange("p (b t) -> p b t", b=B)
        vsq = slotbuf[:, 0:U].rearrange("p (r t) -> p r t", r=2)
        vstd, vinv = mx[:, :].rearrange("p (b t) -> p b t", b=B), first
        scaled = u[6].rearrange("p (n e o) -> p n e o", n=2, e=E1)
        oT = u[2]
        osq = wdec[:, :, :].rearrange("p b t -> p (b t)")
        ostd = ex[:, :, :].rearrange("p t e -> p (t e)")
        oinv = rt[:, :, :].rearrange("p t e -> p (t e)")
        oinvx = u[0]
        mT = u[1]
        selT = abraw[:, :, :].rearrange("p t h -> p (t h)")

        def part_rows(q):
            return slice(q * DP, (q + 1) * DP)

        ld_x = [sem(f"ld_x{g}") for g in range(NG)]
        ld_small = sem("ld_small")
        ld_w1 = sem("ld_w1")
        ld_w2 = sem("ld_w2")
        zeroed = sem("zeroed")
        xs_cleared = [sem(f"xs_cleared{l}") for l in range(L)]
        ld_tile = [sem(f"ld_tile{r}") for r in range(R)]
        consts = sem("consts")
        pool_seq = sem("pool_seq")
        dve_seq = sem("dve_seq")
        layer_x = sem("layer_x")
        xt_tr = sem("xt_tr")
        xt_ready = sem("xt_ready")
        logits_mm = sem("logits_mm")
        shifted = sem("shifted")
        exp_done = sem("exp_done")
        hot_ready = sem("hot_ready")
        rank_mm = sem("rank_mm")
        pos_ready = sem("pos_ready")
        te_ready = sem("te_ready")
        scattered = sem("scattered")
        ld_tok = [sem(f"ld_tok{g}") for g in range(NG)]
        x_tr = sem("x_tr")
        x_ev = sem("x_ev")
        w1_staged = sem("w1_staged")
        w2_staged = sem("w2_staged")
        id_ready = sem("id_ready")
        h_mm = sem("h_mm")
        h_act = sem("h_act")
        y_mm = sem("y_mm")
        y_ev = sem("y_ev")
        y_put = [sem(f"y_put{r}") for r in range(R)]
        w_tr = sem("w_tr")
        w_ready = sem("w_ready")
        dec_sig = sem("dec_sig")
        dec_eps = sem("dec_eps")
        dec_log = sem("dec_log")
        centred = sem("centred")
        squared = sem("squared")
        ln_var = sem("ln_var")
        ln_std = sem("ln_std")
        qkv_mm = sem("qkv_mm")
        qkv_ready = sem("qkv_ready")
        score_mm = sem("score_mm")
        decay_w = sem("decay_w")
        sw_ready = sem("sw_ready")
        ret_mm = sem("ret_mm")
        ret_ev = sem("ret_ev")
        proj_mm = sem("proj_mm")
        attn_added = sem("attn_added")
        st_out = sem("st_out")
        ld_l1 = sem("ld_l1")
        ld_ebias = sem("ld_ebias")
        consts1 = sem("consts1")
        diag_ready = sem("diag_ready")
        pads = sem("pads")
        xstate0 = sem("xstate0")
        pa_mm = sem("pa_mm")
        pa_ev = sem("pa_ev")
        pd_mm = sem("pd_mm")
        pd_ev = sem("pd_ev")
        ab_ready = sem("ab_ready")
        sq_ready = sem("sq_ready")
        tap_ready = sem("tap_ready")
        len2_ready = sem("len2_ready")
        unit_ready = sem("unit_ready")
        conv_done = sem("conv_done")
        post_ready = sem("post_ready")
        ang_red = sem("ang_red")
        sincos = sem("sincos")
        cos_ready = sem("cos_ready")
        prod_ready = sem("prod_ready")
        len_ready = sem("len_ready")
        bk_ready = sem("bk_ready")
        sh1 = sem("sh1")
        ex1 = sem("ex1")
        sel_ready = sem("sel_ready")
        selT_mm = sem("selT_mm")
        selT_ev = sem("selT_ev")
        x_new = sem("x_new")
        ax_ready = sem("ax_ready")
        r_ready = sem("r_ready")
        rT_mm = sem("rT_mm")
        rT_ev = sem("rT_ev")
        trans_mm = sem("trans_mm")
        trans_ev = sem("trans_ev")
        qt0_ready = sem("qt0_ready")
        bd_ready = sem("bd_ready")
        s0_ready = sem("s0_ready")
        scan_mm = [sem(f"scan_mm{b}") for b in range(B)]
        s_ready = [sem(f"s_ready{b}") for b in range(B)]
        bds_ready = sem("bds_ready")
        corr_mm = sem("corr_mm")
        y1_mm = sem("y1_mm")
        y1_ev = sem("y1_ev")
        ysum_mm = sem("ysum_mm")
        ysum_ev = sem("ysum_ev")
        o_ready = sem("o_ready")
        planes_ready = sem("planes_ready")
        vec_done = sem("vec_done")
        v_ready = sem("v_ready")
        vsq_ready = sem("vsq_ready")
        vms_mm = sem("vms_mm")
        vstd_ready = sem("vstd_ready")
        vinv_ready = sem("vinv_ready")
        vp_mm = sem("vp_mm")
        vp_ev = sem("vp_ev")
        gate_mm = sem("gate_mm")
        gate_ev = sem("gate_ev")
        vadd_ready = sem("vadd_ready")
        xg_ready = sem("xg_ready")
        bd_first = sem("bd_first")
        bds_last = sem("bds_last")
        osq_ready = sem("osq_ready")
        oms_mm = sem("oms_mm")
        ostd_ready = sem("ostd_ready")
        oinv_ready = sem("oinv_ready")
        oinvx_ready = sem("oinvx_ready")
        oinv_tr = sem("oinv_tr")
        m_ready = sem("m_ready")
        out_mm = sem("out_mm")
        x3_ready = sem("x3_ready")

        block = ctx.enter_context(nc.Block())

        LD_L1 = 16 * (4 + 2 * 3 + 6 * B + HS * HD + 2 * HS + 3)
        TWO_PI = 2 * math.pi
        TWO_PI_HI = 6.28125
        TWO_PI_LO = TWO_PI - TWO_PI_HI
        PI_DOWN = 3.1415925
        ROUND = 1.5 * 2 ** 23

        y_tiles = y_dram[0:N, :].rearrange("(t p) d -> p t d", p=P)
        xs_tiles = [xs[:, :].rearrange("(t p) d -> p t d", p=P) for xs in xs_dram]
        USES = [(NS - r + R - 1) // R for r in range(R)]

        def passed(l, i, c):
            return i * UR + (c // R + 1 + l * USES[c % R])

        x_tiles = x_in.rearrange("b (t p) d -> p (b t) d", p=P)

        @block.sync
        def _(sp):
            for g in range(NG):
                sp.dma_start(xres[:, g * G:(g + 1) * G, :], x_tiles[:, g * G:(g + 1) * G, :]).then_inc(ld_x[g], 16)
            for n, w in enumerate(("Wq", "Wk", "Wv", "Wo")):
                sp.dma_start(wraw[:, n, :], ins[f"L0_attn_{w}"][:, :]).then_inc(ld_small, 16)
            sp.dma_start(rw[:, :, :], routers.rearrange("l d e -> d l e")).then_inc(ld_small, 16)
            sp.dma_start(rw0[:, 0:E], routers[0, :, :]).then_inc(ld_small, 16)
            sp.dma_start(rw0[:, E:E + 1], ins["L0_attn_Wd"].rearrange("o d -> d o")).then_inc(ld_small, 16)
            sp.dma_start(bd[:, :], ins["L0_attn_bd"].partition_broadcast(P)).then_inc(ld_small, 16)
            sp.dma_start(oscale[:, :], ins["L0_attn_out_scale"].partition_broadcast(P)).then_inc(ld_small, 16)
            sp.wait_ge(zeroed, 1)
            sp.dma_start(xs_tiles[0], blank).then_inc(xs_cleared[0], 16)
            sp.dma_start(W1s[:, :].rearrange("d (e f) -> d e f", e=E), W1.rearrange("e d f -> d e f")).then_inc(ld_w1, 16)
            sp.dma_start(W2s[:, :].rearrange("p (e c d) -> p e c d", e=E, c=FC),
                         W2.rearrange("e (c p) d -> p e c d", p=P)).then_inc(ld_w2, 16)
            def load(dst, src, **how):
                sp.dma_start(dst, src, **how).then_inc(ld_l1, 16)

            b_ctrl = ins["L1_attn_b_ctrl"]
            load(wc[:, :], ins["L1_attn_W_ctrl"][:, :])
            load(ew_raw[:, :, :], ins["L1_ffn_expert_w"].rearrange("e o d -> o e d"))
            load(rw1[:, :], ins["L1_ffn_router_w"][:, :])
            load(rb1[:, :], ins["L1_ffn_router_b"].partition_broadcast(P))
            for n, w in enumerate("kqv"):
                load(taps[:, n, :], ins[f"L1_attn_{w}conv_w"][:, :])
                part = OFF[{"q": 3, "k": 4, "v": 5}[w]]
                load(cbias[:, n:n + 1], b_ctrl[part:part + D].rearrange("(p o) -> p o", o=1))
            for b in range(B):
                half = slice(b * D // 2, (b + 1) * D // 2)
                for n, part in ((0, OFF[0]), (2, OFF[2])):
                    load(pbias[half, n:n + 2], b_ctrl[part:part + D].rearrange("(p r) -> p r", r=2))
                load(pbias[half, 4:5], b_ctrl[OFF[1]:OFF[2]].rearrange("(p o) -> p o", o=1))
                load(wblk[half, :], ins["L1_attn_W_block"].rearrange("p i j -> p (i j)"))
                load(wvcol[half, :], ins["L1_attn_rms_v_w"].rearrange("(p r o) -> r p o", r=2, o=1)[b], allow_slow_non_contiguous=True)
                load(wo_v[half, :], ins["L1_attn_W_out"][D:2 * D, :].rearrange("(p r) o -> r p o", r=2)[b])
            for q in range(HS):
                for j in range(HD):
                    rows = q * DP + j * HP
                    load(wo_m[rows:rows + HP, :], ins["L1_attn_W_out"][q * DP:(q + 1) * DP, :].rearrange("(h j) o -> j h o", h=HP)[j])
                for n in range(2):
                    a = OFF[6 + n] + q * HP
                    load(abbias[part_rows(q), n * HP:(n + 1) * HP], b_ctrl[a:a + HP].partition_broadcast(DP))
            load(ogbias[:, :], b_ctrl[OFF[8]:OFF[9]].partition_broadcast(P))
            load(obias[:, :], ins["L1_attn_b_out"].partition_broadcast(P))
            load(wmrow[:, :], ins["L1_attn_rms_m_w"].rearrange("(o i) -> o i", o=1))
            for l in range(L):
                def load_tile(i, c):
                    k = i * UT + c
                    r = c % R
                    if c >= R:
                        sp.wait_ge(x_tr, k + (l * NS - R + 1))
                        sp.wait_ge(id_ready, k * 2 + 2 * (l * NS - R + 1))
                    src = xs_tiles[l][:, bass.ds(k, 1), :].rearrange("p t d -> p (t d)") if not isinstance(k, int) \
                        else xs_tiles[l][:, k, :]
                    sp.dma_start(xring[:, r, :], src).then_inc(ld_tile[r], 16)
                    if l + 1 < L:
                        to, rows = (xs_tiles[l + 1][:, k, :], blank[:, k, :]) if isinstance(k, int) else \
                            (xs_tiles[l + 1][:, bass.ds(k, 1), :], blank[:, bass.ds(k, 1), :])
                        sp.dma_start(to, rows).then_inc(xs_cleared[l + 1], 16)

                sp.wait_ge(scattered, 16 * NT * (l + 1))
                for k in range(PRE):
                    load_tile(0, k)
                with sp.Fori(0, (NS - PRE) // UT) as i:
                    for n in range(UT):
                        load_tile(i, PRE + n)
                for r in range(R):
                    sp.wait_ge(y_put[r], 16 * USES[r] * (l + 1))
                for g in range(NG):
                    tt = slice(g * G, (g + 1) * G)
                    sp.dma_start(xcur[:, tt, :], y_tiles[:, tt, :]).then_inc(ld_tok[g], 16)
            sp.wait_ge(pads, 1)
            for t in range(G):
                sp.dma_start(ebias[32 * t:32 * t + E1, t, :], ins["L1_ffn_expert_b"][:, :]).then_inc(ld_ebias, 16)
            out_tiles = out.rearrange("b (t p) d -> p (b t) d", p=P)
            for n, g in enumerate(ORDER):
                sp.wait_ge(x3_ready, n + 1)
                sp.dma_start(out_tiles[:, g * G:(g + 1) * G, :], xres[:, g * G:(g + 1) * G, :]).then_inc(st_out, 16)
            sp.wait_ge(st_out, 16 * NG)

        @block.gpsimd
        def _(pool):
            seq = [0]

            def step(ins_):
                seq[0] += 1
                ins_.then_inc(pool_seq, 1)
                pool.wait_ge(pool_seq, seq[0])

            step(pool.memset(slotbuf[:, :], 0.0))
            step(pool.iota(row_i[:, 0:NS], pattern=[[P, NS]], base=N, channel_multiplier=1))
            pool.tensor_copy(blank[:, :, D], row_i[:, 0:NS]).then_inc(zeroed, 1)
            pool.wait_ge(zeroed, 1)
            step(pool.iota(row_i[:, 0:NT], pattern=[[P, NT]], base=0, channel_multiplier=1))
            step(pool.tensor_copy(xrow[:, :, D], row_i[:, 0:NT]))
            step(pool.memset(ident[:, :], 0.0))
            step(pool.affine_select(out=ident[:, :], in_=ident[:, :], compare_op=ALU.not_equal, fill=1.0,
                                    base=0, pattern=[[-1, P]], channel_multiplier=1))
            step(pool.memset(zero_bf[:, :], 0.0))
            step(pool.memset(ones_bf[:, :], 1.0))
            step(pool.affine_select(out=ltri[:, :], in_=ones_bf[:, :], compare_op=ALU.is_gt, fill=0.0,
                                    base=0, pattern=[[1, P]], channel_multiplier=-1))
            step(pool.memset(after[:, :], 1.0))
            step(pool.affine_select(out=after[:, :], in_=after[:, :], compare_op=ALU.is_gt, fill=0.0,
                                    base=0, pattern=[[-1, P]], channel_multiplier=1))
            step(pool.iota(dist_i[:, :], pattern=[[-1, S]], base=S - P - 1, channel_multiplier=1))
            step(pool.tensor_scalar(dist[:, :], dist_i[:, :], 0.0, None, ALU.max))
            step(pool.iota(rev_i[:, :], pattern=[[-1, E]], base=E, channel_multiplier=0))
            step(pool.tensor_copy(rev[:, :], rev_i[:, :]))
            step(pool.iota(tix_i[:, :], pattern=[[1, NS]], base=0, channel_multiplier=0))
            step(pool.tensor_copy(tix[:, :], tix_i[:, :]))
            pool.memset(one_e[:, :], 1.0).then_inc(consts, 1)
            pool.wait_ge(consts, 1)
            step(pool.memset(headsel[:, :], 1.0))
            step(pool.affine_select(out=headsel[:, :], in_=headsel[:, :], compare_op=ALU.is_ge, fill=0.0,
                                    base=0, pattern=[[-HD, H]], channel_multiplier=1))
            step(pool.affine_select(out=headsel[:, :], in_=headsel[:, :], compare_op=ALU.is_ge, fill=0.0,
                                    base=HD - 1, pattern=[[HD, H]], channel_multiplier=-1))
            step(pool.memset(headof[:, :], 0.0))
            head3 = headof[:, :].rearrange("p (q h) -> p q h", q=HS)
            for i in range(HD):
                step(pool.affine_select(out=head3, in_=head3, compare_op=ALU.not_equal, fill=1.0,
                                        base=-HP * i, pattern=[[-DP, HS], [-1, HP]], channel_multiplier=1))
            step(pool.tensor_scalar(headmean[:, :], headof[:, :], 1.0 / HD, None, ALU.mult))
            step(pool.memset(headin[:, :], 0.0))
            for i in range(P // HP):
                step(pool.affine_select(out=headin[:, :], in_=headin[:, :], compare_op=ALU.not_equal, fill=1.0,
                                        base=-HP * i, pattern=[[-1, HP]], channel_multiplier=1))
            step(pool.memset(perm[:, :], 0.0))
            perm4 = perm[:, :].rearrange("p (j i h) -> p j i h", j=JP, h=HP)
            step(pool.affine_select(out=perm4, in_=perm4, compare_op=ALU.not_equal, fill=1.0,
                                    base=0, pattern=[[-DP, JP], [-1, HD], [-HD, HP]], channel_multiplier=1))
            step(pool.memset(sel[:, :, :], 0.0))
            step(pool.memset(seqmean[:, :], 0.0))
            for b in range(B):
                step(pool.memset(seqmean[b * P // B:(b + 1) * P // B, b:b + 1], 1.0 / D))
            step(pool.memset(eps_col[:, :], 1e-6))
            step(pool.memset(eps_kq[:, :], 1e-12))
            pool.memset(ones_row[:, :], 1.0).then_inc(consts1, 1)
            pool.wait_ge(consts1, 1)
            for l in range(L):
                pool.wait_ge(xs_cleared[l], 16 * (NS if l else 1))
                pool.wait_ge(pos_ready, l + 1)
                for t in range(NT):
                    pool.indirect_dma_start(xs_dram[l][:, :], bass.IndirectOffsetOnAxis(ap=pos[:, t:t + 1], axis=0),
                                            xrow[:, t, :], None).then_inc(scattered, 16)

                def put(i, c):
                    k = i * UT + c
                    r = c % R
                    ids, results = (k * 2 + 2 * (l * NS + 1), k + (l * NS + 1))
                    if not isinstance(k, int):
                        ids, results = pool.to_reg(ids), pool.to_reg(results)
                    pool.wait_ge(xs_cleared[l], 16 * (NS if l else 1))
                    pool.wait_ge(id_ready, ids)
                    pool.wait_ge(y_ev, results)
                    pool.indirect_dma_start(y_dram[:, :], bass.IndirectOffsetOnAxis(ap=slot_id[:, r:r + 1], axis=0),
                                            yring[:, r, :], None).then_inc(y_put[r], 16)

                for k in range(PRE):
                    put(0, k)
                with pool.Fori(0, (NS - PRE) // UT) as i:
                    for n in range(UT):
                        put(i, PRE + n)

            step(pool.memset(ebias, 0.0))
            step(pool.memset(pre[:, 0, :, 0:K - 1], 0.0))
            step(pool.memset(pre[:, 1, :, 0:K - 1], 0.0))
            pool.memset(pre[:, 2, :, 0:K - 1], 0.0).then_inc(pads, 1)
            pool.wait_ge(xt_tr, NG * (L + 1))
            step(pool.memset(xcur_f, 0.0))
            pool.affine_select(out=X[0], in_=X[0], compare_op=ALU.not_equal, fill=1.0, base=0,
                               pattern=[[1, 2 * HD], [0, HP], [-1, HD]], channel_multiplier=0).then_inc(xstate0, 1)

            def vec_join(m, z, m0, z0, m_out, z_out, n, op):
                for r in range(2):
                    seq[0] += 1
                    pool.tensor_tensor(vprod[:, r, :, :, 0:n], m[:, r, :, :].unsqueeze(2).to_broadcast([P, 2, 2, n]),
                                       m0, ALU.mult).then_inc(pool_seq, 1)
                step(pool.tensor_tensor(yprod[:, :, :, 0:n], m, z0.unsqueeze(1).to_broadcast([P, 2, 2, n]), ALU.mult))
                seq[0] += 1
                pool.tensor_tensor(m_out, vprod[:, :, 0, :, 0:n], vprod[:, :, 1, :, 0:n], ALU.add).then_inc(pool_seq, 1)
                step(pool.tensor_tensor(ysum[:, :, 0:n], yprod[:, :, 0, 0:n], yprod[:, :, 1, 0:n], ALU.add))
                return pool.tensor_tensor(z_out, ysum[:, :, 0:n], z, op)

            def vec_step(t):
                step(vec_join(Mt[:, :, :, t, :], Zt[:, :, t, :], Mt[:, :, :, t - 1, :], Zt[:, :, t - 1, :],
                              Mt[:, :, :, t, :], Zt[:, :, t, :], VC, ALU.subtract))

            def vec_start(k):
                a, c = 4 * k, 4 * k + 4
                step(pool.tensor_tensor(yprod[:, :, :, 0], mquad[:, :, :, k], y0[:, :, a].unsqueeze(1).to_broadcast([P, 2, 2]),
                                        ALU.mult))
                step(pool.tensor_tensor(ysum[:, :, 0], yprod[:, :, 0, 0], yprod[:, :, 1, 0], ALU.add))
                step(pool.tensor_tensor(y0[:, :, c], ysum[:, :, 0], zquad[:, :, k], ALU.add))

            def vec_fill(stride):
                if stride == 4:
                    n, m, z = VQ, mpair[:, :, :, 0::2], zpair[:, :, 0::2]
                else:
                    n, m, z = VP, Mt[:, :, :, VL - 1, 0::2], Zt[:, :, VL - 1, 0::2]
                step(pool.tensor_tensor(yprod[:, :, :, 0:n], m, y0[:, :, 0::stride].unsqueeze(1).to_broadcast([P, 2, 2, n]), ALU.mult))
                step(pool.tensor_tensor(ysum[:, :, 0:n], yprod[:, :, 0, 0:n], yprod[:, :, 1, 0:n], ALU.add))
                return pool.tensor_tensor(y0[:, :, stride // 2::stride], ysum[:, :, 0:n], z, ALU.add)

            def squared_lengths(n):
                pool.wait_ge(sq_ready, NG * (n + 1))
                sq = squares_of[n].rearrange("p (m i) -> p m i", i=HD)
                step(pool.tensor_tensor(sq[:, :, 0:4], sq[:, :, 0:4], sq[:, :, 4:8], ALU.add))
                step(pool.tensor_tensor(sq[:, :, 0:2], sq[:, :, 0:2], sq[:, :, 2:4], ALU.add))
                pool.tensor_tensor(nstd[:, n, :], sq[:, :, 0], sq[:, :, 1], ALU.add).then_inc(len2_ready, 1)

            pool.wait_ge(sincos, 2)
            step(pool.tensor_tensor(cosp, cosp, cosp, ALU.mult))
            pool.tensor_scalar(cosp, cosp, -2.0, 1.0, ALU.mult, ALU.add).then_inc(cos_ready, 1)
            squared_lengths(0)
            squared_lengths(1)
            for n in range(4):
                if n == BK_AT:
                    pool.wait_ge(unit_ready, 1)
                    pool.wait_ge(ab_ready, 1)
                    pool.tensor_tensor(bKc, Kc, ab[:, :, HP:2 * HP].unsqueeze(3).to_broadcast([P, C, HP, HD]),
                                       ALU.mult).then_inc(bk_ready, 1)
                r, i = n % 2, n // 2
                pool.wait_ge(prod_ready, n + 1)
                pool.wait_ge(pa_ev, U_EV)
                step(pool.tensor_tensor(mpl[:, r, i, :], mpl[:, r, i, :], (u0p, u1p)[r], ALU.mult))
            pool.wait_ge(pa_ev, C_EV)
            pool.wait_ge(unit_ready, 2)
            for t in range(C):
                pool.wait_ge(x_new, 2 * (t + 1))
                if t >= QR:
                    pool.wait_ge(rT_mm, t - QR + 1)
                pool.tensor_tensor(qX[t % QR], X[(t + 1) % 2], Qc[:, t, :, :].unsqueeze(1).to_broadcast([P, 2 * HD, HP, HD]),
                                   ALU.mult).then_inc(r_ready, 1)
                if t < 4:
                    r = t // 2
                    if t % 2 == 0:
                        step(pool.tensor_scalar(swt[:, r, :], swt[:, r, :], 1.0, None, ALU.subtract))
                    else:
                        pool.tensor_tensor(zneg[:, r, :], zneg[:, r, :], swt[:, r, :], ALU.mult).then_inc(planes_ready, 1)
                        pool.wait_ge(planes_ready, r + 1)
                    if t == 3:
                        step(pool.tensor_scalar(Zt[:, :, 0, :], Zt[:, :, 0, :], -1.0, None, ALU.mult))
                elif t < 4 + VSTEPS:
                    for v in range(1 + (t - 4) * (VL - 1) // VSTEPS, 1 + (t - 3) * (VL - 1) // VSTEPS):
                        vec_step(v)
                elif t == 4 + VSTEPS:
                    m, z = Mt[:, :, :, VL - 1, :], Zt[:, :, VL - 1, :]
                    step(vec_join(m[:, :, :, 1::2], z[:, :, 1::2], m[:, :, :, 0::2], z[:, :, 0::2], mpair, zpair, VP, ALU.add))
                elif t == 5 + VSTEPS:
                    step(vec_join(mpair[:, :, :, 1::2], zpair[:, :, 1::2], mpair[:, :, :, 0::2], zpair[:, :, 0::2], mquad, zquad, VQ,
                                  ALU.add))
                    step(pool.memset(y0[:, :, 0], 0.0))
                elif t > 5 + VSTEPS:
                    for k in range(VPER * (t - 6 - VSTEPS), min(VPER * (t - 5 - VSTEPS), VQ - 1)):
                        vec_start(k)
            pool.wait_ge(r_ready, C)
            step(pool.memset(Sall[:, 0:1, :], 0.0))
            pool.memset(Sall[:, NC:NC + 1, :], 0.0).then_inc(s0_ready, 1)
            step(vec_fill(4))
            vec_fill(2).then_inc(vec_done, 1)

            def result_base(n):
                tt = slice(ORDER[n] * G, (ORDER[n] + 1) * G)
                pool.wait_ge(vp_ev, n + 1)
                pool.wait_ge(ysum_ev, NG)
                pool.wait_ge(gate_ev, NG)
                step(pool.tensor_tensor(vproj[:, tt, :], vproj[:, tt, :], obias[:, :].unsqueeze(1).to_broadcast([P, G, D]), ALU.add))
                step(pool.tensor_tensor(vproj[:, tt, :], vproj[:, tt, :], gate[:, tt, :], ALU.mult))
                pool.tensor_tensor(xres[:, tt, :], xres[:, tt, :], vproj[:, tt, :], ALU.add).then_inc(xg_ready, 1)

            for g in range(NCS - 1):
                if g >= SR:
                    pool.wait_ge(corr_mm, B * CS * (g - SR + 1))
                for b in range(B):
                    pool.wait_ge(s_ready[b], CS * (g + 1) - 1)
                    c0 = b * NC + g * CS
                    pool.tensor_tensor(BDS[:, g % SR, b, :, :].rearrange("p c (j h) -> p (c j) h", h=HP),
                                       Sall[:, c0:c0 + CS, :].rearrange("p c j -> p (c j)").unsqueeze(2).to_broadcast([P, CS * HD, HP]),
                                       headin[:, :].unsqueeze(1).to_broadcast([P, CS * HD, HP]),
                                       ALU.mult).then_inc(bds_ready, 1)
            for n in range(NG):
                result_base(n)

        @block.vector
        def _(dve):
            seq = [0]

            def step(ins_):
                seq[0] += 1
                ins_.then_inc(dve_seq, 1)
                dve.wait_ge(dve_seq, seq[0])

            def mark(ins_):
                seq[0] += 1
                ins_.then_inc(dve_seq, 1)
                return seq[0]

            def norm_mean(n, g):
                tt = slice(g * G, (g + 1) * G)
                if n == 0:
                    dve.wait_ge(ld_x[g], 16)
                else:
                    dve.wait_ge(ld_tok[g], 16 * L)
                    dve.wait_ge(attn_added, B * (TB // G))
                    step(dve.tensor_tensor(xres[:, tt, :], xres[:, tt, :], xcur[:, tt, :], ALU.add))
                step(dve.tensor_reduce(stat[:, 0, tt], xres[:, tt, :], AX_X, ALU.add))
                step(dve.tensor_scalar(stat[:, 0, tt], stat[:, 0, tt], 1.0 / D, None, ALU.mult))
                dve.tensor_tensor(xcur[:, tt, :], xres[:, tt, :], stat[:, 0, tt].unsqueeze(2).to_broadcast([P, G, D]),
                                  ALU.subtract).then_inc(centred, 1)

            def norm_var(n, g):
                tt = slice(g * G, (g + 1) * G)
                dve.wait_ge(squared, n * NG + g + 1)
                step(dve.tensor_reduce(stat[:, 1, tt], xT[:, g * 512:(g + 1) * 512].rearrange("p (t d) -> p t d", t=G),
                                       AX_X, ALU.add))
                dve.tensor_scalar(stat[:, 1, tt], stat[:, 1, tt], 1.0 / D, 1e-5, ALU.mult, ALU.add).then_inc(ln_var, 1)

            def norm_scale(n, g):
                tt = slice(g * G, (g + 1) * G)
                dve.wait_ge(ln_std, n * NG + g + 1)
                step(dve.reciprocal(stat[:, 1, tt], stat[:, 2, tt]))
                dve.tensor_tensor(xcur[:, tt, :], xcur[:, tt, :], stat[:, 1, tt].unsqueeze(2).to_broadcast([P, G, D]),
                                  ALU.mult).then_inc(layer_x, 1)

            def layernorm(n):
                for g in range(NG + 2):
                    if g < NG:
                        norm_mean(n, g)
                    if 1 <= g <= NG:
                        norm_var(n, g - 1)
                    if g >= 2:
                        norm_scale(n, g - 2)
                dve.wait_ge(layer_x, (n + 1) * NG)

            layernorm(0)

            dve.wait_ge(w_tr, 1)
            dve.tensor_copy(wT[:, :, :].rearrange("p n d -> p (n d)"), PS[:, 5, :]).then_inc(w_ready, 1)

            def route(l):
                ne = E + 1 if l == 0 else E
                for g in range(NG):
                    tt = slice(g * G, (g + 1) * G)
                    dve.wait_ge(logits_mm, l * NG + g + 1)
                    lg = PS[:, LOGIT_BANKS[g], 0:G * ne].rearrange("p (t e) -> p t e", t=G)
                    if l == 0:
                        dve.tensor_scalar(ldec[:, 0, tt], lg[:, :, E], bd[:, 0:1], None, ALU.add).then_inc(dec_eps, 1)
                    step(dve.tensor_reduce(mx[:, tt], lg[:, :, 0:E], AX_X, ALU.max))
                    dve.tensor_tensor(sh[:, tt, :], lg[:, :, 0:E], mx[:, tt].unsqueeze(2).to_broadcast([P, G, E]),
                                      ALU.subtract).then_inc(shifted, 1)
                    dve.wait_ge(shifted, l * NG + g + 1)
                    step(dve.scalar_tensor_tensor(out=rt[:, tt, :], in0=sh[:, tt, :], scalar=0.0,
                                                  in1=rev[:, :].unsqueeze(1).to_broadcast([P, G, E]),
                                                  op0=ALU.is_ge, op1=ALU.mult))
                    step(dve.tensor_reduce(first[:, tt], rt[:, tt, :], AX_X, ALU.max))
                    dve.tensor_tensor(hot[:, tt, :], rt[:, tt, :], first[:, tt].unsqueeze(2).to_broadcast([P, G, E]),
                                      ALU.is_equal).then_inc(hot_ready, 1)
                step(dve.tensor_tensor(hotf[:, :, :], rt[:, :, :], first[:, :].unsqueeze(2).to_broadcast([P, NT, E]), ALU.is_equal))
                dve.wait_ge(rank_mm, l + 1)
                rounded = mark(dve.tensor_scalar(ecnt[:, 0, :], PS[:, 4, 0:E], (P - 1) / 2, ROUND * P, ALU.add, ALU.add))
                dve.wait_ge(exp_done, l + 1)
                summed = mark(dve.tensor_reduce(esum[:, :], ex[:, :, :], AX_X, ALU.add))
                dve.wait_ge(dve_seq, rounded)
                count = mark(dve.tensor_scalar(ecnt[:, 0, :], ecnt[:, 0, :], ROUND * P, 1.0 / P, ALU.subtract, ALU.mult))
                dve.wait_ge(dve_seq, summed)
                mark(dve.reciprocal(xrow[:, :, D + 1], esum[:, :]))
                dve.wait_ge(dve_seq, count)
                step(dve.tensor_tensor_scan(ecnt[:, 1, :], one_e[:, :], ecnt[:, 0, :], 0.0, ALU.mult, ALU.add))
                step(dve.tensor_tensor(ecnt[:, 2, :], ecnt[:, 1, :], ecnt[:, 0, :], ALU.subtract))
                step(dve.scalar_tensor_tensor(out=rt[:, :, :],
                                              in0=ecnt[:, 2, :].unsqueeze(1).to_broadcast([P, NT, E]), scalar=float(P),
                                              in1=PS[:, 3, 0:NT * E].rearrange("p (t e) -> p t e", t=NT),
                                              op0=ALU.mult, op1=ALU.add))
                step(dve.tensor_tensor(rt[:, :, :], rt[:, :, :], hotf[:, :, :], ALU.mult))
                with nc.allow_low_precision(reason="whole numbers, one of them not zero"):
                    dve.tensor_reduce(pos[:, :], rt[:, :, :], AX_X, ALU.add).then_inc(pos_ready, 1)
                step(dve.tensor_tensor(tcmp[:, :, :], ecnt[:, 1, :].unsqueeze(1).to_broadcast([P, NS, E]),
                                       tix[:, :].unsqueeze(2).to_broadcast([P, NS, E]), ALU.is_le))
                step(dve.tensor_reduce(texp[:, 0, :], tcmp[:, :, :], AX_X, ALU.add))
                dve.tensor_scalar(tile_w[:, :], texp[:, 0, :], float(E - 1), float(FF), ALU.min, ALU.mult).then_inc(te_ready, 1)
                dve.wait_ge(te_ready, l + 1)

            def attention(b):
                for j in reversed(range(TB)):
                    n = b * TB + TB - 1 - j
                    w = (j + 1) * P
                    dve.wait_ge(decay_w, n + 1)
                    step(dve.tensor_tensor(wdec[:, n % 2, w - P:w], wdec[:, n % 2, w - P:w], after[:, :], ALU.mult))
                    dve.wait_ge(score_mm, n + 1)
                    if n >= 2:
                        dve.wait_ge(ret_mm, n - 1)
                    bank = 2 * (n % 2)
                    for h in range(0, w, 512):
                        e = min(w, h + 512)
                        o = dve.scalar_tensor_tensor(out=swt[:, n % 2, h:e], in0=PS[:, bank + h // 512, 0:e - h],
                                                     scalar=SCALE, in1=wdec[:, n % 2, h:e],
                                                     op0=ALU.mult, op1=ALU.mult)
                        if e < w:
                            step(o)
                    o.then_inc(sw_ready, 1)
                    dve.wait_ge(sw_ready, n + 1)
                for g in range(TB // G):
                    dve.wait_ge(proj_mm, b * (TB // G) + g + 1)
                    tt = slice(b * TB + g * G, b * TB + (g + 1) * G)
                    dve.scalar_tensor_tensor(out=xres[:, tt, :], in0=PS[:, 6 + g, :].rearrange("p (t d) -> p t d", t=G),
                                             scalar=oscale[:, 0:1], in1=xres[:, tt, :],
                                             op0=ALU.mult, op1=ALU.add).then_inc(attn_added, 1)

            def prepare():
                dve.wait_ge(ld_l1, LD_L1)
                dve.wait_ge(consts1, 1)
                for n in range(2):
                    dve.wait_ge(pd_mm, n + 1)
                    dve.tensor_copy(ewT[:, n * 512:(n + 1) * 512], PS[:, 6 + n, :]).then_inc(pd_ev, 1)
                for q in range(HS):
                    dve.tensor_copy(wmrow16[:, q, :, :], wmrow[:, :].unsqueeze(2).to_broadcast([1, HD, HP])).then_inc(diag_ready, 1)
                step(dve.tensor_scalar(nwblk[:, :], wblk[:, :], -1.0, None, ALU.mult))
                dve.tensor_scalar(wo_v[:, :], wo_v[:, :], wvcol[:, 0:1], None, ALU.mult).then_inc(diag_ready, 1)
                dve.wait_ge(pd_mm, 3)
                dve.tensor_copy(wmcol[:, :], PS[:, 6, 0:1]).then_inc(pd_ev, 1)
                dve.wait_ge(pd_ev, 3)
                dve.wait_ge(diag_ready, HS + 1)

            def tile_dve(l, i, c, w2=None):
                k = i * UT + c
                at = l * NS
                if c >= 1 and w2 is None:
                    w2 = dve.value_load(tile_w[0:1, bass.ds(k - 1, 1)], min_val=0, max_val=(E - 1) * FF)
                if c < NS:
                    w = dve.value_load(tile_w[0:1, bass.ds(k, 1)], min_val=0, max_val=(E - 1) * FF)
                    if c >= 2:
                        dve.wait_ge(h_mm, k + (at - 1))
                    dve.tensor_copy(w1st[:, c % 2, :], W1s[:, bass.ds(w, FF)]).then_inc(w1_staged, 1)
                    dve.wait_ge(x_tr, k + (at + 1))
                    dve.tensor_copy(xTs[:, c % 2, :], PS[:, c % 2, 0:P]).then_inc(x_ev, 1)
                if c >= 1:
                    r = (c - 1) % R
                    if c > R:
                        dve.wait_ge(y_put[r], passed(l, i, c - 1 - R) * 16)
                    dve.tensor_copy(slot_id[:, r:r + 1], xring[:, r, D:D + 1]).then_inc(id_ready, 1)
                    dve.tensor_copy(slot_w[:, r:r + 1], xring[:, r, D + 1:D + 2]).then_inc(id_ready, 1)
                    if c >= 3:
                        dve.wait_ge(y_mm, k + (at - 2))
                    dve.tensor_copy(w2st[:, (c - 1) % 2, :], W2s[:, bass.ds(w2, FC * D)]).then_inc(w2_staged, 1)
                return w if c < NS else None

            for l in range(L):
                if l == 0:
                    dve.wait_ge(ld_small, 16 * 9)
                    dve.wait_ge(consts, 1)
                route(l)
                if l == 0:
                    dve.wait_ge(dec_sig, 1)
                    dve.tensor_scalar(ldec[:, 1, :], ldec[:, 1, :], 1e-8, None, ALU.add).then_inc(dec_eps, 1)
                if 1 <= l <= B:
                    attention(l - 1)
                elif l == B + 1:
                    prepare()
                if l == 0:
                    dve.wait_ge(ld_w1, 16)
                    dve.wait_ge(ld_w2, 16)
                w = None
                for k in range(PRE):
                    w = tile_dve(l, 0, k, w)
                with dve.Fori(0, (NS - PRE) // UT) as i:
                    w = None
                    for n in range(UT):
                        w = tile_dve(l, i, PRE + n, w)
                tile_dve(l, 0, NS)
            layernorm(1)

            job = [3]

            def bank():
                dve.wait_ge(pd_mm, job[0] + 1)
                job[0] += 1
                return PS[:, 6 + (job[0] - 1) % 2, :]

            def conv(n):
                o = post[n].rearrange("p (b t) -> p b t", b=B)
                if n:
                    dve.wait_ge(tap_ready, n)
                    parts = [slice(0, B)]
                else:
                    dve.wait_ge(pads, 1)
                    parts = [slice(b, b + 1) for b in range(B)]
                for b in parts:
                    if n == 0:
                        dve.wait_ge(pa_ev, NG // B * b.stop)
                        step(dve.tensor_scalar(o[:, b, :], pre[:, 0, b, 0:S], taps[:, 0, 0:1], None, ALU.mult))
                    for j in range(1, K):
                        c = dve.scalar_tensor_tensor(out=o[:, b, :], in0=pre[:, n, b, j:j + S], scalar=taps[:, n, j:j + 1],
                                                     in1=o[:, b, :], op0=ALU.mult, op1=ALU.add)
                        if j < K - 1:
                            step(c)
                    if b.stop < B:
                        step(c)
                c.then_inc(conv_done, 1)
                dve.wait_ge(conv_done, n + 1)

            def unit(n, dst):
                dve.wait_ge(len_ready, n + 1)
                step(dve.reciprocal(nstd[:, n, :], nstd[:, n, :]))
                v = dst.rearrange("p t h i -> p (t h) i")
                dve.tensor_tensor(v, v, nstd[:, n, :].unsqueeze(2).to_broadcast([P, C * HP, HD]), ALU.mult).then_inc(unit_ready, 1)
                dve.wait_ge(unit_ready, n + 1)

            conv(0)
            dve.wait_ge(pa_ev, 2 * NG + 2)
            step(dve.tensor_scalar(kp, angp, 1.0 / TWO_PI, ROUND, ALU.mult, ALU.add))
            step(dve.tensor_scalar(kp, kp, ROUND, None, ALU.subtract))
            step(dve.scalar_tensor_tensor(out=angp, in0=kp, scalar=-TWO_PI_HI, in1=angp, op0=ALU.mult, op1=ALU.add))
            step(dve.scalar_tensor_tensor(out=angp, in0=kp, scalar=-TWO_PI_LO, in1=angp, op0=ALU.mult, op1=ALU.add))
            dve.tensor_scalar(angp, angp, PI_DOWN, -PI_DOWN, ALU.min, ALU.max).then_inc(ang_red, 1)
            conv(1)
            dve.tensor_tensor(abraw[:, :, :], bank().rearrange("p (t h) -> p t h", t=C),
                              abbias[:, :].unsqueeze(1).to_broadcast([P, C, 2 * HP]), ALU.add).then_inc(pd_ev, 1)
            dve.wait_ge(pd_ev, job[0])
            conv(2)
            dve.wait_ge(cos_ready, 1)
            for n in range(4):
                r, i = n % 2, n // 2
                a, w = wblk[:, 2 * i:2 * i + 1], wblk[:, 2 * i + 1:2 * i + 2]
                step(dve.tensor_scalar(cos_part[n], cosp, w if r else a, None, ALU.mult))
                dve.scalar_tensor_tensor(out=mpl[:, r, i, :], in0=sinp, scalar=a if r else nwblk[:, 2 * i + 1:2 * i + 2],
                                         in1=cos_part[n], op0=ALU.mult, op1=ALU.add).then_inc(prod_ready, 1)
            unit(0, Kc)
            unit(1, Qc)
            dve.wait_ge(xstate0, 1)
            dve.wait_ge(bk_ready, 1)
            dve.wait_ge(pa_ev, V_EV)

            SUM_AT = [(C // NT * G) * (g + 1) + 4 for g in range(NG - 1)]

            def expert_sum(g):
                tt = slice(g * G, (g + 1) * G)
                dve.wait_ge(ysum_mm, (g + 1) * G)
                dve.tensor_tensor(xres[:, tt, :], xres[:, tt, :], PS[:, 6 + g % 2, :].rearrange("p (t d) -> p t d", t=G),
                                  ALU.add).then_inc(ysum_ev, 1)

            def route2():
                dve.tensor_tensor(lg1[:, 0, :, :], bank()[:, 0:NT * E1].rearrange("p (t e) -> p t e", t=NT),
                              rb1[:, :].unsqueeze(1).to_broadcast([P, NT, E1]), ALU.add).then_inc(pd_ev, 1)
                dve.wait_ge(pd_ev, job[0])
                step(dve.tensor_reduce(mx[:, :], lg1[:, 0, :, :], AX_X, ALU.max))
                dve.tensor_tensor(lg1[:, 1, :, :], lg1[:, 0, :, :], mx[:, :].unsqueeze(2).to_broadcast([P, NT, E1]),
                                  ALU.subtract).then_inc(sh1, 1)
                dve.wait_ge(sh1, 1)

            def choose2():
                step(dve.scalar_tensor_tensor(out=lg1[:, 3, :, :], in0=lg1[:, 1, :, :], scalar=0.0,
                                              in1=rev1.unsqueeze(1).to_broadcast([P, NT, E1]),
                                              op0=ALU.is_ge, op1=ALU.mult))
                step(dve.tensor_reduce(first[:, :], lg1[:, 3, :, :], AX_X, ALU.max))
                step(dve.tensor_tensor(lg1[:, 0, :, :], lg1[:, 3, :, :], first[:, :].unsqueeze(2).to_broadcast([P, NT, E1]),
                                       ALU.is_equal))
                dve.wait_ge(ex1, 1)
                step(dve.tensor_reduce(esum[:, :], lg1[:, 2, :, :], AX_X, ALU.add))
                step(dve.reciprocal(wprob[:, :], esum[:, :]))
                dve.tensor_tensor(sel[:, :, 0:E1], lg1[:, 0, :, :], wprob[:, :].unsqueeze(2).to_broadcast([P, NT, E1]),
                                  ALU.mult).then_inc(sel_ready, 1)
                dve.wait_ge(sel_ready, 1)

            T_, R_ = slice(0, HD), slice(HD, 2 * HD)
            for t in range(C):
                x, xn = X[t % 2], X[(t + 1) % 2]
                v = Vc[:, t, :, :].rearrange("p h j -> p j h")
                key = Kc[:, t, :, :].unsqueeze(1).to_broadcast([P, HD, HP, HD])
                bkey = bKc[:, t, :, :].unsqueeze(1).to_broadcast([P, HD, HP, HD])
                if t == 0:
                    pred_t = mark(dve.tensor_copy(pred[:, T_, :], Kc[:, 0, :, :].rearrange("p h i -> p i h")))
                    pred_r = mark(dve.tensor_scalar(pred[:, R_, :], v, -1.0, None, ALU.mult))
                    dve.wait_ge(dve_seq, pred_t)
                    outer_t = mark(dve.tensor_tensor(tmp[:, T_, :, :], pred[:, T_, :].unsqueeze(3).to_broadcast([P, HD, HP, HD]),
                                                     bkey, ALU.mult))
                else:
                    dve.wait_ge(x_new, 2 * t)
                    prod_r = mark(dve.tensor_tensor(tmp[:, R_, :, :], x[:, R_, :, :], key, ALU.mult))
                    dve.wait_ge(dve_seq, prod_t)
                    pred_t = mark(dve.tensor_reduce(pred[:, T_, :], tmp[:, T_, :, :], AX_X, ALU.add))
                    dve.wait_ge(dve_seq, prod_r)
                    sum_r = mark(dve.tensor_reduce(pred[:, R_, :], tmp[:, R_, :, :], AX_X, ALU.add))
                    dve.wait_ge(dve_seq, pred_t)
                    outer_t = mark(dve.tensor_tensor(tmp[:, T_, :, :], pred[:, T_, :].unsqueeze(3).to_broadcast([P, HD, HP, HD]),
                                                     bkey, ALU.mult))
                    dve.wait_ge(dve_seq, sum_r)
                    pred_r = mark(dve.tensor_tensor(pred[:, R_, :], pred[:, R_, :], v, ALU.subtract))
                if t == ROUTE_AT:
                    route2()
                elif t == ROUTE_AT + 2:
                    choose2()
                elif t in SUM_AT:
                    expert_sum(SUM_AT.index(t))
                dve.wait_ge(dve_seq, outer_t)
                dve.wait_ge(ax_ready, t + 1)
                if t >= 2:
                    dve.wait_ge(r_ready, t - 1)
                dve.tensor_tensor(xn[:, T_, :, :], aX[:, T_, :, :], tmp[:, T_, :, :], ALU.subtract).then_inc(x_new, 1)
                dve.wait_ge(dve_seq, pred_r)
                outer_r = mark(dve.tensor_tensor(tmp[:, R_, :, :], pred[:, R_, :].unsqueeze(3).to_broadcast([P, HD, HP, HD]),
                                                 bkey, ALU.mult))
                if t < C - 1:
                    dve.wait_ge(x_new, 2 * t + 1)
                    prod_t = mark(dve.tensor_tensor(tmp[:, T_, :, :], xn[:, T_, :, :],
                                                    Kc[:, t + 1, :, :].unsqueeze(1).to_broadcast([P, HD, HP, HD]), ALU.mult))
                dve.wait_ge(dve_seq, outer_r)
                dve.tensor_tensor(xn[:, R_, :, :], aX[:, R_, :, :], tmp[:, R_, :, :], ALU.subtract).then_inc(x_new, 1)

            def vec_final(n):
                r, n = n // (3 + B), n % (3 + B)
                if r == 0 and n == 0:
                    dve.wait_ge(vec_done, 1)
                t4 = sinp.rearrange("p (t c) -> p t c", t=VL)
                if n in (0, 2):
                    i = n // 2
                    step(dve.tensor_tensor(t4, Mt[:, r, i, :, :], y0[:, i, :].unsqueeze(1).to_broadcast([P, VL, VC]), ALU.mult))
                elif n == 1:
                    step(dve.tensor_tensor(Zt[:, r, :, :], Zt[:, r, :, :], t4, ALU.add))
                else:
                    b = n - 3
                    rows = slice(b * P // B, (b + 1) * P // B)
                    dve.tensor_tensor(vT[r * P // 2:(r + 1) * P // 2, b, :].rearrange("p (c t) -> p t c", t=VL),
                                      Zt[rows, r, :, :], t4[rows, :, :], ALU.add).then_inc(v_ready, 1)
                    if b == B - 1:
                        dve.wait_ge(v_ready, B * (r + 1))

            dve.wait_ge(trans_mm, 1)
            dve.tensor_copy(QT0.rearrange("p q m c -> p m q c"),
                            PS[:, 6, :].rearrange("p (m q c) -> p m q c", q=HS, c=CH)).then_inc(qt0_ready, 1)
            dve.wait_ge(trans_ev, 4)
            for b in range(B):
                dve.tensor_tensor(BD[:, 0, b, :, :].rearrange("p c (i h) -> p c i h", h=HP),
                                  PT[:, :, b * NC:b * NC + CG].rearrange("p i c -> p c i").unsqueeze(3).to_broadcast([P, CG, HD, HP]),
                                  headin[:, :].unsqueeze(1).unsqueeze(1).to_broadcast([P, CG, HD, HP]),
                                  ALU.mult).then_inc(bd_first, 1)

            dve.wait_ge(trans_ev, 5)
            dve.wait_ge(s0_ready, 1)
            for b in range(B):
                dve.tensor_copy(Sall[:, b * NC + 1, :], QT[:, :, b * NC]).then_inc(s_ready[b], 1)
            def reads(n):
                half = ORDER[n]
                dve.wait_ge(corr_mm, B * (NC // 2 if half % 2 == 0 else NC))
                src = PS[:, half, :].rearrange("p (c t) -> p c t", t=C)
                cc = slice(half * (CH // NG), (half + 1) * (CH // NG))
                dve.tensor_tensor(oT[:, half * 512:(half + 1) * 512].rearrange("p (c t) -> p c t", t=C), src,
                                  olocT[:, :, cc].rearrange("p t c -> p c t"), ALU.add).then_inc(o_ready, 1)

            def lengths(n):
                half = ORDER[n]
                dve.wait_ge(ostd_ready, n + 1)
                dve.reciprocal(oinv[:, half * G * H:(half + 1) * G * H],
                               ostd[:, half * G * H:(half + 1) * G * H]).then_inc(oinv_ready, 1)

            def normed(n):
                half = ORDER[n]
                dve.wait_ge(o_ready, n + 1)
                dve.wait_ge(oinv_tr, n + 1)
                cols = slice(half * 512, (half + 1) * 512)
                dve.scalar_tensor_tensor(out=mT[:, cols], in0=oT[:, cols], scalar=wmcol[:, 0:1], in1=PS[:, half, :],
                                         op0=ALU.mult, op1=ALU.mult).then_inc(m_ready, 1)

            def result(n):
                half = ORDER[n]
                tt = slice(half * G, (half + 1) * G)
                dve.wait_ge(out_mm, n + 1)
                dve.wait_ge(xg_ready, n + 1)
                step(dve.tensor_tensor(xcur[:, tt, :], PS[:, half, :].rearrange("p (t d) -> p t d", t=G), gate[:, tt, :], ALU.mult))
                dve.tensor_tensor(xres[:, tt, :], xres[:, tt, :], xcur[:, tt, :], ALU.add).then_inc(x3_ready, 1)

            for c in range(1, NC - 1):
                for b in range(B):
                    dve.wait_ge(scan_mm[b], c)
                    dve.tensor_tensor(Sall[:, b * NC + c + 1, :], PS[:, 4 + b, 0:HD], QT[:, :, b * NC + c],
                                      ALU.add).then_inc(s_ready[b], 1)
                if c == 1:
                    expert_sum(NG - 1)
                elif VFINAL <= c < VADD - 1:
                    vec_final(c - VFINAL)
                elif c == VADD:
                    dve.wait_ge(vsq_ready, 2 * B)
                    dve.tensor_tensor(vsq[:, 0, :], vsq[:, 0, :], vsq[:, 1, :], ALU.add).then_inc(vadd_ready, 1)
                elif c == VINV:
                    dve.wait_ge(vstd_ready, 1)
                    dve.reciprocal(vinv[:, :], mx[:, :]).then_inc(vinv_ready, 1)
                for n in range(2):
                    if c == READS_AT + n:
                        reads(n)
                    elif c == LEN_AT + n:
                        lengths(n)
                    elif c == TURN_AT + n:
                        normed(n)
            g = NCS - 1
            dve.wait_ge(corr_mm, B * CS * (g - SR + 1))
            for b in range(B):
                dve.wait_ge(s_ready[b], NC - 1)
                c0 = b * NC + g * CS
                dve.tensor_tensor(BDS[:, g % SR, b, :, :].rearrange("p c (j h) -> p (c j) h", h=HP),
                                  Sall[:, c0:c0 + CS, :].rearrange("p c j -> p (c j)").unsqueeze(2).to_broadcast([P, CS * HD, HP]),
                                  headin[:, :].unsqueeze(1).to_broadcast([P, CS * HD, HP]),
                                  ALU.mult).then_inc(bds_last, 1)

            reads(2)
            reads(3)
            result(0)
            result(1)
            lengths(2)
            lengths(3)
            normed(2)
            normed(3)
            result(2)
            result(3)

        @block.scalar
        def _(act):
            def norm_squares(n, g):
                act.wait_ge(centred, n * NG + g + 1)
                act.activation(xT[:, g * 512:(g + 1) * 512].rearrange("p (t d) -> p t d", t=G),
                               xcur[:, g * G:(g + 1) * G, :], ACT.Square).then_inc(squared, 1)

            def norm_roots(n, g):
                tt = slice(g * G, (g + 1) * G)
                act.wait_ge(ln_var, n * NG + g + 1)
                act.activation(stat[:, 2, tt], stat[:, 1, tt], ACT.Sqrt).then_inc(ln_std, 1)

            def tokens_T(l, g):
                act.wait_ge(xt_tr, l * NG + g + 1)
                act.activation(xT[:, g * 512:(g + 1) * 512], PS[:, g % 2, :], ACT.Copy).then_inc(xt_ready, 1)

            for g in range(NG + 1):
                if g < NG:
                    norm_squares(0, g)
                if g:
                    norm_roots(0, g - 1)

            def qkv():
                for n in range(3 * NG):
                    act.wait_ge(qkv_mm, n + 1)
                    bank = PS[:, 5 + n % 3, :]
                    if n < 2 * NG:
                        dst = (qT, kT)[n // NG][:, (n % NG) * 512:(n % NG + 1) * 512]
                    else:
                        g = n - 2 * NG
                        dst = vtok[:, g * G:(g + 1) * G, :].rearrange("p t d -> p (t d)")
                    act.activation(dst, bank, ACT.Copy).then_inc(qkv_ready, 1)

            def attention(b):
                for j in reversed(range(TB)):
                    n = b * TB + TB - 1 - j
                    w = (j + 1) * P
                    if n >= 2:
                        act.wait_ge(sw_ready, n - 1)
                    act.activation(wdec[:, n % 2, 0:w], dist[:, S - w:S], ACT.Exp,
                                   scale=ldec[:, 2, b * TB + j:b * TB + j + 1]).then_inc(decay_w, 1)
                act.wait_ge(ret_mm, (b + 1) * TB)
                for h in range(S // 512):
                    if b:
                        act.wait_ge(proj_mm, b * (TB // G))
                    act.activation(retT[:, h * 512:(h + 1) * 512], PS[:, 4 + h, :], ACT.Copy).then_inc(ret_ev, 1)

            def tile_act(l, i, c):
                k = i * UT + c
                at = l * NS
                if 1 <= c <= NS:
                    act.wait_ge(h_mm, k + at)
                    if c >= 3:
                        act.wait_ge(y_mm, k + (at - 2))
                    act.activation(hTs[:, (c - 1) % 2, :], PS[:, 2 + (c - 1) % 2, :], ACT.Silu).then_inc(h_act, 1)
                if c >= 2:
                    r = (c - 2) % R
                    act.wait_ge(y_mm, k + (at - 1))
                    act.wait_ge(id_ready, k * 2 + 2 * (at - 1))
                    if c >= R + 2:
                        act.wait_ge(y_put[r], passed(l, i, c - 2 - R) * 16)
                    act.activation(yring[:, r, :], PS[:, 4 + c % 2, 0:D], ACT.Copy,
                                   scale=slot_w[:, r:r + 1]).then_inc(y_ev, 1)

            for l in range(L):
                for g in range(NG):
                    tokens_T(l, g)
                act.wait_ge(shifted, NG * (l + 1))
                act.activation(ex[:, :, :], sh[:, :, :], ACT.Exp).then_inc(exp_done, 1)
                if l == 0:
                    act.wait_ge(dec_eps, NG)
                    act.activation(ldec[:, 1, :], ldec[:, 0, :], ACT.Sigmoid).then_inc(dec_sig, 1)
                    act.wait_ge(dec_eps, NG + 1)
                    act.activation(ldec[:, 2, :], ldec[:, 1, :], ACT.Ln).then_inc(dec_log, 1)
                    act.wait_ge(dec_log, 1)
                    qkv()
                if 1 <= l <= B:
                    attention(l - 1)
                for k in range(1, PRE):
                    tile_act(l, 0, k)
                with act.Fori(0, (NS - PRE) // UT) as i:
                    for n in range(UT):
                        tile_act(l, i, PRE + n)
                for k in range(NS, NS + 2):
                    tile_act(l, 0, k)

            job = [0]

            def bank():
                act.wait_ge(pa_mm, job[0] + 1)
                job[0] += 1
                return PS[:, 2 + (job[0] - 1) % 4, :]

            def plane(n, dst, func):
                by_chunk = dst.rearrange("p (t c) -> p c t", t=VL)
                for h in range(S // 512):
                    act.activation(by_chunk[:, h * 512 // VL:(h + 1) * 512 // VL, :], bank().rearrange("p (c t) -> p c t", t=VL),
                                   func, bias=pbias[:, n:n + 1]).then_inc(pa_ev, 1)

            def ctrl(n, g):
                b, a = g // (S // 512), K - 1 + g % (S // 512) * 512
                act.activation(pre[:, n, b, a:a + 512], bank(), ACT.Identity, bias=cbias[:, n:n + 1]).then_inc(pa_ev, 1)

            def first_tap(n):
                act.wait_ge(pads, 1)
                act.activation(post[n].rearrange("p (b t) -> p b t", b=B), pre[:, n, :, 0:S], ACT.Copy,
                               scale=taps[:, n, 0:1]).then_inc(tap_ready, 1)

            def silu(n):
                act.wait_ge(conv_done, n + 1)
                act.activation(post[n], post[n], ACT.Silu).then_inc(post_ready, 1)

            def chunked(n, dst):
                for g in range(NG):
                    o = bank()
                    act.activation(squares_of[n][:, g * 512:(g + 1) * 512], o, ACT.Square).then_inc(sq_ready, 1)
                    act.activation(dst[:, g * SB:(g + 1) * SB, :, :].rearrange("p t h i -> p (t h i)"), o, ACT.Copy).then_inc(pa_ev, 1)

            def lengths(n):
                act.wait_ge(len2_ready, n + 1)
                act.activation(nstd[:, n, :], nstd[:, n, :], ACT.Sqrt, bias=eps_kq[:, 0:1]).then_inc(len_ready, 1)

            for g in range(NG + 1):
                if g < NG:
                    norm_squares(1, g)
                if g:
                    norm_roots(1, g - 1)
                if g >= 2:
                    tokens_T(L, g - 2)
            ctrl(0, 0)
            tokens_T(L, NG - 1)
            for g in range(1, NG):
                ctrl(0, g)
            for n in range(1, 3):
                if n == 2:
                    plane(4, angp, ACT.Identity)
                for g in range(NG):
                    ctrl(n, g)
                act.wait_ge(pa_ev, job[0])
                first_tap(n)
            silu(0)
            act.wait_ge(ang_red, 1)
            act.activation(cosp, angp, ACT.Sin, scale=0.5).then_inc(sincos, 1)
            act.activation(sinp, angp, ACT.Sin).then_inc(sincos, 1)
            chunked(0, Kc)
            silu(1)
            chunked(1, Qc)
            silu(2)
            plane(0, u0p, ACT.Sigmoid)
            plane(1, u1p, ACT.Sigmoid)
            act.wait_ge(pd_ev, 4)
            act.activation(ab[:, :, :], abraw[:, :, :], ACT.Sigmoid).then_inc(ab_ready, 1)
            lengths(0)
            lengths(1)
            for g in range(NG):
                act.activation(Vc[:, g * SB:(g + 1) * SB, :, :].rearrange("p t h i -> p (t h i)"), bank(), ACT.Copy).then_inc(pa_ev, 1)

            def decayed(t):
                for h in range(HP):
                    o = act.activation(aX[:, :, h, :], X[t % 2][:, :, h, :],
                                       ACT.Copy, scale=ab[:, t, h:h + 1])
                o.then_inc(ax_ready, 1)

            act.wait_ge(ab_ready, 1)
            act.wait_ge(xstate0, 1)
            decayed(0)
            plane(2, zneg[:, 0, :], ACT.Silu)
            plane(3, zneg[:, 1, :], ACT.Silu)

            def reads_evac(g):
                if g == 0:
                    act.wait_ge(planes_ready, 1)
                act.wait_ge(rT_mm, G * (g + 1))
                tt = slice(g * G, (g + 1) * G)
                bank = PS[:, g % 4, :].rearrange("p (t q c) -> p q t c", t=G, q=HS)
                for n, dst in enumerate((qeffT, olocT)):
                    for q in range(HS):
                        o = act.activation(dst[part_rows(q), tt, :], bank[part_rows(n), q, :, :], ACT.Copy)
                o.then_inc(rT_ev, 1)


            def expert_scale(n):
                t = n // 2
                if t >= 2:
                    act.wait_ge(ysum_mm, t - 1)
                act.wait_ge(y1_mm, t + 1)
                act.wait_ge(sel_ready, 1)
                for e in range(n % 2 * (E1 // 2), (n % 2 + 1) * (E1 // 2)):
                    o = act.activation(scaled[:, t % 2, e, :], PS[:, 4 + e // 4, e % 4 * D:(e % 4 + 1) * D], ACT.Copy,
                                       scale=sel[:, t, e:e + 1])
                if n % 2:
                    o.then_inc(y1_ev, 1)

            for t in range(C):
                if t:
                    act.wait_ge(x_new, 2 * t)
                    decayed(t)
                if t % G == 2 and t > G:
                    reads_evac(t // G - 1)
                if 2 <= t < 2 + NG:
                    g = t - 2
                    act.wait_ge(gate_mm, g + 1)
                    act.activation(gate[:, g * G:(g + 1) * G, :].rearrange("p t d -> p (t d)"), PS[:, 7, :],
                                   ACT.Sigmoid).then_inc(gate_ev, 1)
                if t == ROUTE_AT + 1:
                    act.wait_ge(sh1, 1)
                    act.activation(lg1[:, 2, :, :], lg1[:, 1, :, :], ACT.Exp).then_inc(ex1, 1)
                for n in HALVES_AT.get(t, ()):
                    expert_scale(n)
                if t == SELT_AT:
                    act.wait_ge(selT_mm, 1)
                    act.activation(selT, PS[:, 6, :], ACT.Copy).then_inc(selT_ev, 1)
            for n in range(2):
                act.wait_ge(trans_mm, 2 + n)
                bank = PS[:, 1 + n, :].rearrange("p (i q c) -> p q i c", q=HS, c=CH)
                for q in range(HS):
                    act.activation(PT[part_rows(q), 4 * n:4 * n + 4, :], bank[part_rows(0), q, :, :], ACT.Copy).then_inc(trans_ev, 1)
            act.wait_ge(trans_mm, 4)
            act.activation(QT.rearrange("p (m j) c -> p j m c", j=JP), PS[:, 0, :].rearrange("p (j m c) -> p j m c", j=JP, c=CH),
                           ACT.Copy).then_inc(trans_ev, 1)
            act.wait_ge(trans_ev, 5)
            PTb = PT.rearrange("p i (b c) -> p b c i", b=B)

            def vec_proj(half):
                act.wait_ge(vp_mm, half + 1)
                act.wait_ge(vinv_ready, 1)
                g = ORDER[half]
                for t in range(g * G, (g + 1) * G):
                    o = act.activation(vproj[:, t, :], PS[:, 6 + half % 2, t % G * D:(t % G + 1) * D],
                                       ACT.Copy, scale=vinv[:, t:t + 1])
                o.then_inc(vp_ev, 1)

            def squares(n):
                half = ORDER[n]
                act.wait_ge(o_ready, n + 1)
                act.activation(osq[:, half * 512:(half + 1) * 512], oT[:, half * 512:(half + 1) * 512],
                               ACT.Square).then_inc(osq_ready, 1)

            def roots(n):
                half = ORDER[n]
                act.wait_ge(oms_mm, n + 1)
                act.activation(ostd[:, half * G * H:(half + 1) * G * H], PS[:, half, 0:G * H], ACT.Sqrt,
                               bias=eps_col[:, 0:1]).then_inc(ostd_ready, 1)

            def spread(n):
                half = ORDER[n]
                act.wait_ge(oinv_ready, n + 1)
                act.activation(oinvx[:, half * 512:(half + 1) * 512].rearrange("p (n j h) -> p n j h", j=HD, h=HP),
                               oinv[:, half * G * H:(half + 1) * G * H].rearrange("p (n h) -> p n h", h=HP)
                               .unsqueeze(2).to_broadcast([P, G * HS, HD, HP]), ACT.Copy).then_inc(oinvx_ready, 1)

            def blocks(g):
                if g >= 2:
                    for b in range(B):
                        act.wait_ge(scan_mm[b], CG * (g - 1) - 1)
                for h in range(HP):
                    o = act.activation(BD[:, g % 2, :, :, h::HP], PTb[:, :, g * CG:(g + 1) * CG, :],
                                       ACT.Copy, scale=headin[:, h:h + 1])
                o.then_inc(bd_ready, 1)

            def vec_square(r):
                for b in range(B):
                    act.wait_ge(v_ready, B * r + b + 1)
                    act.activation(vsq[b * P // B:(b + 1) * P // B, r, :], vT[r * P // 2:(r + 1) * P // 2, b, :],
                                   ACT.Square).then_inc(vsq_ready, 1)

            blocks(1)
            reads_evac(C // G - 1)
            blocks(2)
            vec_square(0)
            blocks(3)
            vec_square(1)
            blocks(4)
            act.wait_ge(vms_mm, 1)
            act.activation(vstd[:, :], PS[:, 6, 0:NT].rearrange("p (t b) -> p b t", b=B), ACT.Sqrt,
                           bias=eps_col[:, 0:1]).then_inc(vstd_ready, 1)
            blocks(5)
            vec_proj(0)
            blocks(6)
            squares(0)
            vec_proj(1)
            squares(1)
            roots(0)
            roots(1)
            vec_proj(2)
            spread(0)
            spread(1)
            vec_proj(3)
            blocks(7)
            for n in range(2, NG):
                squares(n)
            for n in range(2, NG):
                roots(n)
                spread(n)

        @block.tensor
        def _(pe):
            def tokens_T(l, g):
                if l % L == 0:
                    pe.wait_ge(layer_x, l // L * NG + g + 1)
                else:
                    pe.wait_ge(ld_tok[g], 16 * l)
                if g >= 2:
                    pe.wait_ge(xt_ready, l * NG + g - 1)
                for t in range(G):
                    m = pe.transpose(PS[:, g % 2, t * P:(t + 1) * P], xcur[:, g * G + t, :], ident[:, :])
                m.then_inc(xt_tr, 1)

            def logits(l, g):
                ne = E + 1 if l == 0 else E
                rhs = rw0[:, :] if l == 0 else rw[:, l, :]
                pe.wait_ge(xt_ready, l * NG + g + 1)
                if l == 0 and g == 1:
                    pe.wait_ge(w_ready, 1)
                for n in range(G):
                    t = g * G + n
                    m = pe.matmul(PS[:, LOGIT_BANKS[g], n * ne:(n + 1) * ne], xT[:, t * P:(t + 1) * P], rhs, start=True, stop=True)
                m.then_inc(logits_mm, 1)

            def ranks(l, g):
                pe.wait_ge(hot_ready, l * NG + g + 1)
                tiles = range(g * G, (g + 1) * G)
                pe.matmul(PS[:, 3, g * G * E:(g + 1) * G * E], ltri[:, :],
                          hot[:, tiles.start:tiles.stop, :].rearrange("p t e -> p (t e)"), start=False, stop=False)
                for t in tiles:
                    if t < NT - 1:
                        later = PS[:, 3, (t + 1) * E:NT * E].rearrange("p (t e) -> p t e", e=E)
                        pe.matmul(later, ones_bf[:, :], hot[:, t:t + 1, :].to_broadcast([P, NT - 1 - t, E]),
                                  start=False, stop=(t == NT - 2))
                for t in tiles:
                    m = pe.matmul(PS[:, 4, 0:E], ones_bf[:, :], hot[:, t, :], start=(t == 0), stop=(t == NT - 1))
                if g == NG - 1:
                    m.then_inc(rank_mm, 1)

            def qkv():
                pe.wait_ge(w_ready, 1)
                for n in range(3 * NG):
                    if n >= 3:
                        pe.wait_ge(qkv_ready, n - 2)
                    bank = PS[:, 5 + n % 3, :]
                    g = n % NG
                    if n < 2 * NG:
                        m = pe.matmul(bank, wT[:, n // NG, :], xT[:, g * 512:(g + 1) * 512], start=True, stop=True)
                    else:
                        for t in range(G):
                            m = pe.matmul(bank[:, t * P:(t + 1) * P], xT[:, (g * G + t) * P:(g * G + t + 1) * P],
                                          wT[:, 2, :], start=True, stop=True)
                    m.then_inc(qkv_mm, 1)

            def attention(b):
                pe.wait_ge(qkv_ready, 3 * NG)
                pe.wait_ge(pos_ready, b + 2)

                def scores(j):
                    n = b * TB + TB - 1 - j
                    if n >= 2:
                        pe.wait_ge(sw_ready, n - 1)
                    w = (j + 1) * P
                    s0 = (b * TB + j) * P
                    for h in range(0, w, 512):
                        e = min(w, h + 512)
                        m = pe.matmul(PS[:, 2 * (n % 2) + h // 512, 0:e - h], kT[:, s0:s0 + P],
                                      qT[:, b * S + h:b * S + e], start=True, stop=True)
                    m.then_inc(score_mm, 1)

                def retrieve(j):
                    n = b * TB + TB - 1 - j
                    pe.wait_ge(sw_ready, n + 1)
                    w = (j + 1) * P
                    for h in range(0, w, 512):
                        e = min(w, h + 512)
                        m = pe.matmul(PS[:, 4 + h // 512, 0:e - h], vtok[:, b * TB + j, :], swt[:, n % 2, h:e],
                                      start=(j == TB - 1), stop=(j == h // P))
                    m.then_inc(ret_mm, 1)

                scores(TB - 1)
                for j in reversed(range(TB)):
                    if j:
                        scores(j - 1)
                    retrieve(j)
                if b:
                    pe.wait_ge(attn_added, b * (TB // G))
                for g in range(TB // G):
                    pe.wait_ge(ret_ev, b * (S // 512) + g + 1)
                    for t in range(G):
                        m = pe.matmul(PS[:, 6 + g, t * P:(t + 1) * P], retT[:, (g * G + t) * P:(g * G + t + 1) * P],
                                      wT[:, 3, :], start=True, stop=True)
                    m.then_inc(proj_mm, 1)

            def prepare():
                pe.wait_ge(ld_l1, LD_L1)
                pe.wait_ge(pos_ready, B + 2)
                for n in range(2):
                    for e in range(4):
                        m = pe.transpose(PS[:, 6 + n, e * D:(e + 1) * D], ew_raw[:, n * 4 + e, :], ident[:, :])
                    m.then_inc(pd_mm, 1)
                pe.wait_ge(diag_ready, HS)
                pe.wait_ge(pd_ev, 1)
                pe.matmul(PS[:, 6, 0:1], wmrow16[0:1, :, :, :].rearrange("p q i h -> p (q i h)"), ident[0:1, 0:1],
                          start=True, stop=True).then_inc(pd_mm, 1)
                pe.wait_ge(pd_ev, 3)

            def tile_mm(l, i, c):
                k = i * UT + c
                at = l * NS
                if c < NS:
                    pe.wait_ge(ld_tile[c % R], passed(l, i, c) * 16)
                    pe.transpose(PS[:, c % 2, 0:P], xring[:, c % R, 0:D], ident[:, :]).then_inc(x_tr, 1)
                if 1 <= c <= NS:
                    n = (c - 1) % 2
                    pe.wait_ge(w1_staged, k + at)
                    pe.wait_ge(x_ev, k + at)
                    for f in range(FC):
                        m = pe.matmul(PS[:, 2 + n, f * P:(f + 1) * P], w1st[:, n, f * P:(f + 1) * P], xTs[:, n, :],
                                      start=True, stop=True)
                    m.then_inc(h_mm, 1)
                if c >= 2:
                    n = c % 2
                    pe.wait_ge(w2_staged, k + (at - 1))
                    pe.wait_ge(h_act, k + (at - 1))
                    if c >= 4:
                        pe.wait_ge(y_ev, k + (at - 3))
                    for f in range(FC):
                        m = pe.matmul(PS[:, 4 + n, 0:D], hTs[:, n, f * P:(f + 1) * P], w2st[:, n, f * D:(f + 1) * D],
                                      start=(f == 0), stop=(f == FC - 1))
                    m.then_inc(y_mm, 1)

            pe.wait_ge(consts, 1)
            for l in range(L):
                for g in range(NG):
                    tokens_T(l, g)
                if l == 0:
                    pe.wait_ge(ld_small, 16 * 9)
                    for n in range(4):
                        m = pe.transpose(PS[:, 5, n * P:(n + 1) * P], wraw[:, n, :], ident[:, :])
                    m.then_inc(w_tr, 1)
                pe.matmul(PS[:, 3, 0:NT * E], ltri[:, :], zero_bf[:, :], start=True, stop=False)
                for g in range(NG):
                    logits(l, g)
                for g in range(NG):
                    ranks(l, g)
                if l == 0:
                    qkv()
                if 1 <= l <= B:
                    attention(l - 1)
                    pe.wait_ge(attn_added, l * (TB // G))
                elif l == B + 1:
                    prepare()
                for k in range(PRE):
                    tile_mm(l, 0, k)
                with pe.Fori(0, (NS - PRE) // UT) as i:
                    for n in range(UT):
                        tile_mm(l, i, PRE + n)
                for k in range(NS, NS + 2):
                    tile_mm(l, 0, k)

            pe.wait_ge(diag_ready, HS + 1)

            aj, dj = [0], [3]

            def abank():
                n = aj[0]
                aj[0] += 1
                if n >= 4:
                    pe.wait_ge(pa_ev, n - 3)
                return PS[:, 2 + n % 4, :]

            def dbank():
                n = dj[0]
                dj[0] += 1
                pe.wait_ge(pd_ev, n - 1)
                return PS[:, 6 + n % 2, :]

            def plane(first_col, stride):
                for h in range(S // 512):
                    o = abank()
                    for b in range(B):
                        m = pe.matmul(o[b * 64:(b + 1) * 64, :], wc[:, first_col:first_col + 63 * stride + 1:stride],
                                      xT[:, b * S + h * 512:b * S + (h + 1) * 512], start=True, stop=True)
                    m.then_inc(pa_mm, 1)

            def ctrl(part, g):
                pe.matmul(abank(), wc[:, OFF[part]:OFF[part + 1]], xT[:, g * 512:(g + 1) * 512],
                          start=True, stop=True).then_inc(pa_mm, 1)

            def by_step(v, t):
                return v.rearrange("p (c t) -> p t c", t=C)[:, t, :]

            def chunks(n):
                pe.wait_ge(post_ready, n + 1)
                for g in range(NG):
                    o = abank()
                    for t in range(SB):
                        v = by_step(post[n], g * SB + t)
                        pe.transpose(o[part_rows(0), t * DP:(t + 1) * DP], v[part_rows(0), :], ident[part_rows(0), part_rows(0)])
                        for q in range(1, HS):
                            m = pe.matmul(o[part_rows(q), t * DP:(t + 1) * DP], v[part_rows(q), :],
                                          ident[part_rows(q), part_rows(q)], start=True, stop=True)
                    m.then_inc(pa_mm, 1)

            tokens_T(L, 0)
            for g in range(NG):
                if g + 1 < NG:
                    tokens_T(L, g + 1)
                pe.wait_ge(xt_ready, NG * L + g + 1)
                ctrl(4, g)
            for part in (3, 5):
                if part == 5:
                    plane(OFF[1], 1)
                for g in range(NG):
                    ctrl(part, g)
            o = dbank()
            w_ab = wc[:, OFF[6]:OFF[8]].rearrange("p (n q h) -> p q n h", n=2, q=HS)
            for t in range(C):
                for q in range(HS):
                    m = pe.matmul(o[part_rows(q), t * 2 * HP:(t + 1) * 2 * HP], by_step(xT[:, :], t), w_ab[:, q, :, :],
                                  start=True, stop=True)
            m.then_inc(pd_mm, 1)
            chunks(0)
            chunks(1)
            plane(OFF[0], 2)
            plane(OFF[0] + 1, 2)
            chunks(2)
            plane(OFF[2], 2)
            plane(OFF[2] + 1, 2)
            o = dbank()
            for t in range(NT):
                m = pe.matmul(o[:, t * E1:(t + 1) * E1], xT[:, t * P:(t + 1) * P], rw1[:, :], start=True, stop=True)
            m.then_inc(pd_mm, 1)
            pe.wait_ge(pa_ev, C_EV)
            def experts(t):
                if t:
                    pe.wait_ge(y1_ev, t)
                for n in range(E1 * D // 512):
                    m = pe.matmul(PS[:, 4 + n, :], xT[:, t * P:(t + 1) * P], ewT[:, n * 512:(n + 1) * 512],
                                  start=True, stop=True)
                m.then_inc(y1_mm, 1)

            def expert_sum(t):
                pe.wait_ge(y1_ev, t + 1)
                g, n = t // G, t % G
                if t == 0:
                    pe.wait_ge(selT_ev, 1)
                    pe.wait_ge(ld_ebias, 16 * G)
                if n == 0 and g >= 2:
                    pe.wait_ge(ysum_ev, g - 1)
                if n == 0 and g == 1:
                    pe.wait_ge(gate_ev, NG)
                o = PS[:, 6 + g % 2, n * D:(n + 1) * D]
                for e in range(E1):
                    pe.matmul(o, ident[:, :], scaled[:, t % 2, e, :], start=(e == 0), stop=False)
                pe.matmul(o, selT[:, g * P:(g + 1) * P], ebias[:, n, :], start=False, stop=True).then_inc(ysum_mm, 1)

            def transitions():
                pe.wait_ge(x_new, 2 * C)
                x = X[C % 2]
                pe.wait_ge(ysum_ev, NG - 1)
                for m in range(HD // JP):
                    o = pe.transpose(PS[:, 6, m * P:(m + 1) * P],
                                     x[:, HD + m * JP:HD + (m + 1) * JP, :, :].rearrange("p j h i -> p (j h i)"), ident[:, :])
                o.then_inc(trans_mm, 1)
                pe.wait_ge(rT_ev, C // G - 1)
                for n in range(2):
                    for i in range(4):
                        o = pe.transpose(PS[part_rows(0), 1 + n, i * P:(i + 1) * P],
                                         x.rearrange("p c h i -> p (c h) i")[:, 0:DP, n * 4 + i], ident[:, :])
                    o.then_inc(trans_mm, 1)
                pe.wait_ge(qt0_ready, 1)
                for q in range(HS):
                    for j in range(JP):
                        cols = slice(j * 512 // JP, (j + 1) * 512 // JP)
                        o = pe.matmul(PS[part_rows(q), 0, cols], perm[:, j * DP:(j + 1) * DP],
                                      QT0[:, q, :, :].rearrange("p m c -> p (m c)"), start=True, stop=True)
                o.then_inc(trans_mm, 1)

            def reads(t, part=range(HD)):
                g = t // G
                if t % G == 0 and g >= 4:
                    pe.wait_ge(rT_ev, g - 3)
                pe.wait_ge(r_ready, t + 1)
                for i in part:
                    m = pe.matmul(PS[:, g % 4, (t % G) * P:(t % G + 1) * P],
                                  qX[t % QR].rearrange("p c h i -> p (c h) i")[:, :, i], ident[:, :],
                                  start=(i == 0), stop=(i == HD - 1))
                if part.stop == HD:
                    m.then_inc(rT_mm, 1)

            experts(0)
            for t in range(C):
                if t == SELT_AT - 1:
                    pe.wait_ge(sel_ready, 1)
                    pe.wait_ge(pd_ev, dj[0])
                    for g in range(NG):
                        m = pe.transpose(PS[:, 6, g * P:(g + 1) * P], sel[:, g * G:(g + 1) * G, :].rearrange("p t e -> p (t e)"),
                                         ident[:, :])
                    m.then_inc(selT_mm, 1)
                if t < NG:
                    if t:
                        pe.wait_ge(gate_ev, t)
                    for n in range(G):
                        tt = t * G + n
                        pe.matmul(PS[:, 7, n * D:(n + 1) * D], xT[:, tt * P:(tt + 1) * P], wc[:, OFF[8]:OFF[9]],
                                  start=True, stop=False)
                        m = pe.matmul(PS[:, 7, n * D:(n + 1) * D], ones_row[0:1, :], ogbias[0:1, :],
                                      start=False, stop=True)
                    m.then_inc(gate_mm, 1)
                if t in EXPERTS_AT:
                    experts(EXPERTS_AT[t])
                if t in SUMS_AT:
                    expert_sum(SUMS_AT[t])
                if t:
                    reads(t - 1)
            transitions()

            def correct(b, c):
                g = c // CS
                if c == 0 and b == 0:
                    pe.wait_ge(rT_ev, C // G)
                if c % CS == 0:
                    if g < NCS - 1:
                        pe.wait_ge(bds_ready, B * g + b + 1)
                    else:
                        pe.wait_ge(bds_last, b + 1)
                ch = b * NC + c
                for q in range(HS):
                    m = pe.matmul(PS[part_rows(q), ch // CB, (ch % CB) * C:(ch % CB + 1) * C], BDS[part_rows(q), g % SR, b, c % CS, :],
                                  qeffT[part_rows(q), :, ch], start=True, stop=True)
                m.then_inc(corr_mm, 1)

            def vec_squares(tiles):
                pe.wait_ge(vadd_ready, 1)
                pe.wait_ge(ysum_ev, NG)
                for t in tiles:
                    m = pe.matmul(PS[:, 6, t * B:(t + 1) * B], vsq[:, 0, t * P:(t + 1) * P], seqmean[:, :], start=True, stop=True)
                if t == TB - 1:
                    m.then_inc(vms_mm, 1)

            def vec_proj(n, tiles):
                if n == 0:
                    pe.wait_ge(vstd_ready, 1)
                if n >= 2:
                    pe.wait_ge(vp_ev, n - 1)
                b = n % 2
                for t in tiles:
                    tb = ORDER[n] % 2 * G + t
                    m = pe.matmul(PS[:, 6 + b, t * D:(t + 1) * D], vT[:, b, tb * P:(tb + 1) * P], wo_v[:, :],
                                  start=True, stop=True)
                if t == G - 1:
                    m.then_inc(vp_mm, 1)

            def mean_squares(n):
                half = ORDER[n]
                pe.wait_ge(osq_ready, n + 1)
                for t in range(G):
                    tt = half * G + t
                    m = pe.matmul(PS[:, half, t * H:(t + 1) * H], osq[:, tt * P:(tt + 1) * P], headmean[:, :],
                                  start=True, stop=True)
                m.then_inc(oms_mm, 1)

            def turn(n):
                half = ORDER[n]
                pe.wait_ge(oinvx_ready, n + 1)
                for t in range(G):
                    tt = half * G + t
                    m = pe.transpose(PS[:, half, t * P:(t + 1) * P], oinvx[:, tt * P:(tt + 1) * P], ident[:, :])
                m.then_inc(oinv_tr, 1)

            def project(n):
                half = ORDER[n]
                pe.wait_ge(m_ready, n + 1)
                for t in range(G):
                    tt = half * G + t
                    m = pe.matmul(PS[:, half, t * D:(t + 1) * D], mT[:, tt * P:(tt + 1) * P], wo_m[:, :], start=True, stop=True)
                m.then_inc(out_mm, 1)

            reads(C - 1, range(0, HD // 2))
            pe.wait_ge(trans_ev, 5)
            for c in range(1, NC - 1):
                if c == 1:
                    pe.wait_ge(bd_first, B)
                elif c % CG == 0:
                    pe.wait_ge(bd_ready, c // CG)
                for b in range(B):
                    pe.wait_ge(s_ready[b], c)
                    for q in range(HS):
                        m = pe.matmul(PS[part_rows(q), 4 + b, 0:HD], BD[part_rows(q), (c // CG) % 2, b, c % CG, :],
                                      Sall[part_rows(q), b * NC + c, :], start=True, stop=True)
                    m.then_inc(scan_mm[b], 1)
                    if c >= LAG:
                        correct(b, c - LAG)
                if c == 1:
                    reads(C - 1, range(HD // 2, HD))
                if VSUM <= c < VSUM + 2:
                    vec_squares(range((c - VSUM) * TB // 2, (c - VSUM + 1) * TB // 2))
                if VPROJ <= c < VPROJ + 2 * NG:
                    n, k = (c - VPROJ) // 2, (c - VPROJ) % 2
                    vec_proj(n, range(k * G // 2, (k + 1) * G // 2))
                for n in range(2):
                    if c == READS_AT + 1 + n:
                        mean_squares(n)
                    elif c == TURN_AT - 1 + n:
                        turn(n)
            for c in range(NC - 1 - LAG, NC):
                for b in range(B):
                    correct(b, c)
            project(0)
            project(1)
            mean_squares(2)
            mean_squares(3)
            turn(2)
            turn(3)
            project(2)
            project(3)


_INS = ["L0_attn_x", "L0_attn_Wq", "L0_attn_Wk", "L0_attn_Wv", "L0_attn_Wo", "L0_attn_Wd", "L0_attn_bd",
        "L0_attn_out_scale", "L0_ffn_routers", "L0_ffn_W1", "L0_ffn_W2", "L1_attn_W_ctrl", "L1_attn_b_ctrl",
        "L1_attn_W_block", "L1_attn_qconv_w", "L1_attn_kconv_w", "L1_attn_vconv_w", "L1_attn_rms_m_w",
        "L1_attn_rms_v_w", "L1_attn_W_out", "L1_attn_b_out", "L1_ffn_router_w", "L1_ffn_router_b",
        "L1_ffn_expert_w", "L1_ffn_expert_b"]
_TRANSPOSED = ["L1_ffn_router_w"]
_OUTS = [((2, 1024, 128), "float32")]


def kernel(**inputs):
    import numpy as _np
    import concourse.bacc as _bacc
    from concourse import mybir as _mybir
    from concourse.bass_utils import run_bass_kernel_spmd as _run

    nc = _bacc.Bacc("TRN2", target_bir_lowering=False, num_devices=1)
    arrays, args = {}, {}
    for name in _INS:
        a = _np.ascontiguousarray(_np.asarray(inputs[name]).T if name in _TRANSPOSED else inputs[name])
        arrays[f"in_{name}_dram"] = a
        args[name] = nc.dram_tensor(f"in_{name}_dram", a.shape, _mybir.dt.from_np(a.dtype), kind="ExternalInput").ap()
    outs = []
    for i, (shape, dtype) in enumerate(_OUTS):
        dt = _mybir.dt.from_np(_np.dtype(dtype))
        outs.append(nc.dram_tensor(f"out_{i}_dram", shape, dt, kind="ExternalOutput").ap())
    build(nc, args, outs[0])
    r = _run(nc, [arrays], core_ids=[0])
    return r.results[0]["out_0_dram"]
```
